# Optimizing a Trainium2 kernel written in Bass

```python
import numpy as np
import jax
import jax.numpy as jnp

def _softmax(x, axis=-1):
    return jax.nn.softmax(x, axis=axis)

def _gelu(x):
    return jax.nn.gelu(x, approximate=True)

def _silu(x):
    return jax.nn.silu(x)

def _sigmoid(x):
    return jax.nn.sigmoid(x)

def _layernorm(x, axis=-1, eps=1e-05):
    m = jnp.mean(x, axis=axis, keepdims=True)
    v = jnp.var(x, axis=axis, keepdims=True)
    return (x - m) / jnp.sqrt(v + eps)

def _scatter_add(tgt, idx, src, axis=0):
    return tgt.at[idx].add(src)

def _segment_sum(src, seg, n):
    return jax.ops.segment_sum(src, seg, n)
kernel_name = 'mk_xattn_ffn_d2_seqx_r8_9bba06'

def setup_inputs(seed: int=0):
    np.random.seed(seed)
    _w = jnp.asarray

    def _rec_inputs():
        import jax
        import jax.numpy as jnp
        _rk = jax.random.key(seed)
        x = 0.0002417 + 0.9998 * jax.random.normal(jax.random.fold_in(_rk, 1), (64, 128, 128), jnp.float32)
        _lenS = 128 - jax.random.randint(jax.random.fold_in(_rk, 7), (64,), 0, max(1, 128 // 4) + 1, jnp.int32)
        _lenS2 = 120 - jax.random.randint(jax.random.fold_in(_rk, 8), (64,), 0, max(1, 120 // 4) + 1, jnp.int32)
        _ctx_1024P = jax.random.normal(jax.random.fold_in(_rk, 11), (64, 16, 128), jnp.float32)
        _ctx_1024c = jax.random.dirichlet(jax.random.fold_in(_rk, 511), 0.3 * jnp.ones((16,), jnp.float32), (64, 120))
        _ctx_1024t = jnp.einsum('bsk,bkd->bsd', _ctx_1024c, _ctx_1024P)
        _ctx_1024t = _ctx_1024t * jax.lax.rsqrt(jnp.mean(jnp.square(_ctx_1024t)) + 1e-12) * 0.953939
        ctx_1024 = 7.22013e-05 + 1.00017 * (_ctx_1024t + 0.3 * jax.random.normal(jax.random.fold_in(_rk, 611), (64, 120, 128), jnp.float32))
        _validS = jnp.arange(128)[None, :] < _lenS[:, None]
        _validS2 = jnp.arange(120)[None, :] < _lenS2[:, None]
        _causal = jnp.tril(jnp.ones((128, 128), dtype=bool))
        mask_Bx1xSxS2_if1 = jnp.where(jnp.ones((64, 1, 128, 120), dtype=bool), 1, 0).astype(jnp.int32)
        return (x, ctx_1024, mask_Bx1xSxS2_if1)
    x, ctx_1024, mask_Bx1xSxS2_if1 = _rec_inputs()

    def _L0_xattn_setup():
        import jax, jax.numpy as jnp
        import numpy as np
        D_MODEL = 128
        B, S = (4, 256)
        key = jax.random.key(seed)
        ks = jax.random.split(key, 10)
        s = 1.0 / np.sqrt(D_MODEL)
        return {'k': jax.random.normal(ks[0], (B, S, D_MODEL), jnp.float32), 'v': jax.random.normal(ks[1], (B, S, D_MODEL), jnp.float32), 'q': jax.random.normal(ks[2], (B, S, D_MODEL), jnp.float32), 'Wk': jax.random.normal(ks[3], (D_MODEL, D_MODEL), jnp.float32) * s, 'Wv': jax.random.normal(ks[4], (D_MODEL, D_MODEL), jnp.float32) * s, 'bv': jnp.zeros((D_MODEL,), jnp.float32), 'Wq': jax.random.normal(ks[5], (D_MODEL, D_MODEL), jnp.float32) * s, 'bq': jnp.zeros((D_MODEL,), jnp.float32), 'Wo': jax.random.normal(ks[6], (D_MODEL, D_MODEL), jnp.float32) * s, 'bo': jnp.zeros((D_MODEL,), jnp.float32)}
    _L0_xattn_all = _L0_xattn_setup()
    _L0_xattn_in = {k: v for k, v in _L0_xattn_all.items() if k in ('Wk', 'Wv', 'bv', 'Wq', 'bq', 'Wo', 'bo')}
    del _L0_xattn_all

    def _L0_ffn_setup():
        import jax, jax.numpy as jnp
        import numpy as np
        N_HEADS = 16
        NUM_EXPERTS = 4
        TOP_K = 2
        D_MODEL = 128
        GATE_HID = 128
        key = jax.random.key(seed)
        ks = jax.random.split(key, 12)
        B, T, C, E = (2, 128, D_MODEL, NUM_EXPERTS)
        s = 1.0 / np.sqrt(C)
        return {'hidden_states': jax.random.normal(ks[0], (B, T, C), jnp.float32), 'Wq': jax.random.normal(ks[1], (E, C, C), jnp.float32) * s, 'bq': jnp.zeros((E, C), jnp.float32), 'Wk': jax.random.normal(ks[2], (E, C, C), jnp.float32) * s, 'bk': jnp.zeros((E, C), jnp.float32), 'Wv': jax.random.normal(ks[3], (E, C, C), jnp.float32) * s, 'bv': jnp.zeros((E, C), jnp.float32), 'Wg1': jax.random.normal(ks[4], (C, GATE_HID), jnp.float32) * s, 'bg1': jnp.zeros((GATE_HID,), jnp.float32), 'Wg2': jax.random.normal(ks[5], (GATE_HID, E), jnp.float32) / np.sqrt(GATE_HID), 'bg2': jnp.zeros((E,), jnp.float32), 'Wo': jax.random.normal(ks[6], (C, C), jnp.float32) * s, 'bo': jnp.zeros((C,), jnp.float32)}
    _L0_ffn_all = _L0_ffn_setup()
    _L0_ffn_in = {k: v for k, v in _L0_ffn_all.items() if k in ('Wq', 'bq', 'Wk', 'bk', 'Wv', 'bv', 'Wg1', 'bg1', 'Wg2', 'bg2', 'Wo', 'bo')}
    del _L0_ffn_all

    def _L1_xattn_setup():
        import jax, jax.numpy as jnp
        import numpy as np
        B, S, H, NH = (2, 256, 128, 16)
        DK = H // NH

        def _split_heads(x):
            b, s, _ = x.shape
            return x.reshape(b, s, NH, DK).transpose(0, 2, 1, 3)
        key = jax.random.key(seed)
        ks = jax.random.split(key, 10)
        init = lambda k, shape: jax.random.normal(k, shape, dtype=jnp.float32) * 0.02
        return {'query': jax.random.normal(ks[0], (B, S, H), dtype=jnp.float32), 'key': jax.random.normal(ks[1], (B, S, H), dtype=jnp.float32), 'attn_mask': jnp.ones((B, 1, S, S), dtype=jnp.int32), 'Wq': init(ks[2], (H, H)), 'bq': init(ks[3], (H,)), 'Wk': init(ks[4], (H, H)), 'bk': init(ks[5], (H,)), 'Wv': init(ks[6], (H, H)), 'bv': init(ks[7], (H,)), 'Wo': init(ks[8], (H, H)), 'bo': init(ks[9], (H,))}
    _L1_xattn_all = _L1_xattn_setup()
    _L1_xattn_in = {k: v for k, v in _L1_xattn_all.items() if k in ('Wq', 'bq', 'Wk', 'bk', 'Wv', 'bv', 'Wo', 'bo')}
    del _L1_xattn_all

    def _L1_ffn_setup():
        import jax, jax.numpy as jnp
        import numpy as np
        S, B, H, F, E, K = (256, 2, 128, 256, 8, 2)

        def _moe_forward(hidden_states, router_w, w1, b1, w2, b2):
            s, b, h = hidden_states.shape
            T = s * b
            x = hidden_states.reshape(T, h)
            logits = jnp.einsum('th,eh->te', x, router_w)
            topk_logits, topk_idx = jax.lax.top_k(logits, K)
            probs = jax.nn.softmax(topk_logits, axis=-1)
            combine = jnp.zeros((T, E), dtype=x.dtype)
            combine = combine.at[jnp.arange(T)[:, None], topk_idx].add(probs.astype(x.dtype))
            hmid = jnp.einsum('th,efh->etf', x, w1) + b1[:, None, :]
            hmid = jax.nn.gelu(hmid, approximate=False)
            y = jnp.einsum('etf,ehf->eth', hmid, w2) + b2[:, None, :]
            out = jnp.einsum('eth,te->th', y, combine)
            return out.reshape(s, b, h)
        key = jax.random.key(seed)
        ks = jax.random.split(key, 6)
        std = 0.02
        return {'hidden_states': jax.random.normal(ks[0], (S, B, H), dtype=jnp.float32), 'router_w': jax.random.normal(ks[1], (E, H), dtype=jnp.float32) * std, 'w1': jax.random.normal(ks[2], (E, F, H), dtype=jnp.float32) * (1.0 / np.sqrt(H)), 'b1': jnp.zeros((E, F), dtype=jnp.float32), 'w2': jax.random.normal(ks[3], (E, H, F), dtype=jnp.float32) * (1.0 / np.sqrt(F)), 'b2': jnp.zeros((E, H), dtype=jnp.float32)}
    _L1_ffn_all = _L1_ffn_setup()
    _L1_ffn_in = {k: v for k, v in _L1_ffn_all.items() if k in ('router_w', 'w1', 'b1', 'w2', 'b2')}
    del _L1_ffn_all
    return {'x': x, 'ctx_1024': ctx_1024, 'mask_Bx1xSxS2_if1': mask_Bx1xSxS2_if1, 'L0_xattn_Wk': _L0_xattn_in['Wk'], 'L0_xattn_Wv': _L0_xattn_in['Wv'], 'L0_xattn_bv': _L0_xattn_in['bv'], 'L0_xattn_Wq': _L0_xattn_in['Wq'], 'L0_xattn_bq': _L0_xattn_in['bq'], 'L0_xattn_Wo': _L0_xattn_in['Wo'], 'L0_xattn_bo': _L0_xattn_in['bo'], 'L0_ffn_Wq': _L0_ffn_in['Wq'], 'L0_ffn_bq': _L0_ffn_in['bq'], 'L0_ffn_Wk': _L0_ffn_in['Wk'], 'L0_ffn_bk': _L0_ffn_in['bk'], 'L0_ffn_Wv': _L0_ffn_in['Wv'], 'L0_ffn_bv': _L0_ffn_in['bv'], 'L0_ffn_Wg1': _L0_ffn_in['Wg1'], 'L0_ffn_bg1': _L0_ffn_in['bg1'], 'L0_ffn_Wg2': _L0_ffn_in['Wg2'], 'L0_ffn_bg2': _L0_ffn_in['bg2'], 'L0_ffn_Wo': _L0_ffn_in['Wo'], 'L0_ffn_bo': _L0_ffn_in['bo'], 'L1_xattn_Wq': _L1_xattn_in['Wq'], 'L1_xattn_bq': _L1_xattn_in['bq'], 'L1_xattn_Wk': _L1_xattn_in['Wk'], 'L1_xattn_bk': _L1_xattn_in['bk'], 'L1_xattn_Wv': _L1_xattn_in['Wv'], 'L1_xattn_bv': _L1_xattn_in['bv'], 'L1_xattn_Wo': _L1_xattn_in['Wo'], 'L1_xattn_bo': _L1_xattn_in['bo'], 'L1_ffn_router_w': _L1_ffn_in['router_w'], 'L1_ffn_w1': _L1_ffn_in['w1'], 'L1_ffn_b1': _L1_ffn_in['b1'], 'L1_ffn_w2': _L1_ffn_in['w2'], 'L1_ffn_b2': _L1_ffn_in['b2']}

def reference(x, ctx_1024, mask_Bx1xSxS2_if1, L0_xattn_Wk, L0_xattn_Wv, L0_xattn_bv, L0_xattn_Wq, L0_xattn_bq, L0_xattn_Wo, L0_xattn_bo, L0_ffn_Wq, L0_ffn_bq, L0_ffn_Wk, L0_ffn_bk, L0_ffn_Wv, L0_ffn_bv, L0_ffn_Wg1, L0_ffn_bg1, L0_ffn_Wg2, L0_ffn_bg2, L0_ffn_Wo, L0_ffn_bo, L1_xattn_Wq, L1_xattn_bq, L1_xattn_Wk, L1_xattn_bk, L1_xattn_Wv, L1_xattn_bv, L1_xattn_Wo, L1_xattn_bo, L1_ffn_router_w, L1_ffn_w1, L1_ffn_b1, L1_ffn_w2, L1_ffn_b2):
    import jax
    import jax.numpy as jnp

    def _L0_xattn_ref(k, v, q, Wk, Wv, bv, Wq, bq, Wo, bo):
        import jax, jax.numpy as jnp
        import numpy as np
        D_MODEL = 128
        B, S = (4, 256)
        kp = jnp.einsum('bsd,ed->bse', k, Wk)
        vp = jnp.einsum('bsd,ed->bse', v, Wv) + bv
        qp = jnp.einsum('bsd,ed->bse', q, Wq) + bq
        scale = 1.0 / jnp.sqrt(jnp.float32(kp.shape[-1]))
        scores = jnp.einsum('bqd,bkd->bqk', qp, kp) * scale
        probs = jax.nn.softmax(scores, axis=-1)
        ctx = jnp.einsum('bqk,bkd->bqd', probs, vp)
        return jnp.einsum('bqd,ed->bqe', ctx, Wo) + bo

    def _L0_ffn_ref(hidden_states, Wq, bq, Wk, bk, Wv, bv, Wg1, bg1, Wg2, bg2, Wo, bo):
        import jax, jax.numpy as jnp
        import numpy as np
        N_HEADS = 16
        NUM_EXPERTS = 4
        TOP_K = 2
        D_MODEL = 128
        GATE_HID = 128
        B, T, C = hidden_states.shape
        H = N_HEADS
        D = C // H
        pooled = hidden_states.mean(axis=1)
        logits = jax.nn.relu(pooled @ Wg1 + bg1) @ Wg2 + bg2
        vals, idx = jax.lax.top_k(logits, TOP_K)
        sm = jax.nn.softmax(vals, axis=-1)
        weights = jnp.zeros_like(logits).at[jnp.arange(B)[:, None], idx].set(sm)

        def moe_proj(W, b):
            Wc = jnp.einsum('be,ecd->bcd', weights, W)
            bc = weights @ b
            return jnp.einsum('btc,bcd->btd', hidden_states, Wc) + bc[:, None, :]
        q = moe_proj(Wq, bq).reshape(B, T, H, D)
        k = moe_proj(Wk, bk).reshape(B, T, H, D)
        v = moe_proj(Wv, bv).reshape(B, T, H, D)
        scores = jnp.einsum('bthd,bshd->bhts', q, k) / np.sqrt(D).astype(np.float32)
        attn = jax.nn.softmax(scores, axis=-1)
        out = jnp.einsum('bhts,bshd->bthd', attn, v).reshape(B, T, C)
        return out @ Wo + bo

    def _L1_xattn_ref(query, key, attn_mask, Wq, bq, Wk, bk, Wv, bv, Wo, bo):
        import jax, jax.numpy as jnp
        import numpy as np
        B, S, H, NH = (2, 256, 128, 16)
        DK = H // NH

        def _split_heads(x):
            b, s, _ = x.shape
            return x.reshape(b, s, NH, DK).transpose(0, 2, 1, 3)
        q = _split_heads(query @ Wq.T + bq)
        k = _split_heads(key @ Wk.T + bk)
        v = _split_heads(key @ Wv.T + bv)
        scores = jnp.einsum('bhqd,bhkd->bhqk', q, k) / jnp.sqrt(jnp.float32(DK))
        scores = jnp.where(attn_mask == 0, jnp.float32(-60000.0), scores)
        weights = jax.nn.softmax(scores, axis=-1)
        out = jnp.einsum('bhqk,bhkd->bhqd', weights, v)
        out = out.transpose(0, 2, 1, 3).reshape(query.shape[0], -1, H)
        return out @ Wo.T + bo

    def _L1_ffn_ref(hidden_states, router_w, w1, b1, w2, b2):
        import jax, jax.numpy as jnp
        import numpy as np
        S, B, H, F, E, K = (256, 2, 128, 256, 8, 2)

        def _moe_forward(hidden_states, router_w, w1, b1, w2, b2):
            s, b, h = hidden_states.shape
            T = s * b
            x = hidden_states.reshape(T, h)
            logits = jnp.einsum('th,eh->te', x, router_w)
            topk_logits, topk_idx = jax.lax.top_k(logits, K)
            probs = jax.nn.softmax(topk_logits, axis=-1)
            combine = jnp.zeros((T, E), dtype=x.dtype)
            combine = combine.at[jnp.arange(T)[:, None], topk_idx].add(probs.astype(x.dtype))
            hmid = jnp.einsum('th,efh->etf', x, w1) + b1[:, None, :]
            hmid = jax.nn.gelu(hmid, approximate=False)
            y = jnp.einsum('etf,ehf->eth', hmid, w2) + b2[:, None, :]
            out = jnp.einsum('eth,te->th', y, combine)
            return out.reshape(s, b, h)
        return _moe_forward(hidden_states, router_w, w1, b1, w2, b2)
    x = x + _L0_xattn_ref(ctx_1024, ctx_1024, _layernorm(x, axis=-1), L0_xattn_Wk, L0_xattn_Wv, L0_xattn_bv, L0_xattn_Wq, L0_xattn_bq, L0_xattn_Wo, L0_xattn_bo)
    x = x + _L0_ffn_ref(_layernorm(x, axis=-1), L0_ffn_Wq, L0_ffn_bq, L0_ffn_Wk, L0_ffn_bk, L0_ffn_Wv, L0_ffn_bv, L0_ffn_Wg1, L0_ffn_bg1, L0_ffn_Wg2, L0_ffn_bg2, L0_ffn_Wo, L0_ffn_bo)
    x = x + _L1_xattn_ref(_layernorm(x, axis=-1), ctx_1024, mask_Bx1xSxS2_if1, L1_xattn_Wq, L1_xattn_bq, L1_xattn_Wk, L1_xattn_bk, L1_xattn_Wv, L1_xattn_bv, L1_xattn_Wo, L1_xattn_bo)
    x = x + _L1_ffn_ref(_layernorm(x, axis=-1), L1_ffn_router_w, L1_ffn_w1, L1_ffn_b1, L1_ffn_w2, L1_ffn_b2)
    return x

_drawn_inputs = setup_inputs


def setup_inputs(seed=0):
    import zlib

    import numpy as np

    out = dict(_drawn_inputs(seed))
    spreads = {'L0_xattn_bv': (0.0, 0.1),
     'L0_xattn_bq': (0.0, 0.1),
     'L0_xattn_bo': (0.0, 0.1),
     'L0_ffn_bq': (0.0, 0.463),
     'L0_ffn_bk': (0.0, 2.0),
     'L0_ffn_bv': (0.0, 0.1),
     'L0_ffn_bg1': (0.0, 0.1),
     'L0_ffn_bg2': (0.0, 0.1),
     'L0_ffn_bo': (0.0, 0.1),
     'L1_ffn_b1': (0.0, 0.1),
     'L1_ffn_b2': (0.0, 0.1)}
    factors = {'L1_xattn_Wq': 8.0, 'L1_xattn_bq': 21.82, 'L1_xattn_Wk': 8.0, 'L1_xattn_bk': 64.0}
    for name, (base, spread) in spreads.items():
        noise = np.random.default_rng([zlib.crc32(name.encode()), seed]).standard_normal(out[name].shape)
        drawn = base * np.exp(spread * noise) if base else spread * noise
        out[name] = jnp.asarray(drawn.astype(out[name].dtype))
    for name, factor in factors.items():
        out[name] = (out[name] * factor).astype(out[name].dtype)
    return out
```

```python
from contextlib import ExitStack

import numpy as np

import concourse.bass as bass
from concourse import mybir

ALU = mybir.AluOpType
ACT = mybir.ActivationFunctionType
AX_X = mybir.AxisListType.X
F32 = mybir.dt.float32
BF16 = mybir.dt.bfloat16
I32 = mybir.dt.int32

P = 128
GROUP = 4
HEADS = 16
DH = P // HEADS
HALF = HEADS // 2
VW = 32
EPS = 1e-5
BIG = 1e30
MASKED = -60000.0
HUGE = 3e38
UNITS = 2 * GROUP
STEPS = UNITS + 6
PARTS = (0, 64, 96)


def build(nc, d):
    B, TOK, C = d["x"].shape
    KEYS = d["ctx"].shape[1]
    E0 = d["ffn_bg2"].shape[1]
    E1, HID = d["moe_b1"].shape[1] , d["moe_b1"].shape[2] * P
    FC = HID // P
    NG = B // GROUP
    ctx = ExitStack()
    per = {}

    def sb(name, shape, dt=F32):
        return ctx.enter_context(nc.sbuf_tensor(name, shape, dt))

    def sem(name, per_group=0):
        s = ctx.enter_context(nc.semaphore(name))
        per[name] = per_group
        due[name] = s
        return s

    due = {}

    def at(g, name, n):
        return g * per[name] + n

    with ctx:
        ident = sb("ident", [P, P])
        identb = sb("identb", [P, P], BF16)
        sel = sb("sel", [P, HEADS, P], BF16)
        hmask = sb("hmask", [P, HEADS])
        tri = sb("tri", [P, E1, E1])
        xa_w = sb("xa_w", [P, 4, P])
        xa_b = sb("xa_b", [P, 3])
        bvrep = sb("bvrep", [P, P])
        wvo = sb("wvo", [P, P])
        brow = sb("brow", [P, 3, P])
        bo_a = sb("bo_a", [P, P])
        ff_w = sb("ff_w", [P, E0, 3 * P])
        ff_b = sb("ff_b", [P, 3, E0])
        ff_g1 = sb("ff_g1", [P, P])
        ff_bg1 = sb("ff_bg1", [P, 1])
        ff_g2 = sb("ff_g2", [P, E0])
        ff_bg2 = sb("ff_bg2", [P, E0])
        ff_wo = sb("ff_wo", [P, P])
        xb_w = sb("xb_w", [P, 4, P])
        xb_b = sb("xb_b", [P, 3])
        mo_r = sb("mo_r", [P, E1])
        mo_w1 = sb("mo_w1", [P, E1, HID])
        mo_b1 = sb("mo_b1", [P, E1, FC])
        mo_w2 = sb("mo_w2", [P, E1, FC, P])
        mo_b2 = sb("mo_b2", [P, P])
        powm = sb("powm", [P, GROUP])
        epst = sb("epst", [P, GROUP])
        after_wait = sb("after_wait", [P, 1])

        X = [sb(f"X{i}", [P, GROUP, P]) for i in range(5)]
        XB = [sb(f"XB{i}", [P, GROUP, P]) for i in range(3)]
        ctx_in = sb("ctx_in", [P, GROUP, P])
        msk_in = sb("msk_in", [P, GROUP, KEYS], I32)
        CT = sb("CT", [P, GROUP, P])
        mz = sb("mz", [P, GROUP, KEYS])
        mbig = sb("mbig", [P, GROUP, KEYS], BF16)
        mzT = sb("mzT", [P, GROUP, P])
        anym = sb("anym", [P, GROUP])
        floor0 = sb("floor0", [P, GROUP])
        floor = sb("floor", [P, GROUP])
        bst = [sb(f"bst{i}", [P, GROUP, 6]) for i in range(2)]
        mv = [sb(f"mv{i}", [P, GROUP, 2]) for i in range(2)]
        ve = [sb(f"ve{i}", [P, GROUP]) for i in range(2)]
        rstd = [sb(f"rstd{i}", [P, GROUP]) for i in range(2)]
        xn = [sb(f"xn{i}", [P, GROUP, P]) for i in range(2)]
        XT = sb("XT", [P, GROUP, P])
        XD = sb("XD", [P, GROUP, P])
        qa = sb("qa", [P, GROUP, P])
        ka = sb("ka", [P, GROUP, P])
        va = sb("va", [P, GROUP, P])
        nma = sb("nma", [P, GROUP])
        pa = sb("pa", [P, GROUP, P])
        pta = sb("pta", [P, GROUP, P])
        dena = sb("dena", [P, GROUP])
        rda = sb("rda", [P, GROUP])
        pooled = sb("pooled", [P, GROUP])
        g1 = sb("g1", [P, GROUP])
        g1r = sb("g1r", [P, GROUP, P])
        wc = sb("wc", [P, GROUP, 3 * P])
        bt = sb("bt", [P, GROUP, 3, E0])
        bc = sb("bc", [P, GROUP, 3])
        lg = sb("lg", [P, GROUP, E1])
        gt = sb("gt", [P, GROUP, E1, E1])
        eq = sb("eq", [P, GROUP, E1, E1])
        eqt = sb("eqt", [P, GROUP, E1, E1])
        rk2 = sb("rk2", [P, GROUP, E1, E1])
        rank = sb("rank", [P, GROUP, E1])
        lmx = sb("lmx", [P, GROUP])
        ld = sb("ld", [P, GROUP, E1])
        le = sb("le", [P, GROUP, E1])
        ls = sb("ls", [P, GROUP, E1])
        lsum = sb("lsum", [P, GROUP])
        lrec = sb("lrec", [P, GROUP])
        wgt = sb("wgt", [P, GROUP, E1])
        qt = sb("qt", [P, GROUP, P])
        kt = sb("kt", [P, GROUP, P])
        qm = sb("qm", [P, GROUP, HEADS, P])
        vz = sb("vz", [P, GROUP, HEADS, VW])
        nm = sb("nm", [P, GROUP, HEADS])
        mr = sb("mr", [P, GROUP, P])
        mp = sb("mp", [P, GROUP, P], BF16)
        mres = sb("mres", [P, GROUP, P])
        sd = [sb(f"sd{i}", [P, HALF, P]) for i in range(2)]
        pr = [sb(f"pr{i}", [P, HALF, P]) for i in range(2)]
        pt = [sb(f"pt{i}", [P, HALF, P]) for i in range(2)]
        oa = sb("oa", [P, 2, P])
        ew0 = sb("ew0", [P, GROUP, HEADS])
        ew = sb("ew", [P, GROUP, HEADS])
        mvt = sb("mvt", [P, HEADS, 16])
        osum = sb("osum", [P, HEADS, 16])
        orec = sb("orec", [P, HEADS])
        att = sb("att", [P, HEADS, DH])
        attT = sb("attT", [P, P])
        ct32 = sb("ct32", [P, GROUP, P])
        hid = [sb(f"hid{i}", [P, GROUP * P]) for i in range(2)]
        hsc = [sb(f"hsc{i}", [P, GROUP * P]) for i in range(2)]

        psS = [ctx.enter_context(nc.psum_tensor(f"psS{i}", [P, 2, 512], F32)) for i in range(2)]
        psT = ctx.enter_context(nc.psum_tensor("psT", [P, 2, 512], F32))
        psO = ctx.enter_context(nc.psum_tensor("psO", [P, 512], F32))
        psX = ctx.enter_context(nc.psum_tensor("psX", [P, 512], F32))

        def four(t):
            return t[:, :].rearrange("p (b c) -> p b c", b=GROUP)

        consts = sem("consts")
        fills = sem("fills")
        fold_p = sem("fold_p")
        fold_s = sem("fold_s")
        x_in = sem("x_in", 16)
        c_in = sem("c_in", 16)
        m_in = sem("m_in", 16)
        x_out = sem("x_out", 16)
        ctp = sem("ctp", 1)
        cts = sem("cts", 1)
        mzs = sem("mzs", 5)
        mtp = sem("mtp", 1)
        mts = sem("mts", 1)
        ln_s = sem("ln_s", 4 * 2)
        ln_v = sem("ln_v", 4 * 1)
        ln_r = sem("ln_r", 4 * 1)
        ln_n = sem("ln_n", 4 * GROUP)
        xtp = sem("xtp", 4)
        xts = sem("xts", 4)
        xbs = sem("xbs", 3)
        qa_p = sem("qa_p", 1)
        qa_s = sem("qa_s", 1)
        ka_p = sem("ka_p", 1)
        ka_s = sem("ka_s", 1)
        va_p = sem("va_p", 1)
        va_s = sem("va_s", 1)
        sa_p = sem("sa_p", 1)
        nma_s = sem("nma_s", 1)
        pa_s = sem("pa_s", GROUP)
        pta_p = sem("pta_p", 1)
        pta_s = sem("pta_s", 1)
        oa_p = sem("oa_p", 1)
        rda_s = sem("rda_s", 1)
        x_new = sem("x_new", 3 * GROUP)
        pool_s = sem("pool_s", 1)
        g1_p = sem("g1_p", 1)
        g1_s = sem("g1_s", 1)
        g1r_s = sem("g1r_s", 1)
        lg_p = sem("lg_p", 2)
        tk = sem("tk", 2 * 11)
        le_s = sem("le_s", 2)
        wc_s = sem("wc_s", GROUP * E0)
        bc_s = sem("bc_s", 2)
        q_p = sem("q_p", 2)
        k_p = sem("k_p", 2)
        v_p = sem("v_p", 2)
        q_s = sem("q_s", GROUP + 1)
        k_s = sem("k_s", GROUP + 1)
        v_s = sem("v_s", 4)
        qm_v = sem("qm_v", 2 * 2)
        qm_g = sem("qm_g", 2 * 2)
        s_p = sem("s_p", 2 * UNITS)
        nm_s = sem("nm_s", 2 * UNITS)
        nf_s = sem("nf_s", UNITS)
        sd_s = sem("sd_s", 2 * UNITS)
        pt_p = sem("pt_p", 2 * UNITS)
        pt_s = sem("pt_s", 2 * UNITS)
        pr_s = sem("pr_s", 2 * UNITS)
        pv_p = sem("pv_p", 2 * UNITS)
        oa_s = sem("oa_s", 2 * GROUP)
        ew_v = sem("ew_v", GROUP)
        ew_s = sem("ew_s", GROUP)
        to_p = sem("to_p", 2 * GROUP)
        os_s = sem("os_s", 2 * GROUP)
        or_s = sem("or_s", 2 * GROUP)
        at_s = sem("at_s", 2 * GROUP)
        at_p = sem("at_p", 2 * GROUP)
        atT_s = sem("atT_s", 2 * GROUP)
        out_p = sem("out_p", 2 * GROUP)
        cr_s = sem("cr_s", 2)
        cr_p = sem("cr_p", 1)
        c32_s = sem("c32_s", 1)
        cp_s = sem("cp_s", 4)
        h_p = sem("h_p", E1 * FC)
        cb_p = sem("cb_p", E1)
        h_s = sem("h_s", E1 * FC)
        hs_s = sem("hs_s", E1 * FC)
        y_p = sem("y_p", E1 * FC)
        y_s = sem("y_s", GROUP)

        block = ctx.enter_context(nc.Block())

        LOADS = [(ident, "ident"), (identb, "identb"), (sel, "sel"), (hmask, "hmask"), (tri, "tri"),
                 (xa_w, "xa_w"), (xa_b, "xa_b"), (bvrep, "bvrep"), (brow, "brow"), (ff_w, "ff_w"),
                 (ff_b, "ff_b"), (ff_g1, "ff_g1"), (ff_bg1, "ff_bg1"), (ff_g2, "ff_g2"),
                 (ff_bg2, "ff_bg2"), (ff_wo, "ff_wo"), (xb_w, "xb_w"), (xb_b, "xb_b"), (mo_r, "mo_r"),
                 (mo_w1, "mo_w1"), (mo_b1, "mo_b1"), (mo_w2, "mo_w2")]
        BROADCAST = {"bvrep": P, "ff_bg2": E0, "brow": 3 * P, "tri": E1 * E1}
        ALL_CONSTS = 16 * (len(LOADS) + 1)
        FILLS = 6

        @block.sync
        def _(sp):
            for tile, name in LOADS:
                src = d[name]
                if name in ("ff_bg2", "brow"):
                    sp.dma_start(tile[:], src.partition_broadcast(P)).then_inc(consts, 16)
                else:
                    sp.dma_start(tile[:], src).then_inc(consts, 16)
            sp.wait_ge(fills, FILLS)
            sp.dma_start(mo_b2[0:E1, :], d["mo_b2"]).then_inc(consts, 16)

            def rows(name, first):
                return d[name][bass.ds(first, GROUP), :, :].rearrange("b t c -> t b c")

            sp.sem_inc(x_out, 16)
            sp.dma_start(X[0][:], rows("x", 0)).then_inc(x_in, 16)
            sp.dma_start(ctx_in[0:KEYS, :, :], rows("ctx", 0)).then_inc(c_in, 16)
            sp.dma_start(msk_in[:], rows("mask", 0)).then_inc(m_in, 16)
            with sp.Fori(1, NG) as g:
                sp.wait_ge(ctp, at(g - 1, "ctp", 1))
                sp.dma_start(ctx_in[0:KEYS, :, :], rows("ctx", g * GROUP)).then_inc(c_in, 16)
                sp.wait_ge(mzs, at(g - 1, "mzs", 1))
                sp.dma_start(msk_in[:], rows("mask", g * GROUP)).then_inc(m_in, 16)
                sp.wait_ge(x_new, at(g - 1, "x_new", 1))
                sp.dma_start(X[0][:], rows("x", g * GROUP)).then_inc(x_in, 16)
                sp.wait_ge(y_s, at(g - 1, "y_s", GROUP))
                sp.dma_start(rows("out", g * GROUP - GROUP), X[4][:]).then_inc(x_out, 16)
            sp.wait_ge(y_s, at(NG - 1, "y_s", GROUP))
            sp.dma_start(rows("out", (NG - 1) * GROUP), X[4][:]).then_inc(x_out, 16)
            sp.wait_ge(x_out, 16 + 16 * NG)

        @block.gpsimd
        def _(gp):
            nc.gpsimd.memset(mo_b2[:], 0.0).then_inc(fills, 1)
            nc.gpsimd.memset(vz[:], 0.0).then_inc(fills, 1)
            nc.gpsimd.memset(mr[:], 0.0).then_inc(fills, 1)
            nc.gpsimd.memset(powm[:], -0.5).then_inc(fills, 1)
            nc.gpsimd.memset(epst[:], EPS).then_inc(fills, 1)
            gp.wait_ge(fills, 5)
            vpair = vz[:].rearrange("p b (m u) w -> p (b m) u w", u=2)
            nc.gpsimd.memset(vpair[:, :, 0, DH:DH + 1], 1.0)
            nc.gpsimd.memset(vpair[:, :, 1, 16 + DH:16 + DH + 1], 1.0).then_inc(fills, 1)
            gp.wait_ge(consts, ALL_CONSTS)

            def rstd_of(g, layer):
                k = layer % 2
                gp.wait_ge(ln_s, at(g, "ln_s", 2 * layer + 2))
                nc.gpsimd.tensor_tensor(ve[k][:], mv[k][:, :, 1], epst[:], ALU.add).then_inc(ln_v, 1)
                gp.wait_ge(ln_v, at(g, "ln_v", layer + 1))
                nc.gpsimd.tensor_tensor(rstd[k][:], ve[k][:], powm[:], ALU.pow).then_inc(ln_r, 1)

            def add_bias(g, i):
                bias = bo_a[:] if i == 0 else brow[:, i, :]
                nc.gpsimd.tensor_tensor(XB[i][:], X[i][:],
                                        bias.rearrange("p (o c) -> p o c", o=1).broadcast_to([P, GROUP, P]),
                                        ALU.add).then_inc(xbs, 1)

            def mask_heads(g, which):
                for b in range(2, GROUP):
                    gp.wait_ge(q_s, at(g, "q_s", b + 1 if which == 0 else GROUP + 1))
                    nc.gpsimd.tensor_tensor(
                        qm[:, b, :, :],
                        qt[:, b, :].rearrange("p (o t) -> p o t", o=1).broadcast_to([P, HEADS, P]),
                        hmask[:].rearrange("p (h o) -> p h o", o=1).broadcast_to([P, HEADS, P]),
                        ALU.mult).then_inc(qm_g, 1)

            def branches(g):
                rstd_of(g, 0)
                gp.wait_ge(x_in, at(g, "x_in", 16))
                add_bias(g, 0)
                rstd_of(g, 1)
                add_bias(g, 1)
                mask_heads(g, 0)
                rstd_of(g, 2)
                add_bias(g, 2)
                mask_heads(g, 1)

            gp.wait_ge(fold_s, 2)
            branches(0)
            with gp.Fori(1, NG) as g:
                rstd_of(g - 1, 3)
                branches(g)
            rstd_of(NG - 1, 3)

        @block.scalar
        def _(act):
            act.wait_ge(consts, ALL_CONSTS)
            act.wait_ge(fills, FILLS)
            act.wait_ge(fold_p, 2)
            nc.scalar.activation(wvo[:], psX[:, 0:P], ACT.Copy).then_inc(fold_s, 1)

            def xt_copy(g, layer):
                act.wait_ge(xtp, at(g, "xtp", layer + 1))
                src = (psX, psX, psT[:, 0, :], psT[:, 0, :])[layer]
                nc.scalar.activation(XD[:] if layer == 3 else XT[:], four(src), ACT.Copy).then_inc(xts, 1)

            def top_exp(g, which, n):
                act.wait_ge(tk, at(g, "tk", 11 * which + 7))
                nc.scalar.activation(le[:, :, 0:n], ld[:, :, 0:n], ACT.Exp).then_inc(le_s, 1)

            def hidden(g, first, end):
                if g is None:
                    return
                for n in range(first, end):
                    act.wait_ge(h_p, at(g, "h_p", n + 1))
                    if n >= 2:
                        act.wait_ge(hs_s, at(g, "hs_s", n - 1))
                    nc.scalar.activation(hid[n % 2][:], psS[n % 2][:, 0, :], ACT.Gelu,
                                         bias=mo_b1[:, n // FC, n % FC:n % FC + 1]).then_inc(h_s, 1)

            def v_copy(g, which, nk):
                act.wait_ge(v_p, at(g, "v_p", which + 1))
                src = (psO, psX)[which][0:nk, :].rearrange("p (n u r) -> p n u r", u=2, r=DH)
                dst = vz[0:nk].rearrange("p b (m u) w -> p (b m) u w", u=2)
                for u in range(2):
                    nc.scalar.activation(dst[:, :, u, 16 * u:16 * u + DH], src[:, :, u, :],
                                         ACT.Copy).then_inc(v_s, 1)

            def heads(g, which, nk):
                for n in range(STEPS):
                    i = which * UNITS + n
                    if n < UNITS:
                        act.wait_ge(sd_s, at(g, "sd_s", i + 1))
                        if n >= 2:
                            act.wait_ge(pt_p, at(g, "pt_p", i - 1))
                        nc.scalar.activation(pr[n % 2][:, :, 0:nk], sd[n % 2][:, :, 0:nk],
                                             ACT.Exp).then_inc(pr_s, 1)
                        if which == 1 and n % 2 == 1:
                            b = n // 2
                            act.wait_ge(ew_v, at(g, "ew_v", b + 1))
                            nc.scalar.activation(ew[:, b, :], ew0[:, b, :], ACT.Exp).then_inc(ew_s, 1)
                    if 2 <= n < UNITS + 2:
                        act.wait_ge(pt_p, at(g, "pt_p", i - 1))
                        if n >= 4:
                            act.wait_ge(pv_p, at(g, "pv_p", i - 3))
                        nc.scalar.activation(pt[n % 2][0:nk], psT[0:nk].rearrange(
                            "p a (h t) -> p (a h) t", t=P), ACT.Copy).then_inc(pt_s, 1)
                    if n % 2 == 0 and 4 <= n < UNITS + 4:
                        b = n // 2 - 2
                        act.wait_ge(pv_p, at(g, "pv_p", which * UNITS + 2 * b + 2))
                        nc.scalar.activation(oa[:], psO[:, 0:2 * P].rearrange(
                            "p (a t) -> p a t", a=2), ACT.Copy).then_inc(oa_s, 1)
                    if n % 2 == 0 and 6 <= n:
                        transposed_out(g, which, n // 2 - 3)

            def transposed_out(g, which, b):
                bias = bc[:, b, 2:3] if which == 0 else xb_b[:, 2:3]
                act.wait_ge(at_p, at(g, "at_p", which * GROUP + b + 1))
                nc.scalar.activation(attT[:], psX[:, 0:P], ACT.Identity, bias=bias).then_inc(atT_s, 1)

            def front(a, d_):
                if a is not None:
                    act.wait_ge(ctp, at(a, "ctp", 1))
                    nc.scalar.activation(CT[:, :, 0:KEYS], four(psT[:, 0, :])[:, :, 0:KEYS],
                                         ACT.Copy).then_inc(cts, 1)
                    act.wait_ge(ka_p, at(a, "ka_p", 1))
                    nc.scalar.activation(ka[:, :, 0:KEYS], four(psO)[:, :, 0:KEYS], ACT.Copy).then_inc(ka_s, 1)
                if d_ is not None:
                    xt_copy(d_, 3)
                if a is not None:
                    act.wait_ge(va_p, at(a, "va_p", 1))
                    nc.scalar.activation(va[0:KEYS], four(psX)[0:KEYS], ACT.Copy).then_inc(va_s, 1)
                    xt_copy(a, 0)
                if d_ is not None:
                    top_exp(d_, 1, E1)
                if a is not None:
                    act.wait_ge(nma_s, at(a, "nma_s", 1))
                    for b in range(GROUP):
                        nc.scalar.activation(pa[:, b, 0:KEYS], psT[:, 0, b * P:b * P + KEYS], ACT.Exp,
                                             bias=nma[:, b:b + 1], accum_out=dena[:, b:b + 1]).then_inc(pa_s, 1)
                hidden(d_, 0, 2)
                if a is not None:
                    act.wait_ge(pta_p, at(a, "pta_p", 1))
                    nc.scalar.activation(pta[0:KEYS], four(psT[:, 1, :])[0:KEYS], ACT.Copy).then_inc(pta_s, 1)
                hidden(d_, 2, 6)
                if a is None:
                    return hidden(d_, 6, E1 * FC)
                xt_copy(a, 1)
                hidden(d_, 6, 7)
                act.wait_ge(g1_p, at(a, "g1_p", 1))
                nc.scalar.activation(g1[:], psT[:, 0, 0:GROUP], ACT.Relu, bias=ff_bg1[:, 0:1],
                                     scale=1.0 / TOK).then_inc(g1_s, 1)
                hidden(d_, 7, 8)
                top_exp(a, 0, E0)
                hidden(d_, 8, E1 * FC)
                act.wait_ge(k_p, at(a, "k_p", 1))
                act.wait_ge(bc_s, at(a, "bc_s", 2))
                for b in range(GROUP):
                    nc.scalar.activation(kt[:, b, :], psT[:, 1, b * P:(b + 1) * P], ACT.Identity,
                                         bias=bc[:, b, 1:2]).then_inc(k_s, 1)
                v_copy(a, 0, TOK)

            def back(g):
                heads(g, 0, TOK)
                xt_copy(g, 2)
                act.wait_ge(k_p, at(g, "k_p", 2))
                nc.scalar.activation(kt[:, :, 0:KEYS], four(psO)[:, :, 0:KEYS], ACT.Identity,
                                     bias=xb_b[:, 1:2]).then_inc(k_s, 1)
                v_copy(g, 1, KEYS)
                heads(g, 1, KEYS)

            front(0, None)
            back(0)
            with act.Fori(1, NG) as g:
                front(g, g - 1)
                back(g)
            front(None, NG - 1)

        @block.vector
        def _(ve_):
            dve = ve_
            dve.wait_ge(consts, ALL_CONSTS)
            dve.wait_ge(fills, FILLS)
            dve.wait_ge(fold_s, 1)
            nc.vector.tensor_tensor(bo_a[:], psX[:, P:2 * P], brow[:, 0, :], ALU.add).then_inc(fold_s, 1)

            def statistics(g, layer):
                k = layer % 2
                if layer == 0:
                    dve.wait_ge(x_in, at(g, "x_in", 16))
                else:
                    dve.wait_ge(x_new, at(g, "x_new", layer * GROUP))
                for b in range(GROUP):
                    last = nc.vector.bn_stats(bst[k][:, b, :], X[layer][:, b, :])
                last.then_inc(ln_s, 1)
                dve.wait_ge(ln_s, at(g, "ln_s", 2 * layer + 1))
                nc.vector.memset(after_wait[:], 0.0)
                for b in range(GROUP):
                    last = nc.vector.bn_aggr(mv[k][:, b, :], bst[k][:, b, :])
                last.then_inc(ln_s, 1)

            def normalise(g, layer):
                k = layer % 2
                dve.wait_ge(ln_s, at(g, "ln_s", 2 * layer + 2))
                dve.wait_ge(ln_r, at(g, "ln_r", layer + 1))
                for b in range(GROUP):
                    nc.vector.tensor_scalar(xn[k][:, b, :], X[layer][:, b, :], mv[k][:, b, 0:1],
                                            rstd[k][:, b:b + 1], ALU.subtract, ALU.mult).then_inc(ln_n, 1)

            def top2(g, which, n):
                base = 11 * which
                step = [base]

                def then(ins):
                    ins.then_inc(tk, 1)
                    step[0] += 1
                    dve.wait_ge(tk, at(g, "tk", step[0]))

                dve.wait_ge(lg_p, at(g, "lg_p", which + 1))
                src = psT[:, (0, 1)[which], 0:GROUP * n].rearrange("p (b e) -> p b e", b=GROUP)
                L = lg[:, :, 0:n]
                if which == 0:
                    then(nc.vector.tensor_tensor(
                        L, src, ff_bg2[:].rearrange("p (o e) -> p o e", o=1).broadcast_to([P, GROUP, n]),
                        ALU.add))
                else:
                    then(nc.vector.tensor_copy(L, src))
                other = L.rearrange("p b (o e) -> p b o e", o=1).broadcast_to([P, GROUP, n, n])
                own = L.rearrange("p b (e o) -> p b e o", o=1).broadcast_to([P, GROUP, n, n])
                T = tri[:, 0:n, 0:n].rearrange("p (o e) f -> p o e f", o=1).broadcast_to([P, GROUP, n, n])
                nc.vector.tensor_tensor(gt[:, :, 0:n, 0:n], other, own, ALU.is_gt)
                then(nc.vector.tensor_tensor(eq[:, :, 0:n, 0:n], other, own, ALU.is_equal))
                then(nc.vector.tensor_tensor(eqt[:, :, 0:n, 0:n], eq[:, :, 0:n, 0:n], T, ALU.mult))
                then(nc.vector.tensor_tensor(rk2[:, :, 0:n, 0:n], gt[:, :, 0:n, 0:n],
                                             eqt[:, :, 0:n, 0:n], ALU.add))
                then(nc.vector.tensor_reduce(rank[:, :, 0:n], rk2[:, :, 0:n, 0:n], AX_X, ALU.add))
                then(nc.vector.tensor_reduce(lmx[:], L, AX_X, ALU.max))
                then(nc.vector.tensor_tensor(ld[:, :, 0:n], L, lmx[:].rearrange(
                    "p (b o) -> p b o", o=1).broadcast_to([P, GROUP, n]), ALU.subtract))
                dve.wait_ge(le_s, at(g, "le_s", which + 1))
                then(nc.vector.scalar_tensor_tensor(out=ls[:, :, 0:n], in0=rank[:, :, 0:n], scalar=1.5,
                                                    in1=le[:, :, 0:n], op0=ALU.is_lt, op1=ALU.mult))
                then(nc.vector.tensor_reduce(lsum[:], ls[:, :, 0:n], AX_X, ALU.add))
                then(nc.vector.reciprocal(lrec[:], lsum[:]))
                then(nc.vector.tensor_tensor(wgt[:, :, 0:n], ls[:, :, 0:n], lrec[:].rearrange(
                    "p (b o) -> p b o", o=1).broadcast_to([P, GROUP, n]), ALU.mult))

            def mask_heads(g, which):
                for b in range(2):
                    nc.vector.tensor_tensor(
                        qm[:, b, :, :],
                        qt[:, b, :].rearrange("p (o t) -> p o t", o=1).broadcast_to([P, HEADS, P]),
                        hmask[:].rearrange("p (h o) -> p h o", o=1).broadcast_to([P, HEADS, P]),
                        ALU.mult).then_inc(qm_v, 1)

            def parts(counter, n0, src):
                nc.vector.tensor_copy(mp[:], src[:]).then_inc(counter, 1)
                dve.wait_ge(counter, n0(1))
                nc.vector.tensor_tensor(mres[64:P], src[64:P], mp[64:P], ALU.subtract).then_inc(counter, 1)
                dve.wait_ge(counter, n0(2))
                nc.vector.tensor_copy(mp[64:P], mres[64:P]).then_inc(counter, 1)
                dve.wait_ge(counter, n0(3))
                nc.vector.tensor_tensor(mp[96:P], mres[96:P], mp[96:P], ALU.subtract).then_inc(counter, 1)

            def heads(g, which, nk):
                for n in range(STEPS):
                    if n % 2 == 1 and n >= 7:
                        head_add(g, which, (n - 7) // 2)
                    if n < UNITS:
                        b, half = n // 2, n % 2
                        i = which * UNITS + n
                        dve.wait_ge(s_p, at(g, "s_p", i + 1))
                        src = psS[n % 2][:, :, 0:4 * nk].rearrange("p a (h t) -> p a h t", h=4)
                        m = nm[:, b, half * HALF:(half + 1) * HALF]
                        nc.vector.tensor_reduce(m.rearrange("p (a h) -> p a h", a=2), src, AX_X, ALU.max,
                                                negate=True).then_inc(nm_s, 1)
                        dve.wait_ge(nm_s, at(g, "nm_s", i + 1))
                        if which == 1:
                            nc.vector.tensor_scalar(m, m, floor[:, b:b + 1], None, ALU.min).then_inc(nf_s, 1)
                            dve.wait_ge(nf_s, at(g, "nf_s", n + 1))
                        if n >= 2:
                            dve.wait_ge(pr_s, at(g, "pr_s", i - 1))
                        nc.vector.tensor_tensor(
                            sd[n % 2][:, :, 0:nk].rearrange("p (a h) t -> p a h t", a=2), src,
                            m.rearrange("p (a h o) -> p a h o", a=2, o=1).broadcast_to([P, 2, 4, nk]),
                            ALU.add).then_inc(sd_s, 1)
                        if which == 1 and half == 1:
                            nc.vector.tensor_scalar(ew0[:, b, :], nm[:, b, :], MASKED, None,
                                                    ALU.add).then_inc(ew_v, 1)
                    if n % 2 == 1 and 5 <= n < UNITS + 5:
                        head_out(g, which, (n - 5) // 2)

            def head_out(g, which, b):
                i = which * GROUP + b
                dve.wait_ge(to_p, at(g, "to_p", i + 1))
                O = psX[:, 0:2 * P].rearrange("p (h w) -> p h w", w=16)
                if which == 1:
                    dve.wait_ge(ew_s, at(g, "ew_s", b + 1))
                    M = psX[:, 2 * P:4 * P].rearrange("p (h w) -> p h w", w=16)
                    nc.vector.tensor_tensor(mvt[:], M, ew[:, b, :].rearrange(
                        "p (h o) -> p h o", o=1).broadcast_to([P, HEADS, 16]), ALU.mult).then_inc(os_s, 1)
                    dve.wait_ge(os_s, at(g, "os_s", 2 * b + 1))
                    nc.vector.tensor_tensor(osum[:], O, mvt[:], ALU.add).then_inc(os_s, 1)
                    dve.wait_ge(os_s, at(g, "os_s", 2 * b + 2))
                    O = osum[:]
                nc.vector.reciprocal(orec[:], O[:, :, DH]).then_inc(or_s, 1)
                dve.wait_ge(or_s, at(g, "or_s", i + 1))
                if i >= 1:
                    dve.wait_ge(at_p, at(g, "at_p", i))
                nc.vector.tensor_tensor(att[:], O[:, :, 0:DH], orec[:].rearrange(
                    "p (h o) -> p h o", o=1).broadcast_to([P, HEADS, DH]), ALU.mult).then_inc(at_s, 1)

            def head_add(g, which, b):
                i = which * GROUP + b
                dve.wait_ge(out_p, at(g, "out_p", i + 1))
                dve.wait_ge(xbs, at(g, "xbs", which + 2))
                nc.vector.tensor_tensor(X[which + 2][:, b, :], psX[:, 0:P], XB[which + 1][:, b, :],
                                        ALU.add).then_inc(x_new, 1)

            def scale_hidden(g, first, end):
                if g is None:
                    return
                for n in range(first, end):
                    dve.wait_ge(h_s, at(g, "h_s", n + 1))
                    dve.wait_ge(cb_p, at(g, "cb_p", n // FC + 1))
                    if n >= 2:
                        dve.wait_ge(y_p, at(g, "y_p", n - 1))
                    nc.vector.tensor_tensor(hsc[n % 2][:], psS[0][:, 1, :], hid[n % 2][:],
                                            ALU.mult).then_inc(hs_s, 1)

            def mask_tiles(g):
                dve.wait_ge(m_in, at(g, "m_in", 16))
                nc.vector.tensor_scalar(mz[:], msk_in[:], 0.0, None, ALU.is_equal).then_inc(mzs, 1)
                dve.wait_ge(mzs, at(g, "mzs", 1))
                nc.vector.tensor_scalar(mbig[:], mz[:], -BIG, None, ALU.mult).then_inc(mzs, 1)
                nc.vector.tensor_reduce(anym[:], mz[:], AX_X, ALU.max).then_inc(mzs, 1)
                dve.wait_ge(mzs, at(g, "mzs", 3))
                nc.vector.tensor_scalar(floor0[:], anym[:], -HUGE, HUGE, ALU.mult, ALU.add).then_inc(mzs, 1)
                dve.wait_ge(mzs, at(g, "mzs", 4))
                nc.vector.tensor_scalar(floor[:], floor0[:], -MASKED, None, ALU.add).then_inc(mzs, 1)
                dve.wait_ge(mtp, at(g, "mtp", 1))
                nc.vector.tensor_copy(mzT[0:KEYS], four(psT[:, 1, :])[0:KEYS]).then_inc(mts, 1)

            def front(a, d_):
                if a is not None:
                    mask_tiles(a)
                if d_ is not None:
                    statistics(d_, 3)
                if a is not None:
                    statistics(a, 0)
                if d_ is not None:
                    normalise(d_, 3)
                if a is not None:
                    normalise(a, 0)
                if d_ is not None:
                    top2(d_, 1, E1)
                    nc.vector.tensor_copy(mr[:, :, 0:E1], wgt[:]).then_inc(cr_s, 1)
                    hi = mr[:, :, 64:P].rearrange("p b (s w) -> p b s w", s=2)[:, :, :, 0:E1]
                    nc.vector.tensor_copy(hi, wgt[:].rearrange("p b (o h) -> p b o h", o=1)
                                          .broadcast_to([P, GROUP, 2, E1])).then_inc(cr_s, 1)
                if a is not None:
                    dve.wait_ge(qa_p, at(a, "qa_p", 1))
                    nc.vector.tensor_scalar(qa[:], four(psT[:, 1, :]), xa_b[:, 0:1], float(P) ** -0.5, ALU.add,
                                            ALU.mult).then_inc(qa_s, 1)
                    dve.wait_ge(sa_p, at(a, "sa_p", 1))
                    nc.vector.tensor_reduce(nma[:], four(psT[:, 0, :])[:, :, 0:KEYS], AX_X, ALU.max,
                                            negate=True).then_inc(nma_s, 1)
                if d_ is not None:
                    dve.wait_ge(cr_p, at(d_, "cr_p", 1))
                    nc.vector.tensor_copy(ct32[:], four(psX)).then_inc(c32_s, 1)
                    parts(cp_s, lambda k: at(d_, "cp_s", k), four(psX))
                scale_hidden(d_, 0, 3)
                if a is not None:
                    dve.wait_ge(pa_s, at(a, "pa_s", GROUP))
                    nc.vector.reciprocal(rda[:], dena[:]).then_inc(rda_s, 1)
                    dve.wait_ge(rda_s, at(a, "rda_s", 1))
                    dve.wait_ge(oa_p, at(a, "oa_p", 1))
                    dve.wait_ge(xbs, at(a, "xbs", 1))
                    for b in range(GROUP):
                        nc.vector.scalar_tensor_tensor(out=X[1][:, b, :], in0=psO[:, b * P:(b + 1) * P],
                                                       scalar=rda[:, b:b + 1], in1=XB[0][:, b, :],
                                                       op0=ALU.mult, op1=ALU.add).then_inc(x_new, 1)
                    statistics(a, 1)
                scale_hidden(d_, 3, 5)
                if a is not None:
                    normalise(a, 1)
                scale_hidden(d_, 5, 6)
                if a is not None:
                    dve.wait_ge(xts, at(a, "xts", 2))
                    nc.vector.tensor_reduce(pooled[:], XT[:], AX_X, ALU.add).then_inc(pool_s, 1)
                scale_hidden(d_, 6, 7)
                if a is not None:
                    dve.wait_ge(g1_s, at(a, "g1_s", 1))
                    nc.vector.tensor_copy(g1r[:], g1[:].rearrange("p (b o) -> p b o", o=1)
                                          .broadcast_to([P, GROUP, P])).then_inc(g1r_s, 1)
                scale_hidden(d_, 7, 8)
                if a is not None:
                    top2(a, 0, E0)
                for e in range(E0):
                    if a is not None:
                        mixed_weights(a, e)
                    scale_hidden(d_, 8 + 2 * e, 10 + 2 * e)
                if a is not None:
                    nc.vector.tensor_tensor(
                        bt[:], ff_b[:].rearrange("p (o k) e -> p o k e", o=1).broadcast_to([P, GROUP, 3, E0]),
                        wgt[:, :, 0:E0].rearrange("p b (o e) -> p b o e", o=1).broadcast_to([P, GROUP, 3, E0]),
                        ALU.mult).then_inc(bc_s, 1)
                    dve.wait_ge(bc_s, at(a, "bc_s", 1))
                    nc.vector.tensor_reduce(bc[:], bt[:], AX_X, ALU.add).then_inc(bc_s, 1)
                    dve.wait_ge(bc_s, at(a, "bc_s", 2))
                    dve.wait_ge(q_p, at(a, "q_p", 1))
                    for b in range(GROUP):
                        nc.vector.tensor_scalar(qt[:, b, :], psT[:, 0, b * P:(b + 1) * P], bc[:, b, 0:1],
                                                float(DH) ** -0.5, ALU.add, ALU.mult).then_inc(q_s, 1)
                if d_ is not None:
                    dve.wait_ge(y_p, at(d_, "y_p", E1 * FC))
                    dve.wait_ge(x_out, at(d_, "x_out", 16))
                    for b in range(GROUP):
                        nc.vector.tensor_tensor(X[4][:, b, :], psS[1][:, 1, b * P:(b + 1) * P], X[3][:, b, :],
                                                ALU.add).then_inc(y_s, 1)

            def mixed_weights(g, e):
                for b in range(GROUP):
                    if e == 0:
                        nc.vector.tensor_scalar(wc[:, b, :], ff_w[:, e, :], wgt[:, b, e:e + 1], None,
                                                ALU.mult).then_inc(wc_s, 1)
                    else:
                        dve.wait_ge(wc_s, at(g, "wc_s", (e - 1) * GROUP + b + 1))
                        nc.vector.scalar_tensor_tensor(out=wc[:, b, :], in0=ff_w[:, e, :],
                                                       scalar=wgt[:, b, e:e + 1], in1=wc[:, b, :],
                                                       op0=ALU.mult, op1=ALU.add).then_inc(wc_s, 1)

            def back(g):
                dve.wait_ge(q_s, at(g, "q_s", GROUP))
                mask_heads(g, 0)
                heads(g, 0, TOK)
                statistics(g, 2)
                normalise(g, 2)
                dve.wait_ge(q_p, at(g, "q_p", 2))
                nc.vector.tensor_scalar(qt[:], four(psT[:, 1, :]), xb_b[:, 0:1], float(DH) ** -0.5, ALU.add,
                                        ALU.mult).then_inc(q_s, 1)
                dve.wait_ge(q_s, at(g, "q_s", GROUP + 1))
                mask_heads(g, 1)
                heads(g, 1, KEYS)

            front(0, None)
            back(0)
            with dve.Fori(1, NG) as g:
                front(g, g - 1)
                back(g)
            front(None, NG - 1)

        @block.tensor
        def _(pe):
            def mm(out, lhsT, rhs, start=True, stop=True, **kw):
                return nc.tensor.matmul(out, lhsT, rhs, start=start, stop=stop, **kw)

            pe.wait_ge(consts, ALL_CONSTS)
            pe.wait_ge(fills, FILLS)
            mm(psX[:, 0:P], xa_w[:, 2, :], xa_w[:, 3, :]).then_inc(fold_p, 1)
            mm(psX[:, P:2 * P], bvrep[:], xa_w[:, 3, :]).then_inc(fold_p, 1)
            pe.wait_ge(fold_s, 2)
            def transpose_x(g, layer):
                dst = (psX, psX, psT[:, 0, :], psT[:, 0, :])[layer]
                for b in range(GROUP):
                    pe.wait_ge(ln_n, at(g, "ln_n", layer * GROUP + b + 1))
                    last = nc.tensor.transpose(dst[:, b * P:(b + 1) * P], xn[layer % 2][:, b, :], ident[:])
                last.then_inc(xtp, 1)

            def masked_v(b):
                v = vz[0:KEYS, b, :, :].rearrange("p (m u) w -> p m (u w)", u=2)
                for u in range(2):
                    o = psX[:, 2 * P:4 * P].rearrange("p (m u w) -> p m u w", u=2, w=16)[:, :, u, :]
                    mm(o, mzT[0:KEYS, b, :], v[:, :, u * (VW + 16):u * (VW + 16) + 16])

            def heads(g, which, nk):
                for n in range(STEPS):
                    if n % 2 == 1 and n >= 7:
                        output(g, which, (n - 7) // 2)
                    if n < UNITS:
                        scores(g, which, nk, n)
                    if 2 <= n < UNITS + 2:
                        transpose_probs(g, which, nk, n - 2)
                    if 3 <= n < UNITS + 3:
                        values(g, which, nk, n - 3)
                    if n % 2 == 1 and 5 <= n < UNITS + 5:
                        heads_back(g, which, (n - 5) // 2)
                    if n % 2 == 0 and n >= 6:
                        i = which * GROUP + n // 2 - 3
                        pe.wait_ge(at_s, at(g, "at_s", i + 1))
                        nc.tensor.transpose(psX[:, 0:P], att[:].rearrange("p h c -> p (h c)"),
                                            ident[:]).then_inc(at_p, 1)

            def scores(g, which, nk, n):
                b, half = n // 2, n % 2
                if b < 2:
                    pe.wait_ge(qm_v, at(g, "qm_v", 2 * which + b + 1))
                else:
                    pe.wait_ge(qm_g, at(g, "qm_g", 2 * which + b - 1))
                if n >= 2:
                    pe.wait_ge(sd_s, at(g, "sd_s", which * UNITS + n - 1))
                for a in range(2):
                    if which == 1:
                        mm(psS[n % 2][:, a, 0:4 * nk], identb[:], mbig[:, b, :].rearrange(
                            "p (o k) -> p o k", o=1).broadcast_to([P, 4, nk]), stop=False,
                            skip_group_check=True)
                    for j in range(4):
                        h = half * HALF + 4 * a + j
                        last = mm(psS[n % 2][:, a, j * nk:(j + 1) * nk], qm[:, b, h, :], kt[:, b, 0:nk],
                                  start=which == 0, skip_group_check=which == 1)
                last.then_inc(s_p, 1)

            def transpose_probs(g, which, nk, n):
                i = which * UNITS + n
                pe.wait_ge(pr_s, at(g, "pr_s", i + 1))
                if n >= 1:
                    pe.wait_ge(pt_s, at(g, "pt_s", i))
                for h in range(HALF):
                    last = nc.tensor.transpose(psT[0:nk, h // 4, (h % 4) * P:(h % 4 + 1) * P],
                                               pr[n % 2][:, h, 0:nk], ident[:])
                last.then_inc(pt_p, 1)

            def values(g, which, nk, m):
                b, half = m // 2, m % 2
                pe.wait_ge(pt_s, at(g, "pt_s", which * UNITS + m + 1))
                if m >= 2 and half == 0:
                    pe.wait_ge(oa_s, at(g, "oa_s", which * GROUP + b))
                for u in range(2):
                    for j in range(4):
                        hh = 2 * j + u
                        last = mm(psO[32 * j:32 * j + VW, half * P:(half + 1) * P],
                                  vz[0:nk, b, half * HALF + hh, :], pt[m % 2][0:nk, hh, :],
                                  start=u == 0, stop=u == 1)
                last.then_inc(pv_p, 1)

            def heads_back(g, which, b):
                i = which * GROUP + b
                pe.wait_ge(oa_s, at(g, "oa_s", i + 1))
                if b >= 1:
                    pe.wait_ge(x_new, at(g, "x_new", (which + 1) * GROUP + b))
                if which == 1:
                    masked_v(b)
                for half in range(2):
                    last = nc.tensor.transpose(psX[:, half * P:(half + 1) * P],
                                               oa[:, half, :], ident[:])
                last.then_inc(to_p, 1)

            def output(g, which, b):
                i = which * GROUP + b
                pe.wait_ge(atT_s, at(g, "atT_s", i + 1))
                wo = ff_wo[:] if which == 0 else xb_w[:, 3, :]
                mm(psX[:, 0:P], attT[:], wo).then_inc(out_p, 1)


            def hidden(g, n):
                if n >= 2:
                    pe.wait_ge(h_s, at(g, "h_s", n - 1))
                mm(psS[n % 2][:, 0, :], mo_w1[:, n // FC, (n % FC) * P:(n % FC + 1) * P],
                   XD[:].rearrange("p b t -> p (b t)")).then_inc(h_p, 1)

            def combine(g, e):
                if e >= 1:
                    pe.wait_ge(hs_s, at(g, "hs_s", e * FC))
                mm(psS[0][:, 1, :], sel[:, e, :], mp[:].rearrange("p b t -> p (b t)")).then_inc(cb_p, 1)

            def experts(g, first, end):
                if g is None:
                    return
                for n in range(first, end):
                    if n + 2 < E1 * FC:
                        hidden(g, n + 2)
                    pe.wait_ge(hs_s, at(g, "hs_s", n + 1))
                    if n % FC == FC - 1 and n // FC + 1 < E1:
                        combine(g, n // FC + 1)
                    for b in range(GROUP):
                        last = mm(psS[1][:, 1, b * P:(b + 1) * P], hsc[n % 2][:, b * P:(b + 1) * P],
                                  mo_w2[:, n // FC, n % FC, :], start=False, stop=n == E1 * FC - 1,
                                  skip_group_check=True)
                    last.then_inc(y_p, 1)

            def front(a, d_):
                if a is not None:
                    pe.wait_ge(c_in, at(a, "c_in", 16))
                    for b in range(GROUP):
                        last = nc.tensor.transpose(psT[:, 0, b * P:b * P + KEYS], ctx_in[0:KEYS, b, :],
                                                   ident[0:KEYS, 0:KEYS])
                    last.then_inc(ctp, 1)
                    pe.wait_ge(mzs, at(a, "mzs", 1))
                    for b in range(GROUP):
                        last = nc.tensor.transpose(psT[0:KEYS, 1, b * P:(b + 1) * P], mz[:, b, :], ident[:])
                    last.then_inc(mtp, 1)
                    pe.wait_ge(cts, at(a, "cts", 1))
                    mm(four(psO)[:, :, 0:KEYS], xa_w[:, 1, :], CT[:, :, 0:KEYS]).then_inc(ka_p, 1)
                if d_ is not None:
                    transpose_x(d_, 3)
                    pe.wait_ge(xts, at(d_, "xts", 4))
                    hidden(d_, 0)
                    if a is not None:
                        pe.wait_ge(mts, at(a, "mts", 1))
                    for b in range(GROUP):
                        last = mm(psT[:, 1, b * E1:(b + 1) * E1], XD[:, b, :], mo_r[:])
                    last.then_inc(lg_p, 1)
                if a is not None:
                    for b in range(GROUP):
                        last = mm(psX[0:KEYS, b * P:(b + 1) * P], CT[:, b, 0:KEYS], wvo[:])
                    last.then_inc(va_p, 1)
                    pe.wait_ge(va_s, at(a, "va_s", 1))
                    transpose_x(a, 0)
                if d_ is not None:
                    hidden(d_, 1)
                if a is not None:
                    pe.wait_ge(xts, at(a, "xts", 1))
                    if d_ is not None:
                        pe.wait_ge(tk, at(d_, "tk", 11 + 1))
                    else:
                        pe.wait_ge(mts, at(a, "mts", 1))
                    mm(psT[:, 1, :], xa_w[:, 0, :], XT[:].rearrange("p b t -> p (b t)")).then_inc(qa_p, 1)
                    pe.wait_ge(qa_s, at(a, "qa_s", 1))
                    pe.wait_ge(ka_s, at(a, "ka_s", 1))
                    for b in range(GROUP):
                        last = mm(psT[:, 0, b * P:b * P + KEYS], qa[:, b, :], ka[:, b, 0:KEYS])
                    last.then_inc(sa_p, 1)
                if d_ is not None:
                    pe.wait_ge(cr_s, at(d_, "cr_s", 2))
                    for b in range(GROUP):
                        last = nc.tensor.transpose(psX[:, b * P:(b + 1) * P], mr[:, b, :], ident[:])
                    last.then_inc(cr_p, 1)
                    pe.wait_ge(cp_s, at(d_, "cp_s", 4))
                    combine(d_, 0)
                    for b in range(GROUP):
                        mm(psS[1][:, 1, b * P:(b + 1) * P], ct32[:, b, :], mo_b2[:], start=b == 0, stop=False,
                           skip_group_check=True)
                experts(d_, 0, 2)
                if a is not None:
                    for b in range(GROUP):
                        pe.wait_ge(pa_s, at(a, "pa_s", b + 1))
                        last = nc.tensor.transpose(psT[0:KEYS, 1, b * P:(b + 1) * P], pa[:, b, 0:KEYS], ident[:])
                    last.then_inc(pta_p, 1)
                experts(d_, 2, 3)
                if a is not None:
                    pe.wait_ge(pta_s, at(a, "pta_s", 1))
                    for b in range(GROUP):
                        last = mm(psO[:, b * P:(b + 1) * P], pta[0:KEYS, b, :], va[0:KEYS, b, :])
                    last.then_inc(oa_p, 1)
                experts(d_, 3, 5)
                if a is not None:
                    transpose_x(a, 1)
                experts(d_, 5, 6)
                if a is not None:
                    pe.wait_ge(pool_s, at(a, "pool_s", 1))
                    mm(psT[:, 0, 0:GROUP], ff_g1[:], pooled[:]).then_inc(g1_p, 1)
                experts(d_, 6, 7)
                if a is not None:
                    pe.wait_ge(g1r_s, at(a, "g1r_s", 1))
                    for b in range(GROUP):
                        last = mm(psT[:, 0, b * E0:(b + 1) * E0], g1r[:, b, :], ff_g2[:])
                    last.then_inc(lg_p, 1)
                experts(d_, 7, E1 * FC)
                if a is not None:
                    for b in range(GROUP):
                        pe.wait_ge(wc_s, at(a, "wc_s", (E0 - 1) * GROUP + b + 1))
                        mq = mm(psT[:, 0, b * P:(b + 1) * P], wc[:, b, 0:P], XT[:, b, :])
                        mk = mm(psT[:, 1, b * P:(b + 1) * P], wc[:, b, P:2 * P], XT[:, b, :])
                        mv_ = mm(psO[:, b * P:(b + 1) * P], XT[:, b, :], wc[:, b, 2 * P:3 * P])
                    mq.then_inc(q_p, 1)
                    mk.then_inc(k_p, 1)
                    mv_.then_inc(v_p, 1)

            def back(g):
                pe.wait_ge(k_s, at(g, "k_s", GROUP))
                pe.wait_ge(v_s, at(g, "v_s", 2))
                heads(g, 0, TOK)
                transpose_x(g, 2)
                pe.wait_ge(xts, at(g, "xts", 3))
                mm(psT[:, 1, :], xb_w[:, 0, :], XT[:].rearrange("p b t -> p (b t)")).then_inc(q_p, 1)
                mm(four(psO)[:, :, 0:KEYS], xb_w[:, 1, :], CT[:, :, 0:KEYS]).then_inc(k_p, 1)
                for b in range(GROUP):
                    last = mm(psX[0:KEYS, b * P:(b + 1) * P], CT[:, b, 0:KEYS], xb_w[:, 2, :])
                last.then_inc(v_p, 1)
                pe.wait_ge(k_s, at(g, "k_s", GROUP + 1))
                pe.wait_ge(v_s, at(g, "v_s", 4))
                heads(g, 1, KEYS)

            front(0, None)
            back(0)
            with pe.Fori(1, NG) as g:
                front(g, g - 1)
                back(g)
            front(None, NG - 1)


def lay_out(inputs):
    f = {k: np.asarray(v) for k, v in inputs.items()}
    T = np.ascontiguousarray
    w1, w2 = f["L1_ffn_w1"], f["L1_ffn_w2"]
    E1, HID, _ = w1.shape
    FC = HID // P
    sel = np.zeros((P, HEADS, P), np.float32)
    for h in range(HEADS):
        for p0 in PARTS:
            sel[p0 + h, h, :] = 1.0
    hmask = np.zeros((P, HEADS), np.float32)
    for h in range(HEADS):
        hmask[h * DH:(h + 1) * DH, h] = 1.0
    tri = np.zeros((P, E1, E1), np.float32)
    for e in range(E1):
        tri[:, e, :e] = 1.0
    bf = mybir.dt.np(BF16)
    eye = np.eye(P, dtype=np.float32)
    a = {
        "x": f["x"], "ctx": f["ctx_1024"], "mask": f["mask_Bx1xSxS2_if1"].reshape(f["x"].shape[0], P, -1),
        "ident": eye, "identb": eye.astype(bf), "sel": sel.astype(bf), "hmask": hmask, "tri": tri,
        "xa_w": T(np.stack([f["L0_xattn_Wq"].T, f["L0_xattn_Wk"].T, f["L0_xattn_Wv"], f["L0_xattn_Wo"].T], 1)),
        "xa_b": T(np.stack([f["L0_xattn_bq"], f["L0_xattn_bv"], f["L0_xattn_bv"]], 1)),
        "bvrep": T(np.broadcast_to(f["L0_xattn_bv"][:, None], (P, P))),
        "brow": T(np.stack([f["L0_xattn_bo"], f["L0_ffn_bo"], f["L1_xattn_bo"]])),
        "ff_w": T(np.concatenate([f["L0_ffn_Wq"], f["L0_ffn_Wk"], f["L0_ffn_Wv"]], 2).transpose(1, 0, 2)),
        "ff_b": T(np.stack([f["L0_ffn_bq"], f["L0_ffn_bk"], f["L0_ffn_bv"]]).transpose(2, 0, 1)),
        "ff_g1": f["L0_ffn_Wg1"], "ff_bg1": T(f["L0_ffn_bg1"][:, None]), "ff_g2": f["L0_ffn_Wg2"],
        "ff_bg2": f["L0_ffn_bg2"], "ff_wo": f["L0_ffn_Wo"],
        "xb_w": T(np.stack([f["L1_xattn_" + w].T for w in ("Wq", "Wk", "Wv", "Wo")], 1)),
        "xb_b": T(np.stack([f["L1_xattn_" + b] for b in ("bq", "bk", "bv")], 1)),
        "mo_r": T(f["L1_ffn_router_w"].T), "mo_w1": T(w1.transpose(2, 0, 1)),
        "mo_b1": T(f["L1_ffn_b1"].reshape(E1, FC, P).transpose(2, 0, 1)),
        "mo_w2": T(w2.reshape(E1, P, FC, P).transpose(3, 0, 2, 1)), "mo_b2": f["L1_ffn_b2"],
    }
    return a


def kernel(**inputs):
    import concourse.bacc as bacc
    from concourse.bass_utils import run_bass_kernel_spmd

    nc = bacc.Bacc("TRN2", target_bir_lowering=False, num_devices=1)
    arrays, d = {}, {}
    for name, a in lay_out(inputs).items():
        arrays[f"in_{name}"] = a
        d[name] = nc.dram_tensor(f"in_{name}", a.shape, mybir.dt.from_np(a.dtype), kind="ExternalInput").ap()
    d["out"] = nc.dram_tensor("out_x", d["x"].shape, F32, kind="ExternalOutput").ap()

    class Shaped:
        def __init__(self, shape):
            self.shape = shape
    E1 = arrays["in_mo_b1"].shape[1]
    d["ffn_bg2"] = Shaped((1, arrays["in_ff_bg2"].shape[0]))
    d["moe_b1"] = Shaped((1, E1, arrays["in_mo_b1"].shape[2]))
    build(nc, d)
    r = run_bass_kernel_spmd(nc, [arrays], core_ids=[0])
    return r.results[0]["out_x"]
```

```python
from contextlib import ExitStack

import numpy as np

import concourse.bass as bass
from concourse import mybir

ALU = mybir.AluOpType
ACT = mybir.ActivationFunctionType
AX_X = mybir.AxisListType.X
F32 = mybir.dt.float32
BF16 = mybir.dt.bfloat16
I32 = mybir.dt.int32

P = 128
GROUP = 4
HEADS = 16
DH = P // HEADS
HALF = HEADS // 2
VW = 32
EPS = 1e-5
BIG = 1e30
MASKED = -60000.0
HUGE = 3e38
UNITS = 2 * GROUP
LATER = UNITS + 2
STEPS = LATER + UNITS + 7
QUADS = HEADS // 4
PARTS = (0, 64, 96)


def build(nc, d):
    B, TOK, C = d["x"].shape
    KEYS = d["ctx"].shape[1]
    E0 = d["ffn_bg2"].shape[1]
    E1, HID = d["moe_b1"].shape[1] , d["moe_b1"].shape[2] * P
    FC = HID // P
    NG = B // GROUP
    ctx = ExitStack()
    per = {}

    def sb(name, shape, dt=F32):
        return ctx.enter_context(nc.sbuf_tensor(name, shape, dt))

    def sem(name, per_group=0):
        s = ctx.enter_context(nc.semaphore(name))
        per[name] = per_group
        due[name] = s
        return s

    due = {}

    def at(g, name, n):
        return g * per[name] + n

    with ctx:
        ident = sb("ident", [P, P])
        identb = sb("identb", [P, P], BF16)
        sel = sb("sel", [P, HEADS, P], BF16)
        gmask = sb("gmask", [P, QUADS])
        rmask = sb("rmask", [P, 4])
        tri = sb("tri", [P, E1, E1])
        xa_w = sb("xa_w", [P, 4, P])
        xa_b = sb("xa_b", [P, 3])
        bvrep = sb("bvrep", [P, P])
        wvo = sb("wvo", [P, P])
        brow = sb("brow", [P, 3, P])
        bo_a = sb("bo_a", [P, P])
        ff_w = sb("ff_w", [P, E0, 3 * P])
        ff_b = sb("ff_b", [P, 3, E0])
        ff_g1 = sb("ff_g1", [P, P])
        ff_bg1 = sb("ff_bg1", [P, 1])
        ff_g2 = sb("ff_g2", [P, E0])
        ff_bg2 = sb("ff_bg2", [P, E0])
        ff_wo = sb("ff_wo", [P, P])
        xb_w = sb("xb_w", [P, 4, P])
        xb_b = sb("xb_b", [P, 3])
        mo_r = sb("mo_r", [P, E1])
        mo_w1 = sb("mo_w1", [P, E1, HID])
        mo_b1 = sb("mo_b1", [P, E1, FC])
        mo_w2 = sb("mo_w2", [P, E1, FC, P])
        mo_b2 = sb("mo_b2", [P, P])
        powm = sb("powm", [P, GROUP])
        epst = sb("epst", [P, GROUP])
        after_wait = sb("after_wait", [P, 1])

        X = [sb(f"X{i}", [P, GROUP, P]) for i in range(5)]
        XB = [sb(f"XB{i}", [P, GROUP, P]) for i in range(3)]
        ctx_in = sb("ctx_in", [P, GROUP, P])
        msk_in = sb("msk_in", [P, GROUP, KEYS], I32)
        CT = sb("CT", [P, GROUP, P])
        mz = sb("mz", [P, GROUP, KEYS])
        mbig = sb("mbig", [P, GROUP, KEYS], BF16)
        mzT = sb("mzT", [P, GROUP, P])
        anym = sb("anym", [P, GROUP])
        floor0 = sb("floor0", [P, GROUP])
        floor = sb("floor", [P, GROUP])
        bst = [sb(f"bst{i}", [P, GROUP, 6]) for i in range(3)]
        mv = [sb(f"mv{i}", [P, GROUP, 2]) for i in range(3)]
        ve = [sb(f"ve{i}", [P, GROUP]) for i in range(3)]
        rstd = [sb(f"rstd{i}", [P, GROUP]) for i in range(3)]
        xn = [sb(f"xn{i}", [P, GROUP, P]) for i in range(3)]
        XT = sb("XT", [P, GROUP, P])
        XD = sb("XD", [P, GROUP, P])
        qa = sb("qa", [P, GROUP, P])
        ka = sb("ka", [P, GROUP, P])
        va = sb("va", [P, GROUP, P])
        nma = sb("nma", [P, GROUP])
        pa = sb("pa", [P, GROUP, P])
        pta = sb("pta", [P, GROUP, P])
        dena = sb("dena", [P, GROUP])
        rda = sb("rda", [P, GROUP])
        pooled = sb("pooled", [P, GROUP])
        g1 = sb("g1", [P, GROUP])
        g1r = sb("g1r", [P, GROUP, P])
        wc = sb("wc", [P, GROUP, 3 * P])
        bt = sb("bt", [P, GROUP, 3, E0])
        bc = sb("bc", [P, GROUP, 3])
        lg = sb("lg", [P, GROUP, E1])
        gt = sb("gt", [P, GROUP, E1, E1])
        eq = sb("eq", [P, GROUP, E1, E1])
        eqt = sb("eqt", [P, GROUP, E1, E1])
        rk2 = sb("rk2", [P, GROUP, E1, E1])
        rank = sb("rank", [P, GROUP, E1])
        lmx = sb("lmx", [P, GROUP])
        ld = sb("ld", [P, GROUP, E1])
        le = sb("le", [P, GROUP, E1])
        ls = sb("ls", [P, GROUP, E1])
        lsum = sb("lsum", [P, GROUP])
        lrec = sb("lrec", [P, GROUP])
        wgt = sb("wgt", [P, GROUP, E1])
        qg = sb("qg", [P, GROUP, QUADS, P])
        km = [sb(f"km{i}", [P, GROUP, 4, P]) for i in range(2)]
        vz = [sb(f"vz{i}", [P, GROUP, HEADS, VW]) for i in range(2)]
        kb_c = sb("kb_c", [P, 4])
        kb_b = sb("kb_b", [P, GROUP, 4])
        nm = sb("nm", [P, GROUP, HEADS])
        mr = sb("mr", [P, GROUP, P])
        mp = sb("mp", [P, GROUP, P], BF16)
        mres = sb("mres", [P, GROUP, P])
        sd = [sb(f"sd{i}", [P, 4, P]) for i in range(2)]
        pr = [sb(f"pr{i}", [P, HALF, P]) for i in range(2)]
        pt = [sb(f"pt{i}", [P, HALF, P]) for i in range(2)]
        oa = sb("oa", [P, 2, P])
        ew0 = sb("ew0", [P, GROUP, HEADS])
        ew = sb("ew", [P, GROUP, HEADS])
        mvt = sb("mvt", [P, HEADS, 16])
        osum = sb("osum", [P, HEADS, 16])
        orec = sb("orec", [P, HEADS])
        att = sb("att", [P, HEADS, DH])
        attT = sb("attT", [P, P])
        ct32 = sb("ct32", [P, GROUP, P])
        hid = [sb(f"hid{i}", [P, GROUP * P]) for i in range(2)]
        hsc = [sb(f"hsc{i}", [P, GROUP * P]) for i in range(2)]

        psS = [ctx.enter_context(nc.psum_tensor(f"psS{i}", [P, 2, 512], F32)) for i in range(2)]
        psT = ctx.enter_context(nc.psum_tensor("psT", [P, 2, 512], F32))
        psO = ctx.enter_context(nc.psum_tensor("psO", [P, 512], F32))
        psX = ctx.enter_context(nc.psum_tensor("psX", [P, 512], F32))

        def four(t):
            return t[:, :].rearrange("p (b c) -> p b c", b=GROUP)

        consts = sem("consts")
        fills = sem("fills")
        fold_p = sem("fold_p")
        fold_s = sem("fold_s")
        x_in = sem("x_in", 16)
        c_in = sem("c_in", 16)
        m_in = sem("m_in", 16)
        x_out = sem("x_out", 16)
        ctp = sem("ctp", 1)
        cts = sem("cts", 1)
        mzs = sem("mzs", 5)
        mtp = sem("mtp", 1)
        mts = sem("mts", 1)
        ln_s = sem("ln_s", 4)
        lb_s = sem("lb_s", 4 * GROUP)
        ln_v = sem("ln_v", 2)
        lb_v = sem("lb_v", 2 * GROUP)
        ln_r = sem("ln_r", 2)
        lb_r = sem("lb_r", 2 * GROUP)
        ln_n = sem("ln_n", 2 * GROUP)
        lb_n = sem("lb_n", 2 * GROUP)
        xtp = sem("xtp", 2)
        xts = sem("xts", 2)
        xdp = sem("xdp", 1)
        xds = sem("xds", 1)
        xcp = sem("xcp", GROUP)
        xcs = sem("xcs", GROUP)
        xbs = sem("xbs", 3)
        qa_p = sem("qa_p", 1)
        qa_s = sem("qa_s", 1)
        ka_p = sem("ka_p", 1)
        ka_s = sem("ka_s", 1)
        va_p = sem("va_p", 1)
        va_s = sem("va_s", 1)
        sa_p = sem("sa_p", 1)
        nma_s = sem("nma_s", 1)
        pa_s = sem("pa_s", GROUP)
        pta_p = sem("pta_p", 1)
        pta_s = sem("pta_s", 1)
        oa_p = sem("oa_p", 1)
        rda_s = sem("rda_s", 1)
        xa_new = sem("xa_new", GROUP)
        x_new = sem("x_new", 2 * GROUP)
        pool_s = sem("pool_s", 1)
        g1_p = sem("g1_p", 1)
        g1_s = sem("g1_s", 1)
        g1r_s = sem("g1r_s", 1)
        lg_p = sem("lg_p", 2)
        tk = sem("tk", 2 * 10)
        le_s = sem("le_s", 2)
        wc_s = sem("wc_s", GROUP * E0)
        bc_s = sem("bc_s", 3)
        q_p = sem("q_p", 1)
        k_p = sem("k_p", 1)
        v_p = sem("v_p", 1)
        q_s = sem("q_s", GROUP)
        k_s = sem("k_s", GROUP * 4)
        v_s = sem("v_s", 2)
        qc_p = sem("qc_p", GROUP)
        kc_p = sem("kc_p", 1)
        vc_p = sem("vc_p", 1)
        qc_s = sem("qc_s", GROUP)
        kc_s = sem("kc_s", 4)
        vc_s = sem("vc_s", 2)
        s_p = sem("s_p", 2 * UNITS)
        nm_s = sem("nm_s", 2 * UNITS)
        nf_s = sem("nf_s", UNITS)
        sd_s = sem("sd_s", 2 * UNITS)
        pt_p = sem("pt_p", 2 * UNITS)
        pt_s = sem("pt_s", 2 * UNITS)
        pr_s = sem("pr_s", 2 * UNITS)
        pv_p = sem("pv_p", 2 * UNITS)
        oa_s = sem("oa_s", 2 * GROUP)
        ew_v = sem("ew_v", GROUP)
        ew_s = sem("ew_s", GROUP)
        to_p = sem("to_p", 2 * GROUP)
        os_s = sem("os_s", 2 * GROUP)
        or_s = sem("or_s", 2 * GROUP)
        at_s = sem("at_s", 2 * GROUP)
        at_p = sem("at_p", 2 * GROUP)
        atT_s = sem("atT_s", 2 * GROUP)
        out_p = sem("out_p", 2 * GROUP)
        cr_s = sem("cr_s", 2)
        cr_p = sem("cr_p", 1)
        c32_s = sem("c32_s", 1)
        cp_s = sem("cp_s", 4)
        h_p = sem("h_p", E1 * FC)
        cb_p = sem("cb_p", E1)
        h_s = sem("h_s", E1 * FC)
        hs_s = sem("hs_s", E1 * FC)
        y_p = sem("y_p", E1 * FC)
        y_s = sem("y_s", GROUP)

        block = ctx.enter_context(nc.Block())

        LOADS = [(ident, "ident"), (identb, "identb"), (sel, "sel"), (gmask, "gmask"), (rmask, "rmask"), (tri, "tri"),
                 (xa_w, "xa_w"), (xa_b, "xa_b"), (bvrep, "bvrep"), (brow, "brow"), (ff_w, "ff_w"),
                 (ff_b, "ff_b"), (ff_g1, "ff_g1"), (ff_bg1, "ff_bg1"), (ff_g2, "ff_g2"),
                 (ff_bg2, "ff_bg2"), (ff_wo, "ff_wo"), (xb_w, "xb_w"), (xb_b, "xb_b"), (mo_r, "mo_r"),
                 (mo_w1, "mo_w1"), (mo_b1, "mo_b1"), (mo_w2, "mo_w2")]
        ALL_CONSTS = 16 * (len(LOADS) + 1)
        FILLS = 7
        LAST = E1 * FC - 3

        @block.sync
        def _(sp):
            for tile, name in LOADS:
                src = d[name]
                if name in ("ff_bg2", "brow"):
                    sp.dma_start(tile[:], src.partition_broadcast(P)).then_inc(consts, 16)
                else:
                    sp.dma_start(tile[:], src).then_inc(consts, 16)
            sp.wait_ge(fills, FILLS)
            sp.dma_start(mo_b2[0:E1, :], d["mo_b2"]).then_inc(consts, 16)

            def rows(name, first):
                return d[name][bass.ds(first, GROUP), :, :].rearrange("b t c -> t b c")

            sp.sem_inc(x_out, 16)
            sp.dma_start(X[0][:], rows("x", 0)).then_inc(x_in, 16)
            sp.dma_start(ctx_in[0:KEYS, :, :], rows("ctx", 0)).then_inc(c_in, 16)
            sp.dma_start(msk_in[:], rows("mask", 0)).then_inc(m_in, 16)
            with sp.Fori(1, NG) as g:
                sp.wait_ge(ctp, at(g - 1, "ctp", 1))
                sp.dma_start(ctx_in[0:KEYS, :, :], rows("ctx", g * GROUP)).then_inc(c_in, 16)
                sp.wait_ge(mzs, at(g - 1, "mzs", 1))
                sp.dma_start(msk_in[:], rows("mask", g * GROUP)).then_inc(m_in, 16)
                sp.wait_ge(xa_new, at(g - 1, "xa_new", GROUP))
                sp.dma_start(X[0][:], rows("x", g * GROUP)).then_inc(x_in, 16)
                sp.wait_ge(y_s, at(g - 1, "y_s", GROUP))
                sp.dma_start(rows("out", g * GROUP - GROUP), X[4][:]).then_inc(x_out, 16)
            sp.wait_ge(y_s, at(NG - 1, "y_s", GROUP))
            sp.dma_start(rows("out", (NG - 1) * GROUP), X[4][:]).then_inc(x_out, 16)
            sp.wait_ge(x_out, 16 + 16 * NG)

        @block.gpsimd
        def _(gp):
            nc.gpsimd.memset(mo_b2[:], 0.0).then_inc(fills, 1)
            for v in vz:
                nc.gpsimd.memset(v[:], 0.0).then_inc(fills, 1)
            nc.gpsimd.memset(mr[:], 0.0).then_inc(fills, 1)
            nc.gpsimd.memset(powm[:], -0.5).then_inc(fills, 1)
            nc.gpsimd.memset(epst[:], EPS).then_inc(fills, 1)
            gp.wait_ge(fills, 6)
            for v in vz:
                pair = v[:].rearrange("p b (m u) w -> p (b m) u w", u=2)
                nc.gpsimd.memset(pair[:, :, 0, DH:DH + 1], 1.0)
                last = nc.gpsimd.memset(pair[:, :, 1, 16 + DH:16 + DH + 1], 1.0)
            last.then_inc(fills, 1)
            gp.wait_ge(consts, ALL_CONSTS)

            def rstd_of(g, layer):
                gp.wait_ge(ln_s, at(g, "ln_s", 2 * layer + 2))
                nc.gpsimd.tensor_tensor(ve[layer][:], mv[layer][:, :, 1], epst[:], ALU.add).then_inc(ln_v, 1)
                gp.wait_ge(ln_v, at(g, "ln_v", layer + 1))
                nc.gpsimd.tensor_tensor(rstd[layer][:], ve[layer][:], powm[:], ALU.pow).then_inc(ln_r, 1)

            def rstd_batch(g, w, b):
                i = w * GROUP + b
                k = 2 * w
                one = slice(b, b + 1)
                gp.wait_ge(lb_s, at(g, "lb_s", 2 * i + 2))
                nc.gpsimd.tensor_tensor(ve[k][:, one], mv[k][:, one, 1], epst[:, one], ALU.add).then_inc(lb_v, 1)
                gp.wait_ge(lb_v, at(g, "lb_v", i + 1))
                nc.gpsimd.tensor_tensor(rstd[k][:, one], ve[k][:, one], powm[:, one], ALU.pow).then_inc(lb_r, 1)

            def add_bias(g, i):
                bias = bo_a[:] if i == 0 else brow[:, i, :]
                nc.gpsimd.tensor_tensor(XB[i][:], X[i][:],
                                        bias.rearrange("p (o c) -> p o c", o=1).broadcast_to([P, GROUP, P]),
                                        ALU.add).then_inc(xbs, 1)

            def attention(g, nxt):
                for b in range(GROUP):
                    rstd_batch(g, 0, b)
                add_bias(g, 2)
                if nxt is not None:
                    branch_a_inputs(nxt)
                for b in range(GROUP):
                    rstd_batch(g, 1, b)
                if nxt is not None:
                    branch_b_inputs(nxt)

            def branch_a_inputs(g):
                rstd_of(g, 0)
                gp.wait_ge(x_in, at(g, "x_in", 16))
                add_bias(g, 0)

            def branch_b_inputs(g):
                rstd_of(g, 1)
                add_bias(g, 1)

            gp.wait_ge(fold_s, 2)
            branch_a_inputs(0)
            branch_b_inputs(0)
            with gp.Fori(0, NG - 1) as g:
                attention(g, g + 1)
            attention(NG - 1, None)

        @block.scalar
        def _(act):
            act.wait_ge(consts, ALL_CONSTS)
            act.wait_ge(fills, FILLS)
            act.wait_ge(fold_p, 2)
            nc.scalar.activation(wvo[:], psX[:, 0:P], ACT.Copy).then_inc(fold_s, 1)

            def top_exp(g, which, n):
                act.wait_ge(tk, at(g, "tk", 10 * which + 3))
                nc.scalar.activation(le[:, :, 0:n], ld[:, :, 0:n], ACT.Exp).then_inc(le_s, 1)

            def hidden(g, first, end):
                if g is None:
                    return
                for n in range(first, end):
                    act.wait_ge(h_p, at(g, "h_p", n + 1))
                    if n >= 2:
                        act.wait_ge(hs_s, at(g, "hs_s", n - 1))
                    nc.scalar.activation(hid[n % 2][:], psS[n % 2][:, 0, :], ACT.Gelu,
                                         bias=mo_b1[:, n // FC, n % FC:n % FC + 1]).then_inc(h_s, 1)

            def v_copy(w, src, nk, done):
                src = src[0:nk, :].rearrange("p (n u r) -> p n u r", u=2, r=DH)
                dst = vz[w][0:nk].rearrange("p b (m u) w -> p (b m) u w", u=2)
                for u in range(2):
                    nc.scalar.activation(dst[:, :, u, 16 * u:16 * u + DH], src[:, :, u, :],
                                         ACT.Copy).then_inc(done, 1)

            def k_copy_c(g, first, end):
                for r in range(first, end):
                    nc.scalar.activation(km[1][:, :, r, 0:KEYS], four(psX)[:, :, 0:KEYS], ACT.Identity,
                                         bias=kb_c[:, r:r + 1], scale=rmask[:, r:r + 1]).then_inc(kc_s, 1)

            def attention(g, nxt):
                for s in range(STEPS):
                    if s % 2 == 0 and 10 <= s < 10 + 2 * GROUP:
                        b = (s - 10) // 2
                        act.wait_ge(xcp, at(g, "xcp", b + 1))
                        nc.scalar.activation(XT[:, b, :], psS[0][:, 0, 0:P], ACT.Copy).then_inc(xcs, 1)
                    for w in range(2):
                        n = s - w * LATER
                        nk = (TOK, KEYS)[w]
                        i = w * UNITS + n
                        if 2 <= n < UNITS + 2:
                            act.wait_ge(pt_p, at(g, "pt_p", i - 1))
                            if i >= 4:
                                act.wait_ge(pv_p, at(g, "pv_p", i - 3))
                            nc.scalar.activation(pt[n % 2][0:nk], psT[0:nk].rearrange(
                                "p a (h t) -> p (a h) t", t=P), ACT.Copy).then_inc(pt_s, 1)
                        if n % 2 == 0 and 4 <= n < UNITS + 4:
                            act.wait_ge(pv_p, at(g, "pv_p", i - 2))
                            nc.scalar.activation(oa[:], psO[:, 0:2 * P].rearrange(
                                "p (a t) -> p a t", a=2), ACT.Copy).then_inc(oa_s, 1)
                    for w in range(2):
                        n = s - w * LATER
                        if 0 <= n < UNITS:
                            probabilities(g, w, n)
                        if n % 2 == 0 and 6 <= n < UNITS + 6:
                            transposed_out(g, w, n // 2 - 3)
                    if nxt is not None:
                        branch_a(nxt, s)

            def branch_a(a, s):
                if s == 18:
                    act.wait_ge(ctp, at(a, "ctp", 1))
                    nc.scalar.activation(CT[:, :, 0:KEYS], four(psS[0][:, 0, :])[:, :, 0:KEYS],
                                         ACT.Copy).then_inc(cts, 1)
                if s == 19:
                    act.wait_ge(ka_p, at(a, "ka_p", 1))
                    nc.scalar.activation(ka[:, :, 0:KEYS], four(psS[1][:, 0, :])[:, :, 0:KEYS],
                                         ACT.Copy).then_inc(ka_s, 1)
                    act.wait_ge(xtp, at(a, "xtp", 1))
                    nc.scalar.activation(XT[:], four(psS[0][:, 1, :]), ACT.Copy).then_inc(xts, 1)
                    act.wait_ge(va_p, at(a, "va_p", 1))
                    nc.scalar.activation(va[0:KEYS], four(psS[1][:, 1, :])[0:KEYS], ACT.Copy).then_inc(va_s, 1)
                if s == 21:
                    act.wait_ge(nma_s, at(a, "nma_s", 1))
                    for b in range(GROUP):
                        nc.scalar.activation(pa[:, b, 0:KEYS], psS[1][:, 0, b * P:b * P + KEYS], ACT.Exp,
                                             bias=nma[:, b:b + 1], accum_out=dena[:, b:b + 1]).then_inc(pa_s, 1)
                if s == 22:
                    act.wait_ge(pta_p, at(a, "pta_p", 1))
                    nc.scalar.activation(pta[0:KEYS], four(psS[0][:, 1, :])[0:KEYS], ACT.Copy).then_inc(pta_s, 1)

            def probabilities(g, w, n):
                i = w * UNITS + n
                nk = (TOK, KEYS)[w]
                if w == 0:
                    act.wait_ge(nm_s, at(g, "nm_s", i + 1))
                else:
                    act.wait_ge(nf_s, at(g, "nf_s", n + 1))
                if i >= 2:
                    act.wait_ge(pt_p, at(g, "pt_p", i - 1))
                for r in range(4):
                    h = n % 2 * HALF + 4 + r
                    nc.scalar.activation(pr[n % 2][:, 4 + r, 0:nk], psS[n % 2][:, 1, r * nk:(r + 1) * nk],
                                         ACT.Exp, bias=nm[:, n // 2, h:h + 1])
                act.wait_ge(sd_s, at(g, "sd_s", i + 1))
                nc.scalar.activation(pr[n % 2][:, 0:4, 0:nk], sd[n % 2][:, :, 0:nk], ACT.Exp).then_inc(pr_s, 1)
                if w == 1 and n % 2 == 1:
                    b = n // 2
                    act.wait_ge(ew_v, at(g, "ew_v", b + 1))
                    nc.scalar.activation(ew[:, b, :], ew0[:, b, :], ACT.Exp).then_inc(ew_s, 1)

            def transposed_out(g, w, b):
                bias = bc[:, b, 2:3] if w == 0 else xb_b[:, 2:3]
                act.wait_ge(at_p, at(g, "at_p", w * GROUP + b + 1))
                nc.scalar.activation(attT[:], psX[:, 0:P], ACT.Identity, bias=bias).then_inc(atT_s, 1)

            def front(a, d_):
                if d_ is not None:
                    act.wait_ge(xdp, at(d_, "xdp", 1))
                    nc.scalar.activation(XD[:], four(psT[:, 0, :]), ACT.Copy).then_inc(xds, 1)
                if a is not None:
                    act.wait_ge(xtp, at(a, "xtp", 2))
                    nc.scalar.activation(XT[:], four(psO), ACT.Copy).then_inc(xts, 1)
                    act.wait_ge(kc_p, at(a, "kc_p", 1))
                    k_copy_c(a, 0, 2)
                if d_ is not None:
                    top_exp(d_, 1, E1)
                if a is not None:
                    k_copy_c(a, 2, 4)
                    act.wait_ge(vc_p, at(a, "vc_p", 1))
                    v_copy(1, psT[:, 0, :], KEYS, vc_s)
                    act.wait_ge(g1_p, at(a, "g1_p", 1))
                    nc.scalar.activation(g1[:], psO[:, 0:GROUP], ACT.Relu, bias=ff_bg1[:, 0:1],
                                         scale=1.0 / TOK).then_inc(g1_s, 1)
                hidden(d_, 0, 3)
                if a is None:
                    return hidden(d_, 3, E1 * FC)
                top_exp(a, 0, E0)
                hidden(d_, 3, LAST)
                act.wait_ge(bc_s, at(a, "bc_s", 3))
                act.wait_ge(k_p, at(a, "k_p", 1))
                for b in range(GROUP):
                    for r in range(4):
                        nc.scalar.activation(km[0][:, b, r, :], psT[:, 1, b * P:(b + 1) * P], ACT.Identity,
                                             bias=kb_b[:, b, r:r + 1], scale=rmask[:, r:r + 1]).then_inc(k_s, 1)
                    if b < 3:
                        hidden(d_, LAST + b, LAST + b + 1)
                act.wait_ge(v_p, at(a, "v_p", 1))
                v_copy(0, psO, TOK, v_s)

            act.wait_ge(fold_s, 3)
            for s in range(STEPS):
                branch_a(0, s)
            front(0, None)
            with act.Fori(1, NG) as g:
                attention(g - 1, g)
                front(g, g - 1)
            attention(NG - 1, None)
            front(None, NG - 1)

        @block.vector
        def _(ve_):
            dve = ve_
            dve.wait_ge(consts, ALL_CONSTS)
            dve.wait_ge(fills, FILLS)
            dve.wait_ge(fold_s, 1)
            nc.vector.tensor_tensor(bo_a[:], psX[:, P:2 * P], brow[:, 0, :], ALU.add).then_inc(fold_s, 1)
            nc.vector.tensor_tensor(kb_c[:], rmask[:], xb_b[:, 1:2].broadcast_to([P, 4]),
                                    ALU.mult).then_inc(fold_s, 1)

            def statistics(g, layer):
                if layer == 0:
                    dve.wait_ge(x_in, at(g, "x_in", 16))
                else:
                    dve.wait_ge(xa_new, at(g, "xa_new", GROUP))
                for b in range(GROUP):
                    last = nc.vector.bn_stats(bst[layer][:, b, :], X[layer][:, b, :])
                last.then_inc(ln_s, 1)
                dve.wait_ge(ln_s, at(g, "ln_s", 2 * layer + 1))
                nc.vector.memset(after_wait[:], 0.0)
                for b in range(GROUP):
                    last = nc.vector.bn_aggr(mv[layer][:, b, :], bst[layer][:, b, :])
                last.then_inc(ln_s, 1)

            def normalise(g, layer):
                dve.wait_ge(ln_s, at(g, "ln_s", 2 * layer + 2))
                dve.wait_ge(ln_r, at(g, "ln_r", layer + 1))
                for b in range(GROUP):
                    nc.vector.tensor_scalar(xn[layer][:, b, :], X[layer][:, b, :], mv[layer][:, b, 0:1],
                                            rstd[layer][:, b:b + 1], ALU.subtract, ALU.mult).then_inc(ln_n, 1)

            def statistics_batch(g, w, b):
                i = w * GROUP + b
                k = 2 * w
                dve.wait_ge(x_new, at(g, "x_new", i + 1))
                nc.vector.bn_stats(bst[k][:, b, :], X[w + 2][:, b, :]).then_inc(lb_s, 1)
                dve.wait_ge(lb_s, at(g, "lb_s", 2 * i + 1))
                nc.vector.memset(after_wait[:], 0.0)
                nc.vector.bn_aggr(mv[k][:, b, :], bst[k][:, b, :]).then_inc(lb_s, 1)

            def normalise_batch(g, w, b):
                i = w * GROUP + b
                k = 2 * w
                dve.wait_ge(lb_r, at(g, "lb_r", i + 1))
                nc.vector.tensor_scalar(xn[k][:, b, :], X[w + 2][:, b, :], mv[k][:, b, 0:1],
                                        rstd[k][:, b:b + 1], ALU.subtract, ALU.mult).then_inc(lb_n, 1)

            def top2_ranks(g, which, n):
                base = 10 * which
                dve.wait_ge(lg_p, at(g, "lg_p", which + 1))
                src = psT[:, 1, 0:GROUP * n].rearrange("p (b e) -> p b e", b=GROUP)
                L = lg[:, :, 0:n]
                if which == 0:
                    nc.vector.tensor_tensor(
                        L, src, ff_bg2[:].rearrange("p (o e) -> p o e", o=1).broadcast_to([P, GROUP, n]),
                        ALU.add).then_inc(tk, 1)
                else:
                    nc.vector.tensor_copy(L, src).then_inc(tk, 1)
                dve.wait_ge(tk, at(g, "tk", base + 1))
                other = L.rearrange("p b (o e) -> p b o e", o=1).broadcast_to([P, GROUP, n, n])
                own = L.rearrange("p b (e o) -> p b e o", o=1).broadcast_to([P, GROUP, n, n])
                T = tri[:, 0:n, 0:n].rearrange("p (o e) f -> p o e f", o=1).broadcast_to([P, GROUP, n, n])
                nc.vector.tensor_reduce(lmx[:], L, AX_X, ALU.max)
                nc.vector.tensor_tensor(gt[:, :, 0:n, 0:n], other, own, ALU.is_gt)
                nc.vector.tensor_tensor(eq[:, :, 0:n, 0:n], other, own, ALU.is_equal).then_inc(tk, 1)
                dve.wait_ge(tk, at(g, "tk", base + 2))
                nc.vector.tensor_tensor(ld[:, :, 0:n], L, lmx[:].rearrange(
                    "p (b o) -> p b o", o=1).broadcast_to([P, GROUP, n]), ALU.subtract).then_inc(tk, 1)
                nc.vector.tensor_tensor(eqt[:, :, 0:n, 0:n], eq[:, :, 0:n, 0:n], T, ALU.mult).then_inc(tk, 1)
                dve.wait_ge(tk, at(g, "tk", base + 4))
                nc.vector.tensor_tensor(rk2[:, :, 0:n, 0:n], gt[:, :, 0:n, 0:n], eqt[:, :, 0:n, 0:n],
                                        ALU.add).then_inc(tk, 1)
                dve.wait_ge(tk, at(g, "tk", base + 5))
                nc.vector.tensor_reduce(rank[:, :, 0:n], rk2[:, :, 0:n, 0:n], AX_X, ALU.add).then_inc(tk, 1)

            def top2_weights(g, which, n):
                base = 10 * which
                dve.wait_ge(tk, at(g, "tk", base + 6))
                dve.wait_ge(le_s, at(g, "le_s", which + 1))
                nc.vector.scalar_tensor_tensor(out=ls[:, :, 0:n], in0=rank[:, :, 0:n], scalar=1.5,
                                               in1=le[:, :, 0:n], op0=ALU.is_lt, op1=ALU.mult).then_inc(tk, 1)
                dve.wait_ge(tk, at(g, "tk", base + 7))
                nc.vector.tensor_reduce(lsum[:], ls[:, :, 0:n], AX_X, ALU.add).then_inc(tk, 1)
                dve.wait_ge(tk, at(g, "tk", base + 8))
                nc.vector.reciprocal(lrec[:], lsum[:]).then_inc(tk, 1)
                dve.wait_ge(tk, at(g, "tk", base + 9))
                nc.vector.tensor_tensor(wgt[:, :, 0:n], ls[:, :, 0:n], lrec[:].rearrange(
                    "p (b o) -> p b o", o=1).broadcast_to([P, GROUP, n]), ALU.mult).then_inc(tk, 1)
                dve.wait_ge(tk, at(g, "tk", base + 10))

            def parts(counter, n0, src):
                nc.vector.tensor_copy(mp[:], src[:]).then_inc(counter, 1)
                dve.wait_ge(counter, n0(1))
                nc.vector.tensor_tensor(mres[64:P], src[64:P], mp[64:P], ALU.subtract).then_inc(counter, 1)
                dve.wait_ge(counter, n0(2))
                nc.vector.tensor_copy(mp[64:P], mres[64:P]).then_inc(counter, 1)
                dve.wait_ge(counter, n0(3))
                nc.vector.tensor_tensor(mp[96:P], mres[96:P], mp[96:P], ALU.subtract).then_inc(counter, 1)

            def attention(g, nxt):
                for s in range(STEPS):
                    if s % 2 == 0 and 10 <= s < 10 + 2 * GROUP:
                        b = (s - 10) // 2
                        dve.wait_ge(qc_p, at(g, "qc_p", b + 1))
                        group_heads(b, psS[0][:, 1, 0:P], xb_b[:, 0:1], qc_s)
                    for w in range(2):
                        if 0 <= s - w * LATER < UNITS:
                            less_maximum(g, w, s - w * LATER)
                    for w in range(2):
                        n = s - w * LATER
                        if n % 2 == 1 and 7 <= n < UNITS + 7:
                            head_add(g, w, (n - 7) // 2)
                            statistics_batch(g, w, (n - 7) // 2)
                    for w in range(2):
                        n = s - w * LATER
                        if n % 2 == 1 and 5 <= n < UNITS + 5:
                            head_out(g, w, (n - 5) // 2)
                        if n % 2 == 0 and 8 <= n < UNITS + 8:
                            normalise_batch(g, w, (n - 8) // 2)
                    if nxt is not None:
                        branch_a(nxt, s)

            def branch_a(a, s):
                if s == 16:
                    statistics(a, 0)
                if s == 17:
                    normalise(a, 0)
                if s == 20:
                    dve.wait_ge(qa_p, at(a, "qa_p", 1))
                    nc.vector.tensor_scalar(qa[:], four(psS[0][:, 0, :]), xa_b[:, 0:1], float(P) ** -0.5,
                                            ALU.add, ALU.mult).then_inc(qa_s, 1)
                if s == 21:
                    dve.wait_ge(sa_p, at(a, "sa_p", 1))
                    nc.vector.tensor_reduce(nma[:], four(psS[1][:, 0, :])[:, :, 0:KEYS], AX_X, ALU.max,
                                            negate=True).then_inc(nma_s, 1)
                if s == 23:
                    dve.wait_ge(pa_s, at(a, "pa_s", GROUP))
                    nc.vector.reciprocal(rda[:], dena[:]).then_inc(rda_s, 1)
                    dve.wait_ge(rda_s, at(a, "rda_s", 1))
                    dve.wait_ge(oa_p, at(a, "oa_p", 1))
                    dve.wait_ge(xbs, at(a, "xbs", 1))
                    for b in range(GROUP):
                        nc.vector.scalar_tensor_tensor(
                            out=X[1][:, b, :], in0=psS[1][:, 1, b * P:(b + 1) * P], scalar=rda[:, b:b + 1],
                            in1=XB[0][:, b, :], op0=ALU.mult, op1=ALU.add).then_inc(xa_new, 1)
                if s == 24:
                    statistics(a, 1)

            def group_heads(b, src, bias, done):
                nc.vector.scalar_tensor_tensor(
                    out=qg[:, b], in0=src.rearrange("p (o t) -> p o t", o=1).broadcast_to([P, QUADS, P]),
                    scalar=bias, in1=gmask[:].rearrange("p (j o) -> p j o", o=1).broadcast_to([P, QUADS, P]),
                    op0=ALU.add, op1=ALU.mult).then_inc(done, 1)

            def less_maximum(g, w, n):
                b, half = n // 2, n % 2
                i = w * UNITS + n
                nk = (TOK, KEYS)[w]
                dve.wait_ge(s_p, at(g, "s_p", i + 1))
                src = psS[n % 2][:, :, 0:4 * nk].rearrange("p a (h t) -> p a h t", h=4)
                m = nm[:, b, half * HALF:(half + 1) * HALF]
                nc.vector.tensor_reduce(m.rearrange("p (a h) -> p a h", a=2), src, AX_X, ALU.max,
                                        negate=True).then_inc(nm_s, 1)
                dve.wait_ge(nm_s, at(g, "nm_s", i + 1))
                if w == 1:
                    nc.vector.tensor_scalar(m, m, floor[:, b:b + 1], None, ALU.min).then_inc(nf_s, 1)
                    dve.wait_ge(nf_s, at(g, "nf_s", n + 1))
                if i >= 2:
                    dve.wait_ge(pr_s, at(g, "pr_s", i - 1))
                nc.vector.tensor_tensor(
                    sd[n % 2][:, :, 0:nk], src[:, 0],
                    m[:, 0:4].rearrange("p (h o) -> p h o", o=1).broadcast_to([P, 4, nk]),
                    ALU.add).then_inc(sd_s, 1)
                if w == 1 and half == 1:
                    nc.vector.tensor_scalar(ew0[:, b, :], nm[:, b, :], MASKED, None, ALU.add).then_inc(ew_v, 1)

            def head_out(g, which, b):
                i = which * GROUP + b
                dve.wait_ge(to_p, at(g, "to_p", i + 1))
                O = psX[:, 0:2 * P].rearrange("p (h w) -> p h w", w=16)
                if which == 1:
                    dve.wait_ge(ew_s, at(g, "ew_s", b + 1))
                    M = psX[:, 2 * P:4 * P].rearrange("p (h w) -> p h w", w=16)
                    nc.vector.tensor_tensor(mvt[:], M, ew[:, b, :].rearrange(
                        "p (h o) -> p h o", o=1).broadcast_to([P, HEADS, 16]), ALU.mult).then_inc(os_s, 1)
                    dve.wait_ge(os_s, at(g, "os_s", 2 * b + 1))
                    nc.vector.tensor_tensor(osum[:], O, mvt[:], ALU.add).then_inc(os_s, 1)
                    dve.wait_ge(os_s, at(g, "os_s", 2 * b + 2))
                    O = osum[:]
                nc.vector.reciprocal(orec[:], O[:, :, DH]).then_inc(or_s, 1)
                dve.wait_ge(or_s, at(g, "or_s", i + 1))
                if i >= 1:
                    dve.wait_ge(at_p, at(g, "at_p", i))
                nc.vector.tensor_tensor(att[:], O[:, :, 0:DH], orec[:].rearrange(
                    "p (h o) -> p h o", o=1).broadcast_to([P, HEADS, DH]), ALU.mult).then_inc(at_s, 1)

            def head_add(g, which, b):
                i = which * GROUP + b
                dve.wait_ge(out_p, at(g, "out_p", i + 1))
                dve.wait_ge(xbs, at(g, "xbs", which + 2))
                nc.vector.tensor_tensor(X[which + 2][:, b, :], psX[:, 0:P], XB[which + 1][:, b, :],
                                        ALU.add).then_inc(x_new, 1)

            def scale_hidden(g, first, end):
                if g is None:
                    return
                for n in range(first, end):
                    dve.wait_ge(h_s, at(g, "h_s", n + 1))
                    dve.wait_ge(cb_p, at(g, "cb_p", n // FC + 1))
                    if n >= 2:
                        dve.wait_ge(y_p, at(g, "y_p", n - 1))
                    nc.vector.tensor_tensor(hsc[n % 2][:], psS[0][:, 1, :], hid[n % 2][:],
                                            ALU.mult).then_inc(hs_s, 1)

            def mask_tiles(g):
                dve.wait_ge(m_in, at(g, "m_in", 16))
                nc.vector.tensor_scalar(mz[:], msk_in[:], 0.0, None, ALU.is_equal).then_inc(mzs, 1)
                dve.wait_ge(mzs, at(g, "mzs", 1))
                nc.vector.tensor_scalar(mbig[:], mz[:], -BIG, None, ALU.mult).then_inc(mzs, 1)
                nc.vector.tensor_reduce(anym[:], mz[:], AX_X, ALU.max).then_inc(mzs, 1)
                dve.wait_ge(mzs, at(g, "mzs", 3))
                nc.vector.tensor_scalar(floor0[:], anym[:], -HUGE, HUGE, ALU.mult, ALU.add).then_inc(mzs, 1)
                dve.wait_ge(mzs, at(g, "mzs", 4))
                nc.vector.tensor_scalar(floor[:], floor0[:], -MASKED, None, ALU.add).then_inc(mzs, 1)
                dve.wait_ge(mtp, at(g, "mtp", 1))
                nc.vector.tensor_copy(mzT[0:KEYS], four(psO)[0:KEYS]).then_inc(mts, 1)

            def front(a, d_):
                if a is not None:
                    normalise(a, 1)
                if d_ is not None:
                    top2_ranks(d_, 1, E1)
                if a is not None:
                    dve.wait_ge(xts, at(a, "xts", 2))
                    nc.vector.tensor_reduce(pooled[:], XT[:], AX_X, ALU.add).then_inc(pool_s, 1)
                if d_ is not None:
                    top2_weights(d_, 1, E1)
                    nc.vector.tensor_copy(mr[:, :, 0:E1], wgt[:]).then_inc(cr_s, 1)
                    hi = mr[:, :, 64:P].rearrange("p b (s w) -> p b s w", s=2)[:, :, :, 0:E1]
                    nc.vector.tensor_copy(hi, wgt[:].rearrange("p b (o h) -> p b o h", o=1)
                                          .broadcast_to([P, GROUP, 2, E1])).then_inc(cr_s, 1)
                if a is not None:
                    dve.wait_ge(g1_s, at(a, "g1_s", 1))
                    nc.vector.tensor_copy(g1r[:], g1[:].rearrange("p (b o) -> p b o", o=1)
                                          .broadcast_to([P, GROUP, P])).then_inc(g1r_s, 1)
                if d_ is not None:
                    dve.wait_ge(cr_p, at(d_, "cr_p", 1))
                    nc.vector.tensor_copy(ct32[:], four(psX)).then_inc(c32_s, 1)
                    parts(cp_s, lambda k: at(d_, "cp_s", k), four(psX))
                scale_hidden(d_, 0, 1)
                if a is not None:
                    top2_ranks(a, 0, E0)
                scale_hidden(d_, 1, 2)
                if a is not None:
                    top2_weights(a, 0, E0)
                scale_hidden(d_, 2, 4)
                for e in range(E0):
                    if a is not None:
                        mixed_weights(a, e)
                    scale_hidden(d_, 4 + 2 * e, 6 + 2 * e)
                if a is not None:
                    nc.vector.tensor_tensor(
                        bt[:], ff_b[:].rearrange("p (o k) e -> p o k e", o=1).broadcast_to([P, GROUP, 3, E0]),
                        wgt[:, :, 0:E0].rearrange("p b (o e) -> p b o e", o=1).broadcast_to([P, GROUP, 3, E0]),
                        ALU.mult).then_inc(bc_s, 1)
                    dve.wait_ge(bc_s, at(a, "bc_s", 1))
                    nc.vector.tensor_reduce(bc[:], bt[:], AX_X, ALU.add).then_inc(bc_s, 1)
                    dve.wait_ge(bc_s, at(a, "bc_s", 2))
                    nc.vector.tensor_tensor(kb_b[:], bc[:, :, 1:2].broadcast_to([P, GROUP, 4]),
                                            rmask[:].rearrange("p (o r) -> p o r", o=1)
                                            .broadcast_to([P, GROUP, 4]), ALU.mult).then_inc(bc_s, 1)
                scale_hidden(d_, 12, LAST)
                if a is not None:
                    mask_tiles(a)
                    dve.wait_ge(q_p, at(a, "q_p", 1))
                for b in range(GROUP):
                    if a is not None:
                        group_heads(b, psT[:, 0, b * P:(b + 1) * P], bc[:, b, 0:1], q_s)
                    if b < 3:
                        scale_hidden(d_, LAST + b, LAST + b + 1)
                if d_ is not None:
                    dve.wait_ge(y_p, at(d_, "y_p", E1 * FC))
                    dve.wait_ge(x_out, at(d_, "x_out", 16))
                    for b in range(GROUP):
                        nc.vector.tensor_tensor(X[4][:, b, :], psS[1][:, 1, b * P:(b + 1) * P], X[3][:, b, :],
                                                ALU.add).then_inc(y_s, 1)

            def mixed_weights(g, e):
                for b in range(GROUP):
                    if e == 0:
                        nc.vector.tensor_scalar(wc[:, b, :], ff_w[:, e, :], wgt[:, b, e:e + 1], None,
                                                ALU.mult).then_inc(wc_s, 1)
                    else:
                        dve.wait_ge(wc_s, at(g, "wc_s", (e - 1) * GROUP + b + 1))
                        nc.vector.scalar_tensor_tensor(out=wc[:, b, :], in0=ff_w[:, e, :],
                                                       scalar=wgt[:, b, e:e + 1], in1=wc[:, b, :],
                                                       op0=ALU.mult, op1=ALU.add).then_inc(wc_s, 1)

            for s in range(STEPS):
                branch_a(0, s)
            front(0, None)
            with dve.Fori(1, NG) as g:
                attention(g - 1, g)
                front(g, g - 1)
            attention(NG - 1, None)
            front(None, NG - 1)

        @block.tensor
        def _(pe):
            def mm(out, lhsT, rhs, start=True, stop=True, **kw):
                return nc.tensor.matmul(out, lhsT, rhs, start=start, stop=stop, **kw)

            pe.wait_ge(consts, ALL_CONSTS)
            pe.wait_ge(fills, FILLS)
            mm(psX[:, 0:P], xa_w[:, 2, :], xa_w[:, 3, :]).then_inc(fold_p, 1)
            mm(psX[:, P:2 * P], bvrep[:], xa_w[:, 3, :]).then_inc(fold_p, 1)
            pe.wait_ge(fold_s, 2)
            def transpose_x(g, layer, dst):
                for b in range(GROUP):
                    pe.wait_ge(ln_n, at(g, "ln_n", layer * GROUP + b + 1))
                    last = nc.tensor.transpose(dst[:, b * P:(b + 1) * P], xn[layer][:, b, :], ident[:])
                last.then_inc(xtp, 1)

            def masked_v(b):
                v = vz[1][0:KEYS, b, :, :].rearrange("p (m u) w -> p m (u w)", u=2)
                for u in range(2):
                    o = psX[:, 2 * P:4 * P].rearrange("p (m u w) -> p m u w", u=2, w=16)[:, :, u, :]
                    mm(o, mzT[0:KEYS, b, :], v[:, :, u * (VW + 16):u * (VW + 16) + 16])

            def attention(g, nxt):
                for s in range(STEPS):
                    steps = [(w, s - w * LATER) for w in range(2)]
                    c_query = s % 2 == 0 and 10 <= s < 10 + 2 * GROUP
                    if c_query:
                        pe.wait_ge(xcs, at(g, "xcs", (s - 10) // 2 + 1))
                        mm(psS[0][:, 1, 0:P], xb_w[:, 0, :], XT[:, (s - 10) // 2, :]).then_inc(qc_p, 1)
                    if not c_query:
                        unit_scores(g, steps)
                    for w, n in steps:
                        if n % 2 == 1 and 7 <= n < UNITS + 7:
                            output(g, w, (n - 7) // 2)
                    for w, n in steps:
                        if 2 <= n < UNITS + 2:
                            transpose_probs(g, w, (TOK, KEYS)[w], n - 2)
                    for w, n in steps:
                        if 3 <= n < UNITS + 3:
                            values(g, w, (TOK, KEYS)[w], n - 3)
                    if c_query:
                        unit_scores(g, steps)
                    for w, n in steps:
                        if n % 2 == 1 and 5 <= n < UNITS + 5:
                            heads_back(g, w, (n - 5) // 2)
                        if n % 2 == 0 and 6 <= n < UNITS + 6:
                            pe.wait_ge(at_s, at(g, "at_s", w * GROUP + n // 2 - 2))
                            nc.tensor.transpose(psX[:, 0:P], att[:].rearrange("p h c -> p (h c)"),
                                                ident[:]).then_inc(at_p, 1)
                    if s % 2 == 1 and 9 <= s < 9 + 2 * GROUP:
                        pe.wait_ge(pr_s, at(g, "pr_s", s - 2))
                        pe.wait_ge(lb_n, at(g, "lb_n", (s - 9) // 2 + 1))
                        nc.tensor.transpose(psS[0][:, 0, 0:P], xn[0][:, (s - 9) // 2, :],
                                            ident[:]).then_inc(xcp, 1)
                    if nxt is not None:
                        branch_a(nxt, s, g)

            def branch_a(a, s, before):
                if s == 18:
                    pe.wait_ge(c_in, at(a, "c_in", 16))
                    if before is not None:
                        pe.wait_ge(pr_s, at(before, "pr_s", 2 * UNITS - 1))
                    for b in range(GROUP):
                        last = nc.tensor.transpose(psS[0][:, 0, b * P:b * P + KEYS], ctx_in[0:KEYS, b, :],
                                                   ident[0:KEYS, 0:KEYS])
                    last.then_inc(ctp, 1)
                if s == 19:
                    pe.wait_ge(cts, at(a, "cts", 1))
                    if before is not None:
                        pe.wait_ge(pr_s, at(before, "pr_s", 2 * UNITS))
                    mm(four(psS[1][:, 0, :])[:, :, 0:KEYS], xa_w[:, 1, :], CT[:, :, 0:KEYS]).then_inc(ka_p, 1)
                    transpose_x(a, 0, psS[0][:, 1, :])
                    for b in range(GROUP):
                        last = mm(psS[1][0:KEYS, 1, b * P:(b + 1) * P], CT[:, b, 0:KEYS], wvo[:])
                    last.then_inc(va_p, 1)
                if s == 20:
                    pe.wait_ge(xts, at(a, "xts", 1))
                    mm(psS[0][:, 0, :], xa_w[:, 0, :], XT[:].rearrange("p b t -> p (b t)")).then_inc(qa_p, 1)
                if s == 21:
                    pe.wait_ge(qa_s, at(a, "qa_s", 1))
                    pe.wait_ge(ka_s, at(a, "ka_s", 1))
                    for b in range(GROUP):
                        last = mm(psS[1][:, 0, b * P:b * P + KEYS], qa[:, b, :], ka[:, b, 0:KEYS])
                    last.then_inc(sa_p, 1)
                if s == 22:
                    for b in range(GROUP):
                        pe.wait_ge(pa_s, at(a, "pa_s", b + 1))
                        last = nc.tensor.transpose(psS[0][0:KEYS, 1, b * P:(b + 1) * P], pa[:, b, 0:KEYS],
                                                   ident[:])
                    last.then_inc(pta_p, 1)
                if s == 23:
                    pe.wait_ge(pta_s, at(a, "pta_s", 1))
                    pe.wait_ge(va_s, at(a, "va_s", 1))
                    for b in range(GROUP):
                        last = mm(psS[1][:, 1, b * P:(b + 1) * P], pta[0:KEYS, b, :], va[0:KEYS, b, :])
                    last.then_inc(oa_p, 1)

            def unit_scores(g, steps):
                for w, n in steps:
                    if 0 <= n < UNITS:
                        scores(g, w, (TOK, KEYS)[w], n)

            def scores(g, which, nk, n):
                b, half = n // 2, n % 2
                i = which * UNITS + n
                if half == 0:
                    if which == 0:
                        pe.wait_ge(q_s, at(g, "q_s", b + 1))
                        pe.wait_ge(k_s, at(g, "k_s", 4 * b + 4))
                    else:
                        pe.wait_ge(qc_s, at(g, "qc_s", b + 1))
                        pe.wait_ge(kc_s, at(g, "kc_s", 4))
                if i >= 2:
                    pe.wait_ge(pr_s, at(g, "pr_s", i - 1))
                for a in range(2):
                    out = psS[n % 2][:, a, 0:4 * nk]
                    if which == 1:
                        mm(out, identb[:], mbig[:, b, :].rearrange(
                            "p (o k) -> p o k", o=1).broadcast_to([P, 4, nk]), stop=False)
                    last = mm(out, qg[:, b, 2 * half + a, :], km[which][:, b, :, 0:nk], start=which == 0)
                last.then_inc(s_p, 1)

            def transpose_probs(g, which, nk, n):
                i = which * UNITS + n
                pe.wait_ge(pr_s, at(g, "pr_s", i + 1))
                if i == 0:
                    pe.wait_ge(q_s, at(g, "q_s", GROUP))
                    pe.wait_ge(k_s, at(g, "k_s", 4 * GROUP))
                else:
                    pe.wait_ge(pt_s, at(g, "pt_s", i))
                for h in range(HALF):
                    last = nc.tensor.transpose(psT[0:nk, h // 4, (h % 4) * P:(h % 4 + 1) * P],
                                               pr[n % 2][:, h, 0:nk], ident[:])
                last.then_inc(pt_p, 1)

            def values(g, which, nk, m):
                b, half = m // 2, m % 2
                i = which * GROUP + b
                pe.wait_ge(pt_s, at(g, "pt_s", which * UNITS + m + 1))
                if m == 0:
                    if which == 0:
                        pe.wait_ge(v_s, at(g, "v_s", 2))
                    else:
                        pe.wait_ge(vc_s, at(g, "vc_s", 2))
                if i >= 1 and half == 0:
                    pe.wait_ge(oa_s, at(g, "oa_s", i))
                for u in range(2):
                    for j in range(4):
                        hh = 2 * j + u
                        last = mm(psO[32 * j:32 * j + VW, half * P:(half + 1) * P],
                                  vz[which][0:nk, b, half * HALF + hh, :], pt[m % 2][0:nk, hh, :],
                                  start=u == 0, stop=u == 1)
                last.then_inc(pv_p, 1)

            def heads_back(g, which, b):
                i = which * GROUP + b
                pe.wait_ge(oa_s, at(g, "oa_s", i + 1))
                if i == 0:
                    pe.wait_ge(kc_s, at(g, "kc_s", 4))
                else:
                    pe.wait_ge(x_new, at(g, "x_new", i))
                if which == 1:
                    masked_v(b)
                for half in range(2):
                    last = nc.tensor.transpose(psX[:, half * P:(half + 1) * P],
                                               oa[:, half, :], ident[:])
                last.then_inc(to_p, 1)

            def output(g, which, b):
                i = which * GROUP + b
                pe.wait_ge(atT_s, at(g, "atT_s", i + 1))
                wo = ff_wo[:] if which == 0 else xb_w[:, 3, :]
                mm(psX[:, 0:P], attT[:], wo).then_inc(out_p, 1)


            def hidden(g, n):
                if n >= 2:
                    pe.wait_ge(h_s, at(g, "h_s", n - 1))
                mm(psS[n % 2][:, 0, :], mo_w1[:, n // FC, (n % FC) * P:(n % FC + 1) * P],
                   XD[:].rearrange("p b t -> p (b t)")).then_inc(h_p, 1)

            def combine(g, e):
                if e >= 1:
                    pe.wait_ge(hs_s, at(g, "hs_s", e * FC))
                mm(psS[0][:, 1, :], sel[:, e, :], mp[:].rearrange("p b t -> p (b t)")).then_inc(cb_p, 1)

            def experts(g, first, end):
                if g is None:
                    return
                for n in range(first, end):
                    if n + 2 < E1 * FC:
                        hidden(g, n + 2)
                    pe.wait_ge(hs_s, at(g, "hs_s", n + 1))
                    if n % FC == FC - 1 and n // FC + 1 < E1:
                        combine(g, n // FC + 1)
                    for b in range(GROUP):
                        last = mm(psS[1][:, 1, b * P:(b + 1) * P], hsc[n % 2][:, b * P:(b + 1) * P],
                                  mo_w2[:, n // FC, n % FC, :], start=False, stop=n == E1 * FC - 1,
                                  skip_group_check=True)
                    last.then_inc(y_p, 1)

            def front(a, d_):
                if d_ is not None:
                    for b in range(GROUP):
                        pe.wait_ge(lb_n, at(d_, "lb_n", GROUP + b + 1))
                        last = nc.tensor.transpose(psT[:, 0, b * P:(b + 1) * P], xn[2][:, b, :], ident[:])
                    last.then_inc(xdp, 1)
                    pe.wait_ge(xds, at(d_, "xds", 1))
                    for b in range(GROUP):
                        last = mm(psT[:, 1, b * E1:(b + 1) * E1], XD[:, b, :], mo_r[:])
                    last.then_inc(lg_p, 1)
                    if a is not None:
                        pe.wait_ge(xa_new, at(a, "xa_new", GROUP))
                    hidden(d_, 0)
                    hidden(d_, 1)
                if a is not None:
                    transpose_x(a, 1, psO)
                    mm(four(psX)[:, :, 0:KEYS], xb_w[:, 1, :], CT[:, :, 0:KEYS]).then_inc(kc_p, 1)
                    for b in range(GROUP):
                        last = mm(psT[0:KEYS, 0, b * P:(b + 1) * P], CT[:, b, 0:KEYS], xb_w[:, 2, :])
                    last.then_inc(vc_p, 1)
                    pe.wait_ge(pool_s, at(a, "pool_s", 1))
                    mm(psO[:, 0:GROUP], ff_g1[:], pooled[:]).then_inc(g1_p, 1)
                if d_ is not None:
                    pe.wait_ge(cr_s, at(d_, "cr_s", 2))
                    if a is not None:
                        pe.wait_ge(kc_s, at(a, "kc_s", 4))
                    for b in range(GROUP):
                        last = nc.tensor.transpose(psX[:, b * P:(b + 1) * P], mr[:, b, :], ident[:])
                    last.then_inc(cr_p, 1)
                if a is not None:
                    pe.wait_ge(g1r_s, at(a, "g1r_s", 1))
                    if d_ is not None:
                        pe.wait_ge(tk, at(d_, "tk", 10 + 1))
                    for b in range(GROUP):
                        last = mm(psT[:, 1, b * E0:(b + 1) * E0], g1r[:, b, :], ff_g2[:])
                    last.then_inc(lg_p, 1)
                if d_ is not None:
                    pe.wait_ge(cp_s, at(d_, "cp_s", 4))
                    combine(d_, 0)
                    for b in range(GROUP):
                        mm(psS[1][:, 1, b * P:(b + 1) * P], ct32[:, b, :], mo_b2[:], start=b == 0, stop=False,
                           skip_group_check=True)
                experts(d_, 0, LAST - 1)
                if a is not None:
                    pe.wait_ge(mzs, at(a, "mzs", 1))
                    for b in range(GROUP):
                        last = nc.tensor.transpose(psO[0:KEYS, b * P:(b + 1) * P], mz[:, b, :], ident[:])
                    last.then_inc(mtp, 1)
                    pe.wait_ge(vc_s, at(a, "vc_s", 2))
                    for b in range(GROUP):
                        pe.wait_ge(wc_s, at(a, "wc_s", (E0 - 1) * GROUP + b + 1))
                        mq = mm(psT[:, 0, b * P:(b + 1) * P], wc[:, b, 0:P], XT[:, b, :])
                        mk = mm(psT[:, 1, b * P:(b + 1) * P], wc[:, b, P:2 * P], XT[:, b, :])
                    mq.then_inc(q_p, 1)
                    mk.then_inc(k_p, 1)
                    pe.wait_ge(mts, at(a, "mts", 1))
                    for b in range(GROUP):
                        last = mm(psO[:, b * P:(b + 1) * P], XT[:, b, :], wc[:, b, 2 * P:3 * P])
                    last.then_inc(v_p, 1)
                experts(d_, LAST - 1, E1 * FC)
                if d_ is not None and a is not None:
                    pe.wait_ge(y_s, at(d_, "y_s", GROUP))

            for s in range(STEPS):
                branch_a(0, s, None)
            front(0, None)
            with pe.Fori(1, NG) as g:
                attention(g - 1, g)
                front(g, g - 1)
            attention(NG - 1, None)
            front(None, NG - 1)


def lay_out(inputs):
    f = {k: np.asarray(v) for k, v in inputs.items()}
    T = np.ascontiguousarray
    w1, w2 = f["L1_ffn_w1"], f["L1_ffn_w2"]
    E1, HID, _ = w1.shape
    FC = HID // P
    sel = np.zeros((P, HEADS, P), np.float32)
    for h in range(HEADS):
        for p0 in PARTS:
            sel[p0 + h, h, :] = 1.0
    gmask, rmask = np.zeros((P, QUADS), np.float32), np.zeros((P, 4), np.float32)
    for h in range(HEADS):
        gmask[h * DH:(h + 1) * DH, h // 4] = float(DH) ** -0.5
        rmask[h * DH:(h + 1) * DH, h % 4] = 1.0
    tri = np.zeros((P, E1, E1), np.float32)
    for e in range(E1):
        tri[:, e, :e] = 1.0
    bf = mybir.dt.np(BF16)
    eye = np.eye(P, dtype=np.float32)
    a = {
        "x": f["x"], "ctx": f["ctx_1024"], "mask": f["mask_Bx1xSxS2_if1"].reshape(f["x"].shape[0], P, -1),
        "ident": eye, "identb": eye.astype(bf), "sel": sel.astype(bf), "gmask": gmask, "rmask": rmask, "tri": tri,
        "xa_w": T(np.stack([f["L0_xattn_Wq"].T, f["L0_xattn_Wk"].T, f["L0_xattn_Wv"], f["L0_xattn_Wo"].T], 1)),
        "xa_b": T(np.stack([f["L0_xattn_bq"], f["L0_xattn_bv"], f["L0_xattn_bv"]], 1)),
        "bvrep": T(np.broadcast_to(f["L0_xattn_bv"][:, None], (P, P))),
        "brow": T(np.stack([f["L0_xattn_bo"], f["L0_ffn_bo"], f["L1_xattn_bo"]])),
        "ff_w": T(np.concatenate([f["L0_ffn_Wq"], f["L0_ffn_Wk"], f["L0_ffn_Wv"]], 2).transpose(1, 0, 2)),
        "ff_b": T(np.stack([f["L0_ffn_bq"], f["L0_ffn_bk"], f["L0_ffn_bv"]]).transpose(2, 0, 1)),
        "ff_g1": f["L0_ffn_Wg1"], "ff_bg1": T(f["L0_ffn_bg1"][:, None]), "ff_g2": f["L0_ffn_Wg2"],
        "ff_bg2": f["L0_ffn_bg2"], "ff_wo": f["L0_ffn_Wo"],
        "xb_w": T(np.stack([f["L1_xattn_" + w].T for w in ("Wq", "Wk", "Wv", "Wo")], 1)),
        "xb_b": T(np.stack([f["L1_xattn_" + b] for b in ("bq", "bk", "bv")], 1)),
        "mo_r": T(f["L1_ffn_router_w"].T), "mo_w1": T(w1.transpose(2, 0, 1)),
        "mo_b1": T(f["L1_ffn_b1"].reshape(E1, FC, P).transpose(2, 0, 1)),
        "mo_w2": T(w2.reshape(E1, P, FC, P).transpose(3, 0, 2, 1)), "mo_b2": f["L1_ffn_b2"],
    }
    return a


def kernel(**inputs):
    import concourse.bacc as bacc
    from concourse.bass_utils import run_bass_kernel_spmd

    nc = bacc.Bacc("TRN2", target_bir_lowering=False, num_devices=1)
    arrays, d = {}, {}
    for name, a in lay_out(inputs).items():
        arrays[f"in_{name}"] = a
        d[name] = nc.dram_tensor(f"in_{name}", a.shape, mybir.dt.from_np(a.dtype), kind="ExternalInput").ap()
    d["out"] = nc.dram_tensor("out_x", d["x"].shape, F32, kind="ExternalOutput").ap()

    class Shaped:
        def __init__(self, shape):
            self.shape = shape
    E1 = arrays["in_mo_b1"].shape[1]
    d["ffn_bg2"] = Shaped((1, arrays["in_ff_bg2"].shape[0]))
    d["moe_b1"] = Shaped((1, E1, arrays["in_mo_b1"].shape[2]))
    build(nc, d)
    r = run_bass_kernel_spmd(nc, [arrays], core_ids=[0])
    return r.results[0]["out_x"]
```

```python
from contextlib import ExitStack

import numpy as np

import concourse.bass as bass
from concourse import mybir

ALU = mybir.AluOpType
ACT = mybir.ActivationFunctionType
AX_X = mybir.AxisListType.X
F32 = mybir.dt.float32
BF16 = mybir.dt.bfloat16
I32 = mybir.dt.int32

P = 128
GROUP = 4
HEADS = 16
DH = P // HEADS
HALF = HEADS // 2
VW = 32
EPS = 1e-5
BIG = 1e30
MASKED = -60000.0
HUGE = 3e38
UNITS = 2 * GROUP
LATER = UNITS + 2
STEPS = LATER + UNITS + 6
QUADS = HEADS // 4
AHEAD = 4
PARTS = (0, 64, 96)


def build(nc, d):
    B, TOK, C = d["x"].shape
    KEYS = d["ctx"].shape[1]
    E0 = d["ffn_bg2"].shape[1]
    E1, HID = d["moe_b1"].shape[1] , d["moe_b1"].shape[2] * P
    FC = HID // P
    NG = B // GROUP
    ctx = ExitStack()
    per = {}

    def sb(name, shape, dt=F32):
        return ctx.enter_context(nc.sbuf_tensor(name, shape, dt))

    def sem(name, per_group=0):
        s = ctx.enter_context(nc.semaphore(name))
        per[name] = per_group
        return s

    def at(g, name, n):
        return g * per[name] + n

    with ctx:
        ident = sb("ident", [P, P])
        identb = sb("identb", [P, P], BF16)
        sel = sb("sel", [P, HEADS, P], BF16)
        gmask = sb("gmask", [P, QUADS])
        rmask = sb("rmask", [P, 4])
        tri = sb("tri", [P, E1, E1])
        xa_w = sb("xa_w", [P, 4, P])
        xa_b = sb("xa_b", [P, 3])
        bvrep = sb("bvrep", [P, P])
        wvo = sb("wvo", [P, P])
        brow = sb("brow", [P, 3, P])
        bo_a = sb("bo_a", [P, P])
        ff_w = sb("ff_w", [P, E0, 3 * P])
        ff_b = sb("ff_b", [P, 3, E0])
        ff_g1 = sb("ff_g1", [P, P])
        ff_bg1 = sb("ff_bg1", [P, 1])
        ff_g2 = sb("ff_g2", [P, E0])
        ff_bg2 = sb("ff_bg2", [P, E0])
        ff_wo = sb("ff_wo", [P, P])
        xb_w = sb("xb_w", [P, 4, P])
        xb_b = sb("xb_b", [P, 3])
        mo_r = sb("mo_r", [P, E1])
        mo_w1 = sb("mo_w1", [P, E1, HID])
        mo_b1 = sb("mo_b1", [P, E1, FC])
        mo_w2 = sb("mo_w2", [P, E1, FC, P])
        mo_b2 = sb("mo_b2", [P, P])
        powm = sb("powm", [P, GROUP])
        epst = sb("epst", [P, GROUP])
        after_wait = sb("after_wait", [P, 1])

        X = [sb(f"X{i}", [P, GROUP, P]) for i in range(5)]
        XB = [sb(f"XB{i}", [P, GROUP, P]) for i in range(3)]
        ctx_in = sb("ctx_in", [P, GROUP, P])
        msk_in = sb("msk_in", [P, GROUP, KEYS], I32)
        CT = sb("CT", [P, GROUP, P])
        mz = sb("mz", [P, GROUP, KEYS])
        mbig = sb("mbig", [P, GROUP, KEYS], BF16)
        mzT = sb("mzT", [P, GROUP, P])
        anym = sb("anym", [P, GROUP])
        floor0 = sb("floor0", [P, GROUP])
        floor = sb("floor", [P, GROUP])
        bst = [sb(f"bst{i}", [P, GROUP, 6]) for i in range(3)]
        mv = [sb(f"mv{i}", [P, GROUP, 2]) for i in range(3)]
        ve = [sb(f"ve{i}", [P, GROUP]) for i in range(3)]
        rstd = [sb(f"rstd{i}", [P, GROUP]) for i in range(3)]
        xn = [sb(f"xn{i}", [P, GROUP, P]) for i in range(3)]
        XT = sb("XT", [P, GROUP, P])
        XD = sb("XD", [P, GROUP, P])
        qa = sb("qa", [P, GROUP, P])
        ka = sb("ka", [P, GROUP, P])
        va = sb("va", [P, GROUP, P])
        nma = sb("nma", [P, GROUP])
        pa = sb("pa", [P, GROUP, P])
        pta = sb("pta", [P, GROUP, P])
        dena = sb("dena", [P, GROUP])
        rda = sb("rda", [P, GROUP])
        pooled = sb("pooled", [P, GROUP])
        g1 = sb("g1", [P, GROUP])
        g1r = sb("g1r", [P, GROUP, P])
        wc = sb("wc", [P, GROUP, 3 * P])
        bt = sb("bt", [P, GROUP, 3, E0])
        bc = sb("bc", [P, GROUP, 3])
        lg = sb("lg", [P, GROUP, E1])
        gt = sb("gt", [P, GROUP, E1, E1])
        eq = sb("eq", [P, GROUP, E1, E1])
        eqt = sb("eqt", [P, GROUP, E1, E1])
        rk2 = sb("rk2", [P, GROUP, E1, E1])
        rank = sb("rank", [P, GROUP, E1])
        lmx = sb("lmx", [P, GROUP])
        ld = sb("ld", [P, GROUP, E1])
        le = sb("le", [P, GROUP, E1])
        ls = sb("ls", [P, GROUP, E1])
        lsum = sb("lsum", [P, GROUP])
        lrec = sb("lrec", [P, GROUP])
        wgt = sb("wgt", [P, GROUP, E1])
        qg = sb("qg", [P, GROUP, QUADS, P])
        km = [sb(f"km{i}", [P, GROUP, 4, P]) for i in range(2)]
        vz = [sb(f"vz{i}", [P, GROUP, HEADS, VW]) for i in range(2)]
        kb_c = sb("kb_c", [P, 4])
        kb_b = sb("kb_b", [P, GROUP, 4])
        nm = sb("nm", [P, GROUP, HEADS])
        mr = sb("mr", [P, GROUP, P])
        mp = sb("mp", [P, GROUP, P], BF16)
        wb = sb("wb", [P, GROUP, E1], BF16)
        wres = sb("wres", [P, GROUP, E1])
        sd = [sb(f"sd{i}", [P, 4, P]) for i in range(2)]
        pr = [sb(f"pr{i}", [P, HALF, P]) for i in range(2)]
        pt = [sb(f"pt{i}", [P, HALF, P]) for i in range(2)]
        oa = sb("oa", [P, 2, P])
        ew0 = sb("ew0", [P, GROUP, HEADS])
        ew = sb("ew", [P, GROUP, HEADS])
        mvt = sb("mvt", [P, HEADS, 16])
        osum = sb("osum", [P, HEADS, 16])
        orec = sb("orec", [P, HEADS])
        att = sb("att", [P, HEADS, DH])
        attT = sb("attT", [P, P])
        ct32 = sb("ct32", [P, GROUP, P])
        hid = [sb(f"hid{i}", [P, GROUP * P]) for i in range(AHEAD)]
        hsc = [sb(f"hsc{i}", [P, GROUP * P]) for i in range(2)]

        psS = [ctx.enter_context(nc.psum_tensor(f"psS{i}", [P, 2, 512], F32)) for i in range(2)]
        psT = ctx.enter_context(nc.psum_tensor("psT", [P, 2, 512], F32))
        psO = ctx.enter_context(nc.psum_tensor("psO", [P, 512], F32))
        psX = ctx.enter_context(nc.psum_tensor("psX", [P, 512], F32))

        def four(t):
            return t[:, :].rearrange("p (b c) -> p b c", b=GROUP)

        def finishing(w, n, later):
            for b in range(GROUP):
                if n - later == (2 * b + 5 if (w, b) != (1, GROUP - 1) else 2 * b + 4):
                    return b

        def head_bank(w, b):
            return psX if (w, b) != (1, GROUP - 1) else psT[:, 1, :]

        consts = sem("consts")
        fills = sem("fills")
        fold_p = sem("fold_p")
        fold_s = sem("fold_s")
        x_in = sem("x_in", 16)
        c_in = sem("c_in", 16)
        m_in = sem("m_in", 16)
        x_out = sem("x_out", 16)
        ctp = sem("ctp", 1)
        cts = sem("cts", 1)
        mzs = sem("mzs", 5)
        mtp = sem("mtp", 1)
        mts = sem("mts", 1)
        ln_s = sem("ln_s", 4)
        lb_s = sem("lb_s", 4 * GROUP)
        ln_v = sem("ln_v", 2)
        lb_v = sem("lb_v", 2 * GROUP)
        ln_r = sem("ln_r", 2)
        lb_r = sem("lb_r", 2 * GROUP)
        ln_n = sem("ln_n", 2 * GROUP)
        lb_n = sem("lb_n", 2 * GROUP)
        xtp = sem("xtp", 2)
        xts = sem("xts", 2)
        xdp = sem("xdp", 2)
        xds = sem("xds", 2)
        xcp = sem("xcp", GROUP)
        xcs = sem("xcs", GROUP)
        xbs = sem("xbs", 3)
        qa_p = sem("qa_p", 1)
        qa_s = sem("qa_s", 1)
        ka_p = sem("ka_p", 1)
        ka_s = sem("ka_s", 1)
        va_p = sem("va_p", 1)
        va_s = sem("va_s", 1)
        sa_p = sem("sa_p", 1)
        nma_s = sem("nma_s", 1)
        pa_s = sem("pa_s", GROUP)
        pta_p = sem("pta_p", 1)
        pta_s = sem("pta_s", 1)
        oa_p = sem("oa_p", 1)
        rda_s = sem("rda_s", 1)
        xa_new = sem("xa_new", GROUP)
        x_new = sem("x_new", 2 * GROUP)
        pool_s = sem("pool_s", 1)
        g1_p = sem("g1_p", 1)
        g1_s = sem("g1_s", 1)
        g1r_s = sem("g1r_s", 1)
        lg_p = sem("lg_p", 2)
        tk = sem("tk", 2 * 10)
        le_s = sem("le_s", 2)
        wc_s = sem("wc_s", GROUP * E0)
        bc_s = sem("bc_s", 3)
        q_p = sem("q_p", 1)
        k_p = sem("k_p", 1)
        v_p = sem("v_p", 1)
        q_s = sem("q_s", GROUP)
        k_s = sem("k_s", GROUP * 4)
        v_s = sem("v_s", 2)
        qc_p = sem("qc_p", GROUP)
        kc_p = sem("kc_p", 1)
        vc_p = sem("vc_p", 1)
        qc_s = sem("qc_s", GROUP)
        kc_s = sem("kc_s", 4)
        vc_s = sem("vc_s", 2)
        s_p = sem("s_p", 2 * UNITS)
        nm_s = sem("nm_s", 2 * UNITS)
        nf_s = sem("nf_s", UNITS)
        sd_s = sem("sd_s", 2 * UNITS)
        pt_p = sem("pt_p", 2 * UNITS)
        pt_s = sem("pt_s", 2 * UNITS)
        pr_s = sem("pr_s", 2 * UNITS)
        pv_p = sem("pv_p", 2 * UNITS)
        oa_s = sem("oa_s", 2 * GROUP)
        ew_v = sem("ew_v", GROUP)
        ew_s = sem("ew_s", GROUP)
        to_p = sem("to_p", 2 * GROUP)
        os_s = sem("os_s", 2 * GROUP)
        or_s = sem("or_s", 2 * GROUP)
        at_s = sem("at_s", 2 * GROUP)
        at_p = sem("at_p", 2 * GROUP)
        atT_s = sem("atT_s", 2 * GROUP)
        out_p = sem("out_p", 2 * GROUP)
        cr_s = sem("cr_s", 6)
        cr_p = sem("cr_p", 1)
        c32_s = sem("c32_s", 1)
        cp_s = sem("cp_s", 1)
        h_p = sem("h_p", E1 * FC)
        cb_p = sem("cb_p", E1)
        h_s = sem("h_s", E1 * FC)
        hs_s = sem("hs_s", E1 * FC)
        y_p = sem("y_p", E1 * FC)
        y_s = sem("y_s", GROUP)

        block = ctx.enter_context(nc.Block())

        LOADS = [(ident, "ident"), (identb, "identb"), (sel, "sel"), (gmask, "gmask"), (rmask, "rmask"), (tri, "tri"),
                 (xa_w, "xa_w"), (xa_b, "xa_b"), (bvrep, "bvrep"), (brow, "brow"), (ff_w, "ff_w"),
                 (ff_b, "ff_b"), (ff_g1, "ff_g1"), (ff_bg1, "ff_bg1"), (ff_g2, "ff_g2"),
                 (ff_bg2, "ff_bg2"), (ff_wo, "ff_wo"), (xb_w, "xb_w"), (xb_b, "xb_b"), (mo_r, "mo_r"),
                 (mo_w1, "mo_w1"), (mo_b1, "mo_b1"), (mo_w2, "mo_w2")]
        ALL_CONSTS = 16 * (len(LOADS) + len(PARTS))
        FILLS = 7
        MIXED = (7, 8, 10, 11, 12)
        LAST = E1 * FC - 2

        @block.sync
        def _(sp):
            for tile, name in LOADS:
                src = d[name]
                if name in ("ff_bg2", "brow"):
                    sp.dma_start(tile[:], src.partition_broadcast(P)).then_inc(consts, 16)
                else:
                    sp.dma_start(tile[:], src).then_inc(consts, 16)
            sp.wait_ge(fills, FILLS)
            for p0 in PARTS:
                sp.dma_start(mo_b2[p0:p0 + E1, :], d["mo_b2"]).then_inc(consts, 16)

            def rows(name, first):
                return d[name][bass.ds(first, GROUP), :, :].rearrange("b t c -> t b c")

            sp.sem_inc(x_out, 16)
            sp.dma_start(X[0][:], rows("x", 0)).then_inc(x_in, 16)
            sp.dma_start(ctx_in[0:KEYS, :, :], rows("ctx", 0)).then_inc(c_in, 16)
            sp.dma_start(msk_in[:], rows("mask", 0)).then_inc(m_in, 16)
            with sp.Fori(1, NG) as g:
                sp.wait_ge(ctp, at(g - 1, "ctp", 1))
                sp.dma_start(ctx_in[0:KEYS, :, :], rows("ctx", g * GROUP)).then_inc(c_in, 16)
                sp.wait_ge(mzs, at(g - 1, "mzs", 1))
                sp.dma_start(msk_in[:], rows("mask", g * GROUP)).then_inc(m_in, 16)
                sp.wait_ge(xa_new, at(g - 1, "xa_new", GROUP))
                sp.dma_start(X[0][:], rows("x", g * GROUP)).then_inc(x_in, 16)
                sp.wait_ge(y_s, at(g - 1, "y_s", GROUP))
                sp.dma_start(rows("out", g * GROUP - GROUP), X[4][:]).then_inc(x_out, 16)
            sp.wait_ge(y_s, at(NG - 1, "y_s", GROUP))
            sp.dma_start(rows("out", (NG - 1) * GROUP), X[4][:]).then_inc(x_out, 16)
            sp.wait_ge(x_out, 16 + 16 * NG)

        @block.gpsimd
        def _(gp):
            nc.gpsimd.memset(mo_b2[:], 0.0).then_inc(fills, 1)
            for v in vz:
                nc.gpsimd.memset(v[:], 0.0).then_inc(fills, 1)
            nc.gpsimd.memset(mr[:], 0.0).then_inc(fills, 1)
            nc.gpsimd.memset(powm[:], -0.5).then_inc(fills, 1)
            nc.gpsimd.memset(epst[:], EPS).then_inc(fills, 1)
            gp.wait_ge(fills, 6)
            for v in vz:
                pair = v[:].rearrange("p b (m u) w -> p (b m) u w", u=2)
                nc.gpsimd.memset(pair[:, :, 0, DH:DH + 1], 1.0)
                last = nc.gpsimd.memset(pair[:, :, 1, 16 + DH:16 + DH + 1], 1.0)
            last.then_inc(fills, 1)
            gp.wait_ge(consts, ALL_CONSTS)

            def rstd_of(g, layer):
                gp.wait_ge(ln_s, at(g, "ln_s", 2 * layer + 2))
                nc.gpsimd.tensor_tensor(ve[layer][:], mv[layer][:, :, 1], epst[:], ALU.add).then_inc(ln_v, 1)
                gp.wait_ge(ln_v, at(g, "ln_v", layer + 1))
                nc.gpsimd.tensor_tensor(rstd[layer][:], ve[layer][:], powm[:], ALU.pow).then_inc(ln_r, 1)

            def rstd_batch(g, w, b):
                i = w * GROUP + b
                k = 2 * w
                one = slice(b, b + 1)
                gp.wait_ge(lb_s, at(g, "lb_s", 2 * i + 2))
                nc.gpsimd.tensor_tensor(ve[k][:, one], mv[k][:, one, 1], epst[:, one], ALU.add).then_inc(lb_v, 1)
                gp.wait_ge(lb_v, at(g, "lb_v", i + 1))
                nc.gpsimd.tensor_tensor(rstd[k][:, one], ve[k][:, one], powm[:, one], ALU.pow).then_inc(lb_r, 1)

            def add_bias(g, i):
                bias = bo_a[:] if i == 0 else brow[:, i, :]
                nc.gpsimd.tensor_tensor(XB[i][:], X[i][:],
                                        bias.rearrange("p (o c) -> p o c", o=1).broadcast_to([P, GROUP, P]),
                                        ALU.add).then_inc(xbs, 1)

            def attention(g, nxt):
                for b in range(GROUP):
                    rstd_batch(g, 0, b)
                add_bias(g, 2)
                if nxt is not None:
                    branch_a_inputs(nxt)
                for b in range(GROUP):
                    rstd_batch(g, 1, b)
                if nxt is not None:
                    branch_b_inputs(nxt)

            def branch_a_inputs(g):
                rstd_of(g, 0)
                gp.wait_ge(x_in, at(g, "x_in", 16))
                add_bias(g, 0)

            def branch_b_inputs(g):
                rstd_of(g, 1)
                add_bias(g, 1)

            gp.wait_ge(fold_s, 2)
            branch_a_inputs(0)
            branch_b_inputs(0)
            with gp.Fori(0, NG - 1) as g:
                attention(g, g + 1)
            attention(NG - 1, None)

        @block.scalar
        def _(act):
            act.wait_ge(consts, ALL_CONSTS)
            act.wait_ge(fills, FILLS)
            act.wait_ge(fold_p, 2)
            nc.scalar.activation(wvo[:], psX[:, 0:P], ACT.Copy).then_inc(fold_s, 1)

            def top_exp(g, which, n):
                act.wait_ge(tk, at(g, "tk", 10 * which + 3))
                nc.scalar.activation(le[:, :, 0:n], ld[:, :, 0:n], ACT.Exp).then_inc(le_s, 1)

            def hidden(g, first, end):
                if g is None:
                    return
                for n in range(first, end):
                    act.wait_ge(h_p, at(g, "h_p", n + 1))
                    if n >= AHEAD:
                        act.wait_ge(hs_s, at(g, "hs_s", n - AHEAD + 1))
                    nc.scalar.activation(hid[n % AHEAD][:], psS[n % 2][:, 0, :], ACT.Gelu,
                                         bias=mo_b1[:, n // FC, n % FC:n % FC + 1]).then_inc(h_s, 1)

            def v_copy(w, src, nk, done):
                src = src[0:nk, :].rearrange("p (n u r) -> p n u r", u=2, r=DH)
                dst = vz[w][0:nk].rearrange("p b (m u) w -> p (b m) u w", u=2)
                for u in range(2):
                    nc.scalar.activation(dst[:, :, u, 16 * u:16 * u + DH], src[:, :, u, :],
                                         ACT.Copy).then_inc(done, 1)

            def k_copy_c(g, first, end):
                for r in range(first, end):
                    nc.scalar.activation(km[1][:, :, r, 0:KEYS], four(psX)[:, :, 0:KEYS], ACT.Identity,
                                         bias=kb_c[:, r:r + 1], scale=rmask[:, r:r + 1]).then_inc(kc_s, 1)

            def attention(g, nxt):
                for s in range(STEPS):
                    if nxt is not None and s == 9:
                        branch_a(nxt, s)
                    for w in range(2):
                        n = s - w * LATER
                        nk = (TOK, KEYS)[w]
                        i = w * UNITS + n
                        if 2 <= n < UNITS + 2:
                            act.wait_ge(pt_p, at(g, "pt_p", i - 1))
                            if i >= 4:
                                act.wait_ge(pv_p, at(g, "pv_p", i - 3))
                            nc.scalar.activation(pt[n % 2][0:nk], psT[0:nk].rearrange(
                                "p a (h t) -> p (a h) t", t=P), ACT.Copy).then_inc(pt_s, 1)
                        if n % 2 == 0 and 4 <= n < UNITS + 4:
                            act.wait_ge(pv_p, at(g, "pv_p", i - 2))
                            nc.scalar.activation(oa[:], psO[:, 0:2 * P].rearrange(
                                "p (a t) -> p a t", a=2), ACT.Copy).then_inc(oa_s, 1)
                    for w in range(2):
                        n = s - w * LATER
                        b = finishing(w, n, 1)
                        if w == 0 and b is not None:
                            transposed_out(g, w, b)
                    if nxt is not None and s == 8:
                        branch_a(nxt, s)
                    if s % 2 == 0 and 8 <= s < 8 + 2 * GROUP:
                        b = (s - 8) // 2
                        act.wait_ge(xcp, at(g, "xcp", b + 1))
                        nc.scalar.activation(XT[:, b, :], psO[:, 2 * P:3 * P], ACT.Copy).then_inc(xcs, 1)
                    for w in range(2):
                        n = s - w * LATER
                        if 0 <= n < UNITS:
                            probabilities(g, w, n)
                        b = finishing(w, n, 1)
                        if w == 1 and b is not None:
                            transposed_out(g, w, b)
                    if nxt is not None and s > LATER:
                        branch_a(nxt, s)
                act.wait_ge(xdp, at(g, "xdp", 1))
                nc.scalar.activation(XD[:, 0:GROUP - 1, :], four(psT[:, 0, :])[:, 0:GROUP - 1],
                                     ACT.Copy).then_inc(xds, 1)

            def branch_a(a, s):
                if s == 8:
                    act.wait_ge(ctp, at(a, "ctp", 1))
                    nc.scalar.activation(CT[:, :, 0:KEYS], four(psS[0][:, 0, :])[:, :, 0:KEYS],
                                         ACT.Copy).then_inc(cts, 1)
                if s == 9:
                    act.wait_ge(ka_p, at(a, "ka_p", 1))
                    nc.scalar.activation(ka[:, :, 0:KEYS], four(psS[1][:, 0, :])[:, :, 0:KEYS],
                                         ACT.Copy).then_inc(ka_s, 1)
                    act.wait_ge(va_p, at(a, "va_p", 1))
                    nc.scalar.activation(va[0:KEYS], four(psS[1][:, 1, :])[0:KEYS], ACT.Copy).then_inc(va_s, 1)
                if s == 18:
                    act.wait_ge(xtp, at(a, "xtp", 1))
                    nc.scalar.activation(XT[:], four(psS[0][:, 1, :]), ACT.Copy).then_inc(xts, 1)
                if s == 20:
                    act.wait_ge(nma_s, at(a, "nma_s", 1))
                    for b in range(GROUP):
                        nc.scalar.activation(pa[:, b, 0:KEYS], psS[1][:, 0, b * P:b * P + KEYS], ACT.Exp,
                                             bias=nma[:, b:b + 1], accum_out=dena[:, b:b + 1]).then_inc(pa_s, 1)
                if s == 21:
                    act.wait_ge(pta_p, at(a, "pta_p", 1))
                    nc.scalar.activation(pta[0:KEYS], four(psS[0][:, 1, :])[0:KEYS], ACT.Copy).then_inc(pta_s, 1)

            def probabilities(g, w, n):
                i = w * UNITS + n
                nk = (TOK, KEYS)[w]
                if w == 0:
                    act.wait_ge(nm_s, at(g, "nm_s", i + 1))
                else:
                    act.wait_ge(nf_s, at(g, "nf_s", n + 1))
                if i >= 2:
                    act.wait_ge(pt_p, at(g, "pt_p", i - 1))
                for r in range(4):
                    h = n % 2 * HALF + 4 + r
                    nc.scalar.activation(pr[n % 2][:, 4 + r, 0:nk], psS[n % 2][:, 1, r * nk:(r + 1) * nk],
                                         ACT.Exp, bias=nm[:, n // 2, h:h + 1])
                act.wait_ge(sd_s, at(g, "sd_s", i + 1))
                nc.scalar.activation(pr[n % 2][:, 0:4, 0:nk], sd[n % 2][:, :, 0:nk], ACT.Exp).then_inc(pr_s, 1)
                if w == 1 and n % 2 == 1:
                    b = n // 2
                    act.wait_ge(ew_v, at(g, "ew_v", b + 1))
                    nc.scalar.activation(ew[:, b, :], ew0[:, b, :], ACT.Exp).then_inc(ew_s, 1)

            def transposed_out(g, w, b):
                bias = bc[:, b, 2:3] if w == 0 else xb_b[:, 2:3]
                act.wait_ge(at_p, at(g, "at_p", w * GROUP + b + 1))
                nc.scalar.activation(attT[:], head_bank(w, b)[:, 0:P], ACT.Identity, bias=bias).then_inc(atT_s, 1)

            def front(a, d_):
                if d_ is not None:
                    act.wait_ge(xdp, at(d_, "xdp", 2))
                    nc.scalar.activation(XD[:, GROUP - 1, :], psT[:, 0, (GROUP - 1) * P:], ACT.Copy).then_inc(xds, 1)
                    top_exp(d_, 1, E1)
                hidden(d_, 0, 4)
                if a is not None:
                    act.wait_ge(xtp, at(a, "xtp", 2))
                    nc.scalar.activation(XT[:], four(psO), ACT.Copy).then_inc(xts, 1)
                if d_ is not None:
                    act.wait_ge(cp_s, at(d_, "cp_s", 1))
                    nc.scalar.activation(ct32[:], four(psX), ACT.Copy).then_inc(c32_s, 1)
                hidden(d_, 4, 6)
                if a is None:
                    return hidden(d_, 6, E1 * FC)
                act.wait_ge(g1_p, at(a, "g1_p", 1))
                nc.scalar.activation(g1[:], psO[:, 0:GROUP], ACT.Relu, bias=ff_bg1[:, 0:1],
                                     scale=1.0 / TOK).then_inc(g1_s, 1)
                hidden(d_, 6, 8)
                top_exp(a, 0, E0)
                hidden(d_, 8, 9)
                act.wait_ge(kc_p, at(a, "kc_p", 1))
                k_copy_c(a, 0, 1)
                for r in range(1, 4):
                    hidden(d_, 8 + r, 9 + r)
                    k_copy_c(a, r, r + 1)
                hidden(d_, 12, 13)
                act.wait_ge(vc_p, at(a, "vc_p", 1))
                v_copy(1, psT[:, 0, :], KEYS, vc_s)
                hidden(d_, 13, E1 * FC)
                act.wait_ge(bc_s, at(a, "bc_s", 3))
                act.wait_ge(k_p, at(a, "k_p", 1))
                for b in range(GROUP):
                    for r in range(4):
                        nc.scalar.activation(km[0][:, b, r, :], psT[:, 1, b * P:(b + 1) * P], ACT.Identity,
                                             bias=kb_b[:, b, r:r + 1], scale=rmask[:, r:r + 1]).then_inc(k_s, 1)
                act.wait_ge(v_p, at(a, "v_p", 1))
                v_copy(0, psO, TOK, v_s)

            act.wait_ge(fold_s, 3)
            for s in range(STEPS):
                branch_a(0, s)
            front(0, None)
            with act.Fori(1, NG) as g:
                attention(g - 1, g)
                front(g, g - 1)
            attention(NG - 1, None)
            front(None, NG - 1)

        @block.vector
        def _(ve_):
            dve = ve_
            dve.wait_ge(consts, ALL_CONSTS)
            dve.wait_ge(fills, FILLS)
            dve.wait_ge(fold_s, 1)
            nc.vector.tensor_tensor(bo_a[:], psX[:, P:2 * P], brow[:, 0, :], ALU.add).then_inc(fold_s, 1)
            nc.vector.tensor_tensor(kb_c[:], rmask[:], xb_b[:, 1:2].broadcast_to([P, 4]),
                                    ALU.mult).then_inc(fold_s, 1)

            def statistics(g, layer):
                if layer == 0:
                    dve.wait_ge(x_in, at(g, "x_in", 16))
                else:
                    dve.wait_ge(xa_new, at(g, "xa_new", GROUP))
                for b in range(GROUP):
                    last = nc.vector.bn_stats(bst[layer][:, b, :], X[layer][:, b, :])
                last.then_inc(ln_s, 1)
                dve.wait_ge(ln_s, at(g, "ln_s", 2 * layer + 1))
                nc.vector.memset(after_wait[:], 0.0)
                for b in range(GROUP):
                    last = nc.vector.bn_aggr(mv[layer][:, b, :], bst[layer][:, b, :])
                last.then_inc(ln_s, 1)

            def normalise(g, layer):
                dve.wait_ge(ln_s, at(g, "ln_s", 2 * layer + 2))
                dve.wait_ge(ln_r, at(g, "ln_r", layer + 1))
                for b in range(GROUP):
                    nc.vector.tensor_scalar(xn[layer][:, b, :], X[layer][:, b, :], mv[layer][:, b, 0:1],
                                            rstd[layer][:, b:b + 1], ALU.subtract, ALU.mult).then_inc(ln_n, 1)

            def statistics_batch(g, w, b):
                i = w * GROUP + b
                k = 2 * w
                dve.wait_ge(x_new, at(g, "x_new", i + 1))
                nc.vector.bn_stats(bst[k][:, b, :], X[w + 2][:, b, :]).then_inc(lb_s, 1)
                dve.wait_ge(lb_s, at(g, "lb_s", 2 * i + 1))
                nc.vector.memset(after_wait[:], 0.0)
                nc.vector.bn_aggr(mv[k][:, b, :], bst[k][:, b, :]).then_inc(lb_s, 1)

            def normalise_batch(g, w, b):
                i = w * GROUP + b
                k = 2 * w
                dve.wait_ge(lb_r, at(g, "lb_r", i + 1))
                nc.vector.tensor_scalar(xn[k][:, b, :], X[w + 2][:, b, :], mv[k][:, b, 0:1],
                                        rstd[k][:, b:b + 1], ALU.subtract, ALU.mult).then_inc(lb_n, 1)

            def top2_ranks(g, which, n):
                base = 10 * which
                dve.wait_ge(lg_p, at(g, "lg_p", which + 1))
                src = psT[:, 1, 0:GROUP * n].rearrange("p (b e) -> p b e", b=GROUP)
                L = lg[:, :, 0:n]
                if which == 0:
                    nc.vector.tensor_tensor(
                        L, src, ff_bg2[:].rearrange("p (o e) -> p o e", o=1).broadcast_to([P, GROUP, n]),
                        ALU.add).then_inc(tk, 1)
                else:
                    nc.vector.tensor_copy(L, src).then_inc(tk, 1)
                dve.wait_ge(tk, at(g, "tk", base + 1))
                other = L.rearrange("p b (o e) -> p b o e", o=1).broadcast_to([P, GROUP, n, n])
                own = L.rearrange("p b (e o) -> p b e o", o=1).broadcast_to([P, GROUP, n, n])
                T = tri[:, 0:n, 0:n].rearrange("p (o e) f -> p o e f", o=1).broadcast_to([P, GROUP, n, n])
                nc.vector.tensor_reduce(lmx[:], L, AX_X, ALU.max)
                nc.vector.tensor_tensor(gt[:, :, 0:n, 0:n], other, own, ALU.is_gt)
                nc.vector.tensor_tensor(eq[:, :, 0:n, 0:n], other, own, ALU.is_equal).then_inc(tk, 1)
                dve.wait_ge(tk, at(g, "tk", base + 2))
                nc.vector.tensor_tensor(ld[:, :, 0:n], L, lmx[:].rearrange(
                    "p (b o) -> p b o", o=1).broadcast_to([P, GROUP, n]), ALU.subtract).then_inc(tk, 1)
                nc.vector.tensor_tensor(eqt[:, :, 0:n, 0:n], eq[:, :, 0:n, 0:n], T, ALU.mult).then_inc(tk, 1)
                dve.wait_ge(tk, at(g, "tk", base + 4))
                nc.vector.tensor_tensor(rk2[:, :, 0:n, 0:n], gt[:, :, 0:n, 0:n], eqt[:, :, 0:n, 0:n],
                                        ALU.add).then_inc(tk, 1)
                dve.wait_ge(tk, at(g, "tk", base + 5))
                nc.vector.tensor_reduce(rank[:, :, 0:n], rk2[:, :, 0:n, 0:n], AX_X, ALU.add).then_inc(tk, 1)

            def top2_weights(g, which, n):
                base = 10 * which
                dve.wait_ge(tk, at(g, "tk", base + 6))
                dve.wait_ge(le_s, at(g, "le_s", which + 1))
                nc.vector.scalar_tensor_tensor(out=ls[:, :, 0:n], in0=rank[:, :, 0:n], scalar=1.5,
                                               in1=le[:, :, 0:n], op0=ALU.is_lt, op1=ALU.mult).then_inc(tk, 1)
                dve.wait_ge(tk, at(g, "tk", base + 7))
                nc.vector.tensor_reduce(lsum[:], ls[:, :, 0:n], AX_X, ALU.add).then_inc(tk, 1)
                dve.wait_ge(tk, at(g, "tk", base + 8))
                nc.vector.reciprocal(lrec[:], lsum[:]).then_inc(tk, 1)
                dve.wait_ge(tk, at(g, "tk", base + 9))
                nc.vector.tensor_tensor(wgt[:, :, 0:n], ls[:, :, 0:n], lrec[:].rearrange(
                    "p (b o) -> p b o", o=1).broadcast_to([P, GROUP, n]), ALU.mult).then_inc(tk, 1)
                dve.wait_ge(tk, at(g, "tk", base + 10))

            def weight_parts(g):
                part = [mr[:, :, p0:p0 + E1] for p0 in PARTS]
                nc.vector.tensor_copy(wb[:], wgt[:]).then_inc(cr_s, 1)
                dve.wait_ge(cr_s, at(g, "cr_s", 1))
                nc.vector.tensor_copy(part[0], wb[:]).then_inc(cr_s, 1)
                nc.vector.tensor_tensor(wres[:], wgt[:], wb[:], ALU.subtract).then_inc(cr_s, 1)
                dve.wait_ge(cr_s, at(g, "cr_s", 3))
                nc.vector.tensor_copy(wb[:], wres[:]).then_inc(cr_s, 1)
                dve.wait_ge(cr_s, at(g, "cr_s", 4))
                nc.vector.tensor_copy(part[1], wb[:]).then_inc(cr_s, 1)
                nc.vector.tensor_tensor(part[2], wres[:], wb[:], ALU.subtract).then_inc(cr_s, 1)

            def attention(g, nxt):
                for s in range(STEPS):
                    for w in range(2):
                        n = s - w * LATER
                        b = finishing(w, n, 3)
                        if b is not None:
                            normalise_batch(g, w, b)
                    if s % 2 == 1 and 9 <= s < 9 + 2 * GROUP:
                        b = (s - 9) // 2
                        dve.wait_ge(qc_p, at(g, "qc_p", b + 1))
                        group_heads(b, psO[:, 3 * P:4 * P], xb_b[:, 0:1], qc_s)
                    for w in range(2):
                        n = s - w * LATER
                        b = finishing(w, n, 2)
                        if b is not None:
                            head_add(g, w, b)
                            statistics_batch(g, w, b)
                    for w in range(2):
                        if 0 <= s - w * LATER < UNITS:
                            less_maximum(g, w, s - w * LATER)
                    for w in range(2):
                        n = s - w * LATER
                        b = finishing(w, n, 0)
                        if b is not None:
                            head_out(g, w, b)
                    if nxt is not None:
                        branch_a(nxt, s)

            def branch_a(a, s):
                if s == 16:
                    statistics(a, 0)
                if s == 17:
                    normalise(a, 0)
                if s == 19:
                    dve.wait_ge(qa_p, at(a, "qa_p", 1))
                    nc.vector.tensor_scalar(qa[:], four(psS[0][:, 0, :]), xa_b[:, 0:1], float(P) ** -0.5,
                                            ALU.add, ALU.mult).then_inc(qa_s, 1)
                if s == 20:
                    dve.wait_ge(sa_p, at(a, "sa_p", 1))
                    nc.vector.tensor_reduce(nma[:], four(psS[1][:, 0, :])[:, :, 0:KEYS], AX_X, ALU.max,
                                            negate=True).then_inc(nma_s, 1)
                if s == 23:
                    dve.wait_ge(pa_s, at(a, "pa_s", GROUP))
                    nc.vector.reciprocal(rda[:], dena[:]).then_inc(rda_s, 1)
                    dve.wait_ge(rda_s, at(a, "rda_s", 1))
                    dve.wait_ge(oa_p, at(a, "oa_p", 1))
                    dve.wait_ge(xbs, at(a, "xbs", 1))
                    for b in range(GROUP):
                        nc.vector.scalar_tensor_tensor(
                            out=X[1][:, b, :], in0=psS[1][:, 1, b * P:(b + 1) * P], scalar=rda[:, b:b + 1],
                            in1=XB[0][:, b, :], op0=ALU.mult, op1=ALU.add).then_inc(xa_new, 1)

            def group_heads(b, src, bias, done):
                nc.vector.scalar_tensor_tensor(
                    out=qg[:, b], in0=src.rearrange("p (o t) -> p o t", o=1).broadcast_to([P, QUADS, P]),
                    scalar=bias, in1=gmask[:].rearrange("p (j o) -> p j o", o=1).broadcast_to([P, QUADS, P]),
                    op0=ALU.add, op1=ALU.mult).then_inc(done, 1)

            def less_maximum(g, w, n):
                b, half = n // 2, n % 2
                i = w * UNITS + n
                nk = (TOK, KEYS)[w]
                dve.wait_ge(s_p, at(g, "s_p", i + 1))
                src = psS[n % 2][:, :, 0:4 * nk].rearrange("p a (h t) -> p a h t", h=4)
                m = nm[:, b, half * HALF:(half + 1) * HALF]
                nc.vector.tensor_reduce(m.rearrange("p (a h) -> p a h", a=2), src, AX_X, ALU.max,
                                        negate=True).then_inc(nm_s, 1)
                dve.wait_ge(nm_s, at(g, "nm_s", i + 1))
                if w == 1:
                    nc.vector.tensor_scalar(m, m, floor[:, b:b + 1], None, ALU.min).then_inc(nf_s, 1)
                    dve.wait_ge(nf_s, at(g, "nf_s", n + 1))
                if i >= 2:
                    dve.wait_ge(pr_s, at(g, "pr_s", i - 1))
                nc.vector.tensor_tensor(
                    sd[n % 2][:, :, 0:nk], src[:, 0],
                    m[:, 0:4].rearrange("p (h o) -> p h o", o=1).broadcast_to([P, 4, nk]),
                    ALU.add).then_inc(sd_s, 1)
                if w == 1 and half == 1:
                    nc.vector.tensor_scalar(ew0[:, b, :], nm[:, b, :], MASKED, None, ALU.add).then_inc(ew_v, 1)

            def head_out(g, which, b):
                bank = head_bank(which, b)
                i = which * GROUP + b
                dve.wait_ge(to_p, at(g, "to_p", i + 1))
                O = bank[:, 0:2 * P].rearrange("p (h w) -> p h w", w=16)
                if which == 1:
                    dve.wait_ge(ew_s, at(g, "ew_s", b + 1))
                    M = bank[:, 2 * P:4 * P].rearrange("p (h w) -> p h w", w=16)
                    nc.vector.tensor_tensor(mvt[:], M, ew[:, b, :].rearrange(
                        "p (h o) -> p h o", o=1).broadcast_to([P, HEADS, 16]), ALU.mult).then_inc(os_s, 1)
                    dve.wait_ge(os_s, at(g, "os_s", 2 * b + 1))
                    nc.vector.tensor_tensor(osum[:], O, mvt[:], ALU.add).then_inc(os_s, 1)
                    dve.wait_ge(os_s, at(g, "os_s", 2 * b + 2))
                    O = osum[:]
                nc.vector.reciprocal(orec[:], O[:, :, DH]).then_inc(or_s, 1)
                dve.wait_ge(or_s, at(g, "or_s", i + 1))
                if i >= 1:
                    dve.wait_ge(at_p, at(g, "at_p", i))
                nc.vector.tensor_tensor(att[:], O[:, :, 0:DH], orec[:].rearrange(
                    "p (h o) -> p h o", o=1).broadcast_to([P, HEADS, DH]), ALU.mult).then_inc(at_s, 1)

            def head_add(g, which, b):
                i = which * GROUP + b
                dve.wait_ge(out_p, at(g, "out_p", i + 1))
                dve.wait_ge(xbs, at(g, "xbs", which + 2))
                nc.vector.tensor_tensor(X[which + 2][:, b, :], head_bank(which, b)[:, 0:P], XB[which + 1][:, b, :],
                                        ALU.add).then_inc(x_new, 1)

            def scale_hidden(g, first, end):
                if g is None:
                    return
                for n in range(first, end):
                    dve.wait_ge(h_s, at(g, "h_s", n + 1))
                    dve.wait_ge(cb_p, at(g, "cb_p", n // FC + 1))
                    if n >= 2:
                        dve.wait_ge(y_p, at(g, "y_p", n - 1))
                    nc.vector.tensor_tensor(hsc[n % 2][:], psS[0][:, 1, :], hid[n % AHEAD][:],
                                            ALU.mult).then_inc(hs_s, 1)

            def mask_values(g):
                dve.wait_ge(m_in, at(g, "m_in", 16))
                nc.vector.tensor_scalar(mz[:], msk_in[:], 0.0, None, ALU.is_equal).then_inc(mzs, 1)
                dve.wait_ge(mzs, at(g, "mzs", 1))
                nc.vector.tensor_scalar(mbig[:], mz[:], -BIG, None, ALU.mult).then_inc(mzs, 1)
                nc.vector.tensor_reduce(anym[:], mz[:], AX_X, ALU.max).then_inc(mzs, 1)
                dve.wait_ge(mzs, at(g, "mzs", 3))
                nc.vector.tensor_scalar(floor0[:], anym[:], -HUGE, HUGE, ALU.mult, ALU.add).then_inc(mzs, 1)
                dve.wait_ge(mzs, at(g, "mzs", 4))
                nc.vector.tensor_scalar(floor[:], floor0[:], -MASKED, None, ALU.add).then_inc(mzs, 1)

            def front(a, d_):
                if d_ is not None:
                    top2_ranks(d_, 1, E1)
                if a is not None:
                    statistics(a, 1)
                if d_ is not None:
                    top2_weights(d_, 1, E1)
                    weight_parts(d_)
                if a is not None:
                    normalise(a, 1)
                if d_ is not None:
                    dve.wait_ge(cr_p, at(d_, "cr_p", 1))
                    nc.vector.tensor_copy(mp[:], four(psX)).then_inc(cp_s, 1)
                scale_hidden(d_, 0, 2)
                if a is not None:
                    dve.wait_ge(xts, at(a, "xts", 2))
                    nc.vector.tensor_reduce(pooled[:], XT[:], AX_X, ALU.add).then_inc(pool_s, 1)
                scale_hidden(d_, 2, 3)
                if a is not None:
                    mask_values(a)
                scale_hidden(d_, 3, 4)
                if a is not None:
                    dve.wait_ge(g1_s, at(a, "g1_s", 1))
                    nc.vector.tensor_copy(g1r[:], g1[:].rearrange("p (b o) -> p b o", o=1)
                                          .broadcast_to([P, GROUP, P])).then_inc(g1r_s, 1)
                scale_hidden(d_, 4, 5)
                if a is not None:
                    top2_ranks(a, 0, E0)
                scale_hidden(d_, 5, 6)
                if a is not None:
                    top2_weights(a, 0, E0)
                    dve.wait_ge(mtp, at(a, "mtp", 1))
                    nc.vector.tensor_copy(mzT[0:KEYS], four(psO)[0:KEYS]).then_inc(mts, 1)
                scale_hidden(d_, 6, 7)
                for e in range(E0):
                    if a is not None:
                        mixed_weights(a, e)
                    scale_hidden(d_, MIXED[e], MIXED[e + 1])
                if a is not None:
                    nc.vector.tensor_tensor(
                        bt[:], ff_b[:].rearrange("p (o k) e -> p o k e", o=1).broadcast_to([P, GROUP, 3, E0]),
                        wgt[:, :, 0:E0].rearrange("p b (o e) -> p b o e", o=1).broadcast_to([P, GROUP, 3, E0]),
                        ALU.mult).then_inc(bc_s, 1)
                    dve.wait_ge(bc_s, at(a, "bc_s", 1))
                    nc.vector.tensor_reduce(bc[:], bt[:], AX_X, ALU.add).then_inc(bc_s, 1)
                    dve.wait_ge(bc_s, at(a, "bc_s", 2))
                    nc.vector.tensor_tensor(kb_b[:], bc[:, :, 1:2].broadcast_to([P, GROUP, 4]),
                                            rmask[:].rearrange("p (o r) -> p o r", o=1)
                                            .broadcast_to([P, GROUP, 4]), ALU.mult).then_inc(bc_s, 1)
                scale_hidden(d_, 12, LAST)
                if a is not None:
                    dve.wait_ge(q_p, at(a, "q_p", 1))
                for b in range(GROUP):
                    if a is not None:
                        group_heads(b, psT[:, 0, b * P:(b + 1) * P], bc[:, b, 0:1], q_s)
                    scale_hidden(d_, LAST + b, min(LAST + b + 1, E1 * FC))
                if d_ is not None:
                    dve.wait_ge(y_p, at(d_, "y_p", E1 * FC))
                    dve.wait_ge(x_out, at(d_, "x_out", 16))
                    for b in range(GROUP):
                        nc.vector.tensor_tensor(X[4][:, b, :], psS[1][:, 1, b * P:(b + 1) * P], X[3][:, b, :],
                                                ALU.add).then_inc(y_s, 1)

            def mixed_weights(g, e):
                for b in range(GROUP):
                    if e == 0:
                        nc.vector.tensor_scalar(wc[:, b, :], ff_w[:, e, :], wgt[:, b, e:e + 1], None,
                                                ALU.mult).then_inc(wc_s, 1)
                    else:
                        dve.wait_ge(wc_s, at(g, "wc_s", (e - 1) * GROUP + b + 1))
                        nc.vector.scalar_tensor_tensor(out=wc[:, b, :], in0=ff_w[:, e, :],
                                                       scalar=wgt[:, b, e:e + 1], in1=wc[:, b, :],
                                                       op0=ALU.mult, op1=ALU.add).then_inc(wc_s, 1)

            for s in range(STEPS):
                branch_a(0, s)
            front(0, None)
            with dve.Fori(1, NG) as g:
                attention(g - 1, g)
                front(g, g - 1)
            attention(NG - 1, None)
            front(None, NG - 1)

        @block.tensor
        def _(pe):
            def mm(out, lhsT, rhs, start=True, stop=True, **kw):
                return nc.tensor.matmul(out, lhsT, rhs, start=start, stop=stop, **kw)

            pe.wait_ge(consts, ALL_CONSTS)
            pe.wait_ge(fills, FILLS)
            mm(psX[:, 0:P], xa_w[:, 2, :], xa_w[:, 3, :]).then_inc(fold_p, 1)
            mm(psX[:, P:2 * P], bvrep[:], xa_w[:, 3, :]).then_inc(fold_p, 1)
            pe.wait_ge(fold_s, 2)
            def transpose_x(g, layer, dst):
                for b in range(GROUP):
                    pe.wait_ge(ln_n, at(g, "ln_n", layer * GROUP + b + 1))
                    last = nc.tensor.transpose(dst[:, b * P:(b + 1) * P], xn[layer][:, b, :], ident[:])
                last.then_inc(xtp, 1)

            def masked_v(b):
                v = vz[1][0:KEYS, b, :, :].rearrange("p (m u) w -> p m (u w)", u=2)
                for u in range(2):
                    o = head_bank(1, b)[:, 2 * P:4 * P].rearrange("p (m u w) -> p m u w", u=2, w=16)[:, :, u, :]
                    mm(o, mzT[0:KEYS, b, :], v[:, :, u * (VW + 16):u * (VW + 16) + 16])

            def attention(g, nxt):
                for s in range(1, STEPS):
                    steps = [(w, s - w * LATER) for w in range(2)]
                    if nxt is not None and s == 9:
                        branch_a(nxt, s, g)
                    if s == LATER + 1 and nxt is not None:
                        pe.wait_ge(ka_s, at(nxt, "ka_s", 1))
                        pe.wait_ge(va_s, at(nxt, "va_s", 1))
                    for w, n in steps:
                        if 0 <= n < UNITS:
                            scores(g, w, (TOK, KEYS)[w], n)
                    c_query = s % 2 == 1 and 9 <= s < 9 + 2 * GROUP
                    if c_query:
                        pe.wait_ge(xcs, at(g, "xcs", (s - 9) // 2 + 1))
                        mm(psO[:, 3 * P:4 * P], xb_w[:, 0, :], XT[:, (s - 9) // 2, :]).then_inc(qc_p, 1)
                    for w, n in steps:
                        b = finishing(w, n, 2)
                        if b is not None:
                            output(g, w, b)
                    for w, n in steps:
                        if 2 <= n < UNITS + 2:
                            transpose_probs(g, w, (TOK, KEYS)[w], n - 2)
                    if c_query:
                        pe.wait_ge(qc_s, at(g, "qc_s", (s - 9) // 2 + 1))
                    for w, n in steps:
                        if 3 <= n < UNITS + 3:
                            values(g, w, (TOK, KEYS)[w], n - 3)
                    for w, n in steps:
                        b = finishing(w, n, 1)
                        if b is not None:
                            pe.wait_ge(at_s, at(g, "at_s", w * GROUP + b + 1))
                            nc.tensor.transpose(head_bank(w, b)[:, 0:P], att[:].rearrange("p h c -> p (h c)"),
                                                ident[:]).then_inc(at_p, 1)
                        b = finishing(w, n, 0)
                        if b is not None:
                            heads_back(g, w, b)
                    if nxt is not None and s == 8:
                        branch_a(nxt, s, g)
                    if s % 2 == 0 and 8 <= s < 8 + 2 * GROUP:
                        b = (s - 8) // 2
                        pe.wait_ge(oa_s, at(g, "oa_s", (3, 4, 4, 5)[b]))
                        pe.wait_ge(lb_n, at(g, "lb_n", b + 1))
                        nc.tensor.transpose(psO[:, 2 * P:3 * P], xn[0][:, b, :], ident[:]).then_inc(xcp, 1)
                    if s == STEPS - 2:
                        for b in range(GROUP - 1):
                            pe.wait_ge(lb_n, at(g, "lb_n", GROUP + b + 1))
                            last = nc.tensor.transpose(psT[:, 0, b * P:(b + 1) * P], xn[2][:, b, :], ident[:])
                        last.then_inc(xdp, 1)
                    if nxt is not None and s > LATER:
                        branch_a(nxt, s, g)

            def branch_a(a, s, before):
                if s == 8:
                    pe.wait_ge(c_in, at(a, "c_in", 16))
                    if before is not None:
                        pe.wait_ge(pr_s, at(before, "pr_s", UNITS - 1))
                    for b in range(GROUP):
                        last = nc.tensor.transpose(psS[0][:, 0, b * P:b * P + KEYS], ctx_in[0:KEYS, b, :],
                                                   ident[0:KEYS, 0:KEYS])
                    last.then_inc(ctp, 1)
                if s == 9:
                    pe.wait_ge(cts, at(a, "cts", 1))
                    if before is not None:
                        pe.wait_ge(pr_s, at(before, "pr_s", UNITS))
                    mm(four(psS[1][:, 0, :])[:, :, 0:KEYS], xa_w[:, 1, :], CT[:, :, 0:KEYS]).then_inc(ka_p, 1)
                    for b in range(GROUP):
                        last = mm(psS[1][0:KEYS, 1, b * P:(b + 1) * P], CT[:, b, 0:KEYS], wvo[:])
                    last.then_inc(va_p, 1)
                if s == 18:
                    if before is not None:
                        pe.wait_ge(pr_s, at(before, "pr_s", 2 * UNITS - 1))
                    transpose_x(a, 0, psS[0][:, 1, :])
                if s == 19:
                    pe.wait_ge(xts, at(a, "xts", 1))
                    mm(psS[0][:, 0, :], xa_w[:, 0, :], XT[:].rearrange("p b t -> p (b t)")).then_inc(qa_p, 1)
                if s == 20:
                    if before is not None:
                        pe.wait_ge(pr_s, at(before, "pr_s", 2 * UNITS))
                    pe.wait_ge(qa_s, at(a, "qa_s", 1))
                    pe.wait_ge(ka_s, at(a, "ka_s", 1))
                    for b in range(GROUP):
                        last = mm(psS[1][:, 0, b * P:b * P + KEYS], qa[:, b, :], ka[:, b, 0:KEYS])
                    last.then_inc(sa_p, 1)
                if s == 21:
                    for b in range(GROUP):
                        pe.wait_ge(pa_s, at(a, "pa_s", b + 1))
                        last = nc.tensor.transpose(psS[0][0:KEYS, 1, b * P:(b + 1) * P], pa[:, b, 0:KEYS],
                                                   ident[:])
                    last.then_inc(pta_p, 1)
                if s == 22:
                    pe.wait_ge(pta_s, at(a, "pta_s", 1))
                    pe.wait_ge(va_s, at(a, "va_s", 1))
                    for b in range(GROUP):
                        last = mm(psS[1][:, 1, b * P:(b + 1) * P], pta[0:KEYS, b, :], va[0:KEYS, b, :])
                    last.then_inc(oa_p, 1)

            def scores(g, which, nk, n):
                b, half = n // 2, n % 2
                i = which * UNITS + n
                if half == 0:
                    if which == 0:
                        pe.wait_ge(q_s, at(g, "q_s", b + 1))
                        pe.wait_ge(k_s, at(g, "k_s", 4 * b + 4))
                    else:
                        pe.wait_ge(qc_s, at(g, "qc_s", b + 1))
                        pe.wait_ge(kc_s, at(g, "kc_s", 4))
                if i >= 2:
                    pe.wait_ge(pr_s, at(g, "pr_s", i - 1))
                for a in range(2):
                    out = psS[n % 2][:, a, 0:4 * nk]
                    if which == 1:
                        mm(out, identb[:], mbig[:, b, :].rearrange(
                            "p (o k) -> p o k", o=1).broadcast_to([P, 4, nk]), stop=False)
                    last = mm(out, qg[:, b, 2 * half + a, :], km[which][:, b, :, 0:nk], start=which == 0)
                last.then_inc(s_p, 1)

            def transpose_probs(g, which, nk, n):
                i = which * UNITS + n
                pe.wait_ge(pr_s, at(g, "pr_s", i + 1))
                if i == 0:
                    pe.wait_ge(q_s, at(g, "q_s", GROUP))
                    pe.wait_ge(k_s, at(g, "k_s", 4 * GROUP))
                else:
                    pe.wait_ge(pt_s, at(g, "pt_s", i))
                for h in range(HALF):
                    last = nc.tensor.transpose(psT[0:nk, h // 4, (h % 4) * P:(h % 4 + 1) * P],
                                               pr[n % 2][:, h, 0:nk], ident[:])
                last.then_inc(pt_p, 1)

            def values(g, which, nk, m):
                b, half = m // 2, m % 2
                i = which * GROUP + b
                pe.wait_ge(pt_s, at(g, "pt_s", which * UNITS + m + 1))
                if m == 0:
                    if which == 0:
                        pe.wait_ge(v_s, at(g, "v_s", 2))
                    else:
                        pe.wait_ge(vc_s, at(g, "vc_s", 2))
                if i >= 1 and half == 0:
                    pe.wait_ge(oa_s, at(g, "oa_s", i))
                for u in range(2):
                    for j in range(4):
                        hh = 2 * j + u
                        last = mm(psO[32 * j:32 * j + VW, half * P:(half + 1) * P],
                                  vz[which][0:nk, b, half * HALF + hh, :], pt[m % 2][0:nk, hh, :],
                                  start=u == 0, stop=u == 1)
                last.then_inc(pv_p, 1)

            def heads_back(g, which, b):
                i = which * GROUP + b
                pe.wait_ge(oa_s, at(g, "oa_s", i + 1))
                if i == 0:
                    pe.wait_ge(kc_s, at(g, "kc_s", 4))
                elif i == 2 * GROUP - 1:
                    pe.wait_ge(pt_s, at(g, "pt_s", 2 * UNITS))
                else:
                    pe.wait_ge(x_new, at(g, "x_new", i))
                if which == 1:
                    masked_v(b)
                for half in range(2):
                    last = nc.tensor.transpose(head_bank(which, b)[:, half * P:(half + 1) * P],
                                               oa[:, half, :], ident[:])
                last.then_inc(to_p, 1)

            def output(g, which, b):
                i = which * GROUP + b
                pe.wait_ge(atT_s, at(g, "atT_s", i + 1))
                wo = ff_wo[:] if which == 0 else xb_w[:, 3, :]
                mm(head_bank(which, b)[:, 0:P], attT[:], wo).then_inc(out_p, 1)


            def hidden(g, n):
                if n >= 2:
                    pe.wait_ge(h_s, at(g, "h_s", n - 1))
                mm(psS[n % 2][:, 0, :], mo_w1[:, n // FC, (n % FC) * P:(n % FC + 1) * P],
                   XD[:].rearrange("p b t -> p (b t)")).then_inc(h_p, 1)

            def combine(g, e):
                if e >= 1:
                    pe.wait_ge(hs_s, at(g, "hs_s", e * FC))
                mm(psS[0][:, 1, :], sel[:, e, :], mp[:].rearrange("p b t -> p (b t)")).then_inc(cb_p, 1)

            def experts(g, first, end):
                if g is None:
                    return
                for n in range(first, end):
                    if n + AHEAD < E1 * FC:
                        hidden(g, n + AHEAD)
                    pe.wait_ge(hs_s, at(g, "hs_s", n + 1))
                    if n % FC == FC - 1 and n // FC + 1 < E1:
                        combine(g, n // FC + 1)
                    for b in range(GROUP):
                        last = mm(psS[1][:, 1, b * P:(b + 1) * P], hsc[n % 2][:, b * P:(b + 1) * P],
                                  mo_w2[:, n // FC, n % FC, :], start=False, stop=n == E1 * FC - 1,
                                  skip_group_check=True)
                    last.then_inc(y_p, 1)

            def front(a, d_):
                if d_ is not None:
                    pe.wait_ge(xds, at(d_, "xds", 1))
                    pe.wait_ge(lb_n, at(d_, "lb_n", 2 * GROUP))
                    nc.tensor.transpose(psT[:, 0, (GROUP - 1) * P:], xn[2][:, GROUP - 1, :],
                                        ident[:]).then_inc(xdp, 1)
                    for b in range(GROUP):
                        if b == GROUP - 1:
                            pe.wait_ge(xds, at(d_, "xds", 2))
                        last = mm(psT[:, 1, b * E1:(b + 1) * E1], XD[:, b, :], mo_r[:])
                    last.then_inc(lg_p, 1)
                    if a is not None:
                        pe.wait_ge(xa_new, at(a, "xa_new", GROUP))
                    for n in range(AHEAD):
                        hidden(d_, n)
                    pe.wait_ge(cr_s, at(d_, "cr_s", 6))
                    for b in range(GROUP):
                        last = nc.tensor.transpose(psX[:, b * P:(b + 1) * P], mr[:, b, :], ident[:])
                    last.then_inc(cr_p, 1)
                if a is not None:
                    transpose_x(a, 1, psO)
                if d_ is not None:
                    pe.wait_ge(cp_s, at(d_, "cp_s", 1))
                    combine(d_, 0)
                    pe.wait_ge(c32_s, at(d_, "c32_s", 1))
                    for b in range(GROUP):
                        mm(psS[1][:, 1, b * P:(b + 1) * P], ct32[:, b, :], mo_b2[:], start=b == 0, stop=False,
                           skip_group_check=True)
                experts(d_, 0, 2)
                if a is not None:
                    mm(four(psX)[:, :, 0:KEYS], xb_w[:, 1, :], CT[:, :, 0:KEYS]).then_inc(kc_p, 1)
                    pe.wait_ge(pool_s, at(a, "pool_s", 1))
                    mm(psO[:, 0:GROUP], ff_g1[:], pooled[:]).then_inc(g1_p, 1)
                experts(d_, 2, 4)
                if a is not None:
                    pe.wait_ge(g1r_s, at(a, "g1r_s", 1))
                    for b in range(GROUP):
                        last = mm(psT[:, 1, b * E0:(b + 1) * E0], g1r[:, b, :], ff_g2[:])
                    last.then_inc(lg_p, 1)
                    pe.wait_ge(mzs, at(a, "mzs", 1))
                    for b in range(GROUP):
                        last = nc.tensor.transpose(psO[0:KEYS, b * P:(b + 1) * P], mz[:, b, :], ident[:])
                    last.then_inc(mtp, 1)
                experts(d_, 4, 6)
                if a is not None:
                    for b in range(GROUP):
                        last = mm(psT[0:KEYS, 0, b * P:(b + 1) * P], CT[:, b, 0:KEYS], xb_w[:, 2, :])
                    last.then_inc(vc_p, 1)
                experts(d_, 6, LAST - 2)
                if a is not None:
                    pe.wait_ge(vc_s, at(a, "vc_s", 2))
                    for b in range(GROUP):
                        pe.wait_ge(wc_s, at(a, "wc_s", (E0 - 1) * GROUP + b + 1))
                        mq = mm(psT[:, 0, b * P:(b + 1) * P], wc[:, b, 0:P], XT[:, b, :])
                        mk = mm(psT[:, 1, b * P:(b + 1) * P], wc[:, b, P:2 * P], XT[:, b, :])
                    mq.then_inc(q_p, 1)
                    mk.then_inc(k_p, 1)
                    pe.wait_ge(mts, at(a, "mts", 1))
                    for b in range(GROUP):
                        last = mm(psO[:, b * P:(b + 1) * P], XT[:, b, :], wc[:, b, 2 * P:3 * P])
                    last.then_inc(v_p, 1)
                experts(d_, LAST - 2, E1 * FC)
                if a is not None:
                    scores(a, 0, TOK, 0)
                    if d_ is not None:
                        pe.wait_ge(y_s, at(d_, "y_s", GROUP))

            for s in range(STEPS):
                branch_a(0, s, None)
            front(0, None)
            with pe.Fori(1, NG) as g:
                attention(g - 1, g)
                front(g, g - 1)
            attention(NG - 1, None)
            front(None, NG - 1)


def lay_out(inputs):
    f = {k: np.asarray(v) for k, v in inputs.items()}
    T = np.ascontiguousarray
    w1, w2 = f["L1_ffn_w1"], f["L1_ffn_w2"]
    E1, HID, _ = w1.shape
    FC = HID // P
    sel = np.zeros((P, HEADS, P), np.float32)
    for h in range(HEADS):
        for p0 in PARTS:
            sel[p0 + h, h, :] = 1.0
    gmask, rmask = np.zeros((P, QUADS), np.float32), np.zeros((P, 4), np.float32)
    for h in range(HEADS):
        gmask[h * DH:(h + 1) * DH, h // 4] = float(DH) ** -0.5
        rmask[h * DH:(h + 1) * DH, h % 4] = 1.0
    tri = np.zeros((P, E1, E1), np.float32)
    for e in range(E1):
        tri[:, e, :e] = 1.0
    bf = mybir.dt.np(BF16)
    eye = np.eye(P, dtype=np.float32)
    a = {
        "x": f["x"], "ctx": f["ctx_1024"], "mask": f["mask_Bx1xSxS2_if1"].reshape(f["x"].shape[0], P, -1),
        "ident": eye, "identb": eye.astype(bf), "sel": sel.astype(bf), "gmask": gmask, "rmask": rmask, "tri": tri,
        "xa_w": T(np.stack([f["L0_xattn_Wq"].T, f["L0_xattn_Wk"].T, f["L0_xattn_Wv"], f["L0_xattn_Wo"].T], 1)),
        "xa_b": T(np.stack([f["L0_xattn_bq"], f["L0_xattn_bv"], f["L0_xattn_bv"]], 1)),
        "bvrep": T(np.broadcast_to(f["L0_xattn_bv"][:, None], (P, P))),
        "brow": T(np.stack([f["L0_xattn_bo"], f["L0_ffn_bo"], f["L1_xattn_bo"]])),
        "ff_w": T(np.concatenate([f["L0_ffn_Wq"], f["L0_ffn_Wk"], f["L0_ffn_Wv"]], 2).transpose(1, 0, 2)),
        "ff_b": T(np.stack([f["L0_ffn_bq"], f["L0_ffn_bk"], f["L0_ffn_bv"]]).transpose(2, 0, 1)),
        "ff_g1": f["L0_ffn_Wg1"], "ff_bg1": T(f["L0_ffn_bg1"][:, None]), "ff_g2": f["L0_ffn_Wg2"],
        "ff_bg2": f["L0_ffn_bg2"], "ff_wo": f["L0_ffn_Wo"],
        "xb_w": T(np.stack([f["L1_xattn_" + w].T for w in ("Wq", "Wk", "Wv", "Wo")], 1)),
        "xb_b": T(np.stack([f["L1_xattn_" + b] for b in ("bq", "bk", "bv")], 1)),
        "mo_r": T(f["L1_ffn_router_w"].T), "mo_w1": T(w1.transpose(2, 0, 1)),
        "mo_b1": T(f["L1_ffn_b1"].reshape(E1, FC, P).transpose(2, 0, 1)),
        "mo_w2": T(w2.reshape(E1, P, FC, P).transpose(3, 0, 2, 1)), "mo_b2": f["L1_ffn_b2"],
    }
    return a


def kernel(**inputs):
    import concourse.bacc as bacc
    from concourse.bass_utils import run_bass_kernel_spmd

    nc = bacc.Bacc("TRN2", target_bir_lowering=False, num_devices=1)
    arrays, d = {}, {}
    for name, a in lay_out(inputs).items():
        arrays[f"in_{name}"] = a
        d[name] = nc.dram_tensor(f"in_{name}", a.shape, mybir.dt.from_np(a.dtype), kind="ExternalInput").ap()
    d["out"] = nc.dram_tensor("out_x", d["x"].shape, F32, kind="ExternalOutput").ap()

    class Shaped:
        def __init__(self, shape):
            self.shape = shape
    E1 = arrays["in_mo_b1"].shape[1]
    d["ffn_bg2"] = Shaped((1, arrays["in_ff_bg2"].shape[0]))
    d["moe_b1"] = Shaped((1, E1, arrays["in_mo_b1"].shape[2]))
    build(nc, d)
    r = run_bass_kernel_spmd(nc, [arrays], core_ids=[0])
    return r.results[0]["out_x"]
```
